# Optimizing a Trainium2 kernel written in Bass

```python
import numpy as np
import jax
import jax.numpy as jnp

def _softmax(x, axis=-1):
    return jax.nn.softmax(x, axis=axis)

def _gelu(x):
    return jax.nn.gelu(x, approximate=True)

def _silu(x):
    return jax.nn.silu(x)

def _sigmoid(x):
    return jax.nn.sigmoid(x)

def _layernorm(x, axis=-1, eps=1e-05):
    m = jnp.mean(x, axis=axis, keepdims=True)
    v = jnp.var(x, axis=axis, keepdims=True)
    return (x - m) / jnp.sqrt(v + eps)

def _scatter_add(tgt, idx, src, axis=0):
    return tgt.at[idx].add(src)

def _segment_sum(src, seg, n):
    return jax.ops.segment_sum(src, seg, n)
kernel_name = 'mk_recurrent_d2_jaxref_r8_880052'

def setup_inputs(seed: int=0):
    np.random.seed(seed)
    _w = jnp.asarray

    def _L0_attn_setup():
        import math
        import jax, jax.numpy as jnp
        import numpy as np
        H = 32
        NOPE = 64
        ROPE = 64
        VD = 128
        QHD = NOPE + ROPE
        KVR = 32
        EPS = 1e-06

        def _yarn_cos_sin(seq_len, dim=ROPE, base=10000.0, factor=128.0, beta_fast=32.0, beta_slow=1.0, orig_max=1024, mscale=1.0, mscale_all_dim=1.0):

            def corr_dim(r):
                return dim * math.log(orig_max / (r * 2 * math.pi)) / (2 * math.log(base))
            low = max(math.floor(corr_dim(beta_fast)), 0)
            high = min(math.ceil(corr_dim(beta_slow)), dim - 1)
            hi = high + 0.001 if low == high else float(high)
            ramp = np.clip((np.arange(dim // 2, dtype=np.float32) - low) / (hi - low), 0.0, 1.0)
            inv_freq_mask = 1.0 - ramp
            freq_extra = 1.0 / base ** (np.arange(0, dim, 2, dtype=np.float32) / dim)
            freq_inter = freq_extra / factor
            inv_freq = freq_inter * (1.0 - inv_freq_mask) + freq_extra * inv_freq_mask
            t = np.arange(seq_len, dtype=np.float32)
            freqs = np.outer(t, inv_freq)
            emb = np.concatenate([freqs, freqs], axis=-1)

            def gm(s, m):
                return 1.0 if s <= 1 else 0.1 * m * math.log(s) + 1.0
            ms = gm(factor, mscale) / gm(factor, mscale_all_dim)
            return (jnp.asarray(np.cos(emb) * ms), jnp.asarray(np.sin(emb) * ms))

        def _rmsnorm(x, w, eps=EPS):
            var = jnp.mean(jnp.square(x), axis=-1, keepdims=True)
            return x * jax.lax.rsqrt(var + eps) * w

        def _deinterleave(x):
            d = x.shape[-1]
            x = x.reshape(*x.shape[:-1], d // 2, 2)
            return jnp.concatenate([x[..., 0], x[..., 1]], axis=-1)

        def _rotate_half(x):
            d = x.shape[-1] // 2
            return jnp.concatenate([-x[..., d:], x[..., :d]], axis=-1)

        def _apply_rope(x, cos, sin):
            return x * cos + _rotate_half(x) * sin
        key = jax.random.key(seed)
        ks = jax.random.split(key, 6)
        B, S, D = (1, 256, 512)
        std = 0.02
        return {'x': jax.random.normal(ks[0], (B, S, D), dtype=jnp.float32), 'wq_a': jax.random.normal(ks[1], (128, D), dtype=jnp.float32) * std, 'q_a_ln_w': jnp.ones((128,), dtype=jnp.float32), 'wq_b': jax.random.normal(ks[2], (H * QHD, 128), dtype=jnp.float32) * std, 'wkv_a': jax.random.normal(ks[3], (KVR + ROPE, D), dtype=jnp.float32) * std, 'kv_a_ln_w': jnp.ones((KVR,), dtype=jnp.float32), 'wkv_b': jax.random.normal(ks[4], (H * (NOPE + VD), KVR), dtype=jnp.float32) * std, 'wo': jax.random.normal(ks[5], (D, H * VD), dtype=jnp.float32) * std}
    _L0_attn_in = _L0_attn_setup()

    def _L0_ffn_setup():
        import jax, jax.numpy as jnp
        import numpy as np
        IMAGE_START_POS = 34
        Q_START = IMAGE_START_POS + 72 + 1
        Q_END = -1
        LORA_ALPHA = 32
        LORA_RANK = 16
        SCALING = LORA_ALPHA / LORA_RANK
        key = jax.random.key(seed)
        ks = jax.random.split(key, 7)
        B_, S, D, O, E, R = (4, 256, 512, 512, 8, LORA_RANK)
        s = 0.02
        return {'x': jax.random.normal(ks[0], (B_, S, D), jnp.float32), 'W': jax.random.normal(ks[1], (O, D), jnp.float32) * s, 'b': jax.random.normal(ks[2], (O,), jnp.float32) * s, 'A': jax.random.normal(ks[3], (E, R, D), jnp.float32) * s, 'B': jax.random.normal(ks[4], (E, O, R), jnp.float32) * s, 'router_W': jax.random.normal(ks[5], (E, D), jnp.float32) * s, 'router_b': jax.random.normal(ks[6], (E,), jnp.float32) * s}
    _L0_ffn_in = _L0_ffn_setup()

    def _L1_attn_setup():
        import jax, jax.numpy as jnp
        import numpy as np
        B, C, L = (64, 64, 512)
        key = jax.random.key(seed)
        x = jax.random.normal(key, (B, C, L), dtype=jnp.float32)
        return {'x': x}
    _L1_attn_in = _L1_attn_setup()

    def _L1_ffn_setup():
        import jax, jax.numpy as jnp
        import numpy as np
        H, F, E, K = (512, 800, 8, 2)
        B, S = (1, 64)
        key = jax.random.key(seed)
        k0, k1, k2, k3, k4 = jax.random.split(key, 5)
        x = jax.random.normal(k0, (B, S, H), dtype=jnp.float32)
        gate_w = jax.random.normal(k1, (E, H), dtype=jnp.float32) * 0.02
        w1 = jax.random.normal(k2, (E, F, H), dtype=jnp.float32) * 0.02
        w3 = jax.random.normal(k3, (E, F, H), dtype=jnp.float32) * 0.02
        w2 = jax.random.normal(k4, (E, H, F), dtype=jnp.float32) * 0.02
        return {'x': x, 'gate_w': gate_w, 'w1': w1, 'w2': w2, 'w3': w3}
    _L1_ffn_in = _L1_ffn_setup()
    _d = {'L0_attn_x': _L0_attn_in['x'], 'L0_attn_wq_a': _L0_attn_in['wq_a'], 'L0_attn_q_a_ln_w': _L0_attn_in['q_a_ln_w'], 'L0_attn_wq_b': _L0_attn_in['wq_b'], 'L0_attn_wkv_a': _L0_attn_in['wkv_a'], 'L0_attn_kv_a_ln_w': _L0_attn_in['kv_a_ln_w'], 'L0_attn_wkv_b': _L0_attn_in['wkv_b'], 'L0_attn_wo': _L0_attn_in['wo'], 'L0_ffn_W': _L0_ffn_in['W'], 'L0_ffn_b': _L0_ffn_in['b'], 'L0_ffn_A': _L0_ffn_in['A'], 'L0_ffn_B': _L0_ffn_in['B'], 'L0_ffn_router_W': _L0_ffn_in['router_W'], 'L0_ffn_router_b': _L0_ffn_in['router_b'], 'L1_ffn_gate_w': _L1_ffn_in['gate_w'], 'L1_ffn_w1': _L1_ffn_in['w1'], 'L1_ffn_w2': _L1_ffn_in['w2'], 'L1_ffn_w3': _L1_ffn_in['w3']}
    _x0 = _d['L0_attn_x']
    _d['L0_attn_x'] = jax.random.normal(jax.random.fold_in(jax.random.key(seed), 1), (8, 256, 512), dtype=_x0.dtype)
    del _x0
    return _d

def reference(L0_attn_x, L0_attn_wq_a, L0_attn_q_a_ln_w, L0_attn_wq_b, L0_attn_wkv_a, L0_attn_kv_a_ln_w, L0_attn_wkv_b, L0_attn_wo, L0_ffn_W, L0_ffn_b, L0_ffn_A, L0_ffn_B, L0_ffn_router_W, L0_ffn_router_b, L1_ffn_gate_w, L1_ffn_w1, L1_ffn_w2, L1_ffn_w3):

    def _L0_attn_ref(x, wq_a, q_a_ln_w, wq_b, wkv_a, kv_a_ln_w, wkv_b, wo):
        import math
        import jax, jax.numpy as jnp
        import numpy as np
        H = 32
        NOPE = 64
        ROPE = 64
        VD = 128
        QHD = NOPE + ROPE
        KVR = 32
        EPS = 1e-06

        def _yarn_cos_sin(seq_len, dim=ROPE, base=10000.0, factor=128.0, beta_fast=32.0, beta_slow=1.0, orig_max=1024, mscale=1.0, mscale_all_dim=1.0):

            def corr_dim(r):
                return dim * math.log(orig_max / (r * 2 * math.pi)) / (2 * math.log(base))
            low = max(math.floor(corr_dim(beta_fast)), 0)
            high = min(math.ceil(corr_dim(beta_slow)), dim - 1)
            hi = high + 0.001 if low == high else float(high)
            ramp = np.clip((np.arange(dim // 2, dtype=np.float32) - low) / (hi - low), 0.0, 1.0)
            inv_freq_mask = 1.0 - ramp
            freq_extra = 1.0 / base ** (np.arange(0, dim, 2, dtype=np.float32) / dim)
            freq_inter = freq_extra / factor
            inv_freq = freq_inter * (1.0 - inv_freq_mask) + freq_extra * inv_freq_mask
            t = np.arange(seq_len, dtype=np.float32)
            freqs = np.outer(t, inv_freq)
            emb = np.concatenate([freqs, freqs], axis=-1)

            def gm(s, m):
                return 1.0 if s <= 1 else 0.1 * m * math.log(s) + 1.0
            ms = gm(factor, mscale) / gm(factor, mscale_all_dim)
            return (jnp.asarray(np.cos(emb) * ms), jnp.asarray(np.sin(emb) * ms))

        def _rmsnorm(x, w, eps=EPS):
            var = jnp.mean(jnp.square(x), axis=-1, keepdims=True)
            return x * jax.lax.rsqrt(var + eps) * w

        def _deinterleave(x):
            d = x.shape[-1]
            x = x.reshape(*x.shape[:-1], d // 2, 2)
            return jnp.concatenate([x[..., 0], x[..., 1]], axis=-1)

        def _rotate_half(x):
            d = x.shape[-1] // 2
            return jnp.concatenate([-x[..., d:], x[..., :d]], axis=-1)

        def _apply_rope(x, cos, sin):
            return x * cos + _rotate_half(x) * sin
        B, S, D = x.shape
        m = 0.1 * 1.0 * math.log(128.0) + 1.0
        softmax_scale = QHD ** (-0.5) * m * m
        q = _rmsnorm(x @ wq_a.T, q_a_ln_w) @ wq_b.T
        q = q.reshape(B, S, H, QHD)
        q_nope, q_pe = (q[..., :NOPE], q[..., NOPE:])
        ckv_kpe = x @ wkv_a.T
        ckv, k_pe = (ckv_kpe[..., :KVR], ckv_kpe[..., KVR:])
        kv = _rmsnorm(ckv, kv_a_ln_w) @ wkv_b.T
        kv = kv.reshape(B, S, H, NOPE + VD)
        k_nope, v = (kv[..., :NOPE], kv[..., NOPE:])
        cos, sin = _yarn_cos_sin(S)
        q_pe = _apply_rope(_deinterleave(q_pe), cos[None, :, None, :], sin[None, :, None, :])
        k_pe = _apply_rope(_deinterleave(k_pe), cos[None, :, :], sin[None, :, :])
        q_full = jnp.concatenate([q_nope, q_pe], axis=-1)
        k_full = jnp.concatenate([k_nope, jnp.broadcast_to(k_pe[:, :, None, :], (B, S, H, ROPE))], axis=-1)
        scores = jnp.einsum('bqhd,bkhd->bhqk', q_full, k_full) * softmax_scale
        causal = jnp.tril(jnp.ones((S, S), dtype=bool))
        scores = jnp.where(causal[None, None], scores, jnp.finfo(scores.dtype).min)
        attn = jax.nn.softmax(scores, axis=-1)
        out = jnp.einsum('bhqk,bkhd->bqhd', attn, v).reshape(B, S, H * VD)
        return out @ wo.T

    def _L0_ffn_ref(x, W, b, A, B, router_W, router_b):
        import jax, jax.numpy as jnp
        import numpy as np
        IMAGE_START_POS = 34
        Q_START = IMAGE_START_POS + 72 + 1
        Q_END = -1
        LORA_ALPHA = 32
        LORA_RANK = 16
        SCALING = LORA_ALPHA / LORA_RANK
        x_q = x[:, Q_START:Q_END, :]
        q = x_q.mean(axis=1)
        logits = q @ router_W.T + router_b
        routing = jax.nn.softmax(logits, axis=-1)
        base = x @ W.T + b
        t = jnp.einsum('bsd,erd->bser', x, A)
        lora = jnp.einsum('bser,eor,be->bso', t, B, routing) * SCALING
        return base + lora

    def _L1_attn_ref(x):
        import jax, jax.numpy as jnp
        import numpy as np
        B, C, L = (64, 64, 512)
        b, c, l = x.shape
        q = jnp.transpose(x, (2, 0, 1))
        scale = jnp.asarray(c, x.dtype) ** 0.5
        scores = jnp.einsum('lnc,lmc->lnm', q, q) / scale
        prob = jax.nn.softmax(scores, axis=-1)
        msg = jnp.einsum('lnm,lmc->lnc', prob, q)
        return x + jnp.transpose(msg, (1, 2, 0))

    def _L1_ffn_ref(x, gate_w, w1, w2, w3):
        import jax, jax.numpy as jnp
        import numpy as np
        H, F, E, K = (512, 800, 8, 2)
        B, S = (1, 64)
        b, s, h = x.shape
        xt = x.reshape(-1, h)
        T = xt.shape[0]
        logits = xt @ gate_w.T
        probs = jax.nn.softmax(logits, axis=-1)
        top_vals, top_idx = jax.lax.top_k(probs, K)
        top_vals = top_vals / jnp.sum(top_vals, axis=-1, keepdims=True)
        w_full = jnp.zeros((T, E), dtype=xt.dtype).at[jnp.arange(T)[:, None], top_idx].add(top_vals)
        h1 = jnp.einsum('th,efh->tef', xt, w1)
        h3 = jnp.einsum('th,efh->tef', xt, w3)
        act = jax.nn.silu(h1) * h3
        expert_out = jnp.einsum('tef,ehf->teh', act, w2)
        y = jnp.einsum('te,teh->th', w_full, expert_out)
        return y.reshape(b, s, h)
    x = L0_attn_x
    xn = _layernorm(x, axis=-1)
    s = _L0_attn_ref(xn, L0_attn_wq_a, L0_attn_q_a_ln_w, L0_attn_wq_b, L0_attn_wkv_a, L0_attn_kv_a_ln_w, L0_attn_wkv_b, L0_attn_wo)
    g = _silu(_L0_ffn_ref(xn, L0_ffn_W, L0_ffn_b, L0_ffn_A, L0_ffn_B, L0_ffn_router_W, L0_ffn_router_b))
    x = x + s * g
    xn = _layernorm(x, axis=-1)
    s = _L1_attn_ref(xn)
    g = _silu(_L1_ffn_ref(xn, L1_ffn_gate_w, L1_ffn_w1, L1_ffn_w2, L1_ffn_w3))
    x = x + s * g
    return x

_drawn_inputs = setup_inputs


def setup_inputs(seed=0):
    import zlib

    import numpy as np

    out = dict(_drawn_inputs(seed))
    spreads = {'L0_attn_q_a_ln_w': (1.0, 0.6), 'L0_attn_kv_a_ln_w': (1.0, 0.6)}
    factors = {'L0_attn_wq_a': 8.0,
     'L0_attn_wq_b': 8.0,
     'L0_attn_wkv_a': 6.703,
     'L0_attn_wkv_b': 6.364,
     'L0_attn_wo': 7.035,
     'L0_ffn_W': 7.728,
     'L0_ffn_b': 8.0,
     'L0_ffn_A': 8.0,
     'L0_ffn_B': 8.0,
     'L0_ffn_router_W': 8.0,
     'L0_ffn_router_b': 8.0,
     'L1_ffn_gate_w': 8.0,
     'L1_ffn_w1': 8.0,
     'L1_ffn_w2': 8.0,
     'L1_ffn_w3': 8.0}
    for name, (base, spread) in spreads.items():
        noise = np.random.default_rng([zlib.crc32(name.encode()), seed]).standard_normal(out[name].shape)
        drawn = base * np.exp(spread * noise) if base else spread * noise
        out[name] = jnp.asarray(drawn.astype(out[name].dtype))
    for name, factor in factors.items():
        out[name] = (out[name] * factor).astype(out[name].dtype)
    return out
```

```python
import math
from contextlib import ExitStack

import numpy as np

import concourse.bass as bass
from concourse import mybir

F32 = mybir.dt.float32
BF16 = mybir.dt.bfloat16
I32 = mybir.dt.int32
ALU = mybir.AluOpType
ACT = mybir.ActivationFunctionType
AX = mybir.AxisListType
ds = bass.ds

P = 128
NB, SEQ, D = 8, 256, 512
NT = NB * SEQ // P
KT_PER_D = D // P
H, NOPE, ROPE, VD, KVR, QR = 32, 64, 64, 128, 32, 128
KC = ROPE + KVR
QKW = QR + KC
NE, RANK = 8, 16
E, FF = 8, 800
FT = FF // P
FR = FF - FT * P
MSCALE = 0.1 * math.log(128.0) + 1.0
SCALE = (NOPE + ROPE) ** -0.5 * MSCALE * MSCALE
LORA_SCALE = 2.0
MEAN_FROM, MEAN_TO = 107, 255
LN_EPS, RMS_EPS = 1e-5, 1e-6
BIG = -1.0e30
NBLK = 2 * NB * SEQ // P + E - 1

CONSTS = {}
_at = 0
for _name, _n in (("ident", P), ("causal", P), ("same_l", P), ("before", P), ("cos", 2 * KC), ("sin", 2 * ROPE),
                  ("mean", 2 * 15), ("earlier_e", E * E), ("tile_starts", 16), ("block_ids", NBLK)):
    CONSTS[_name] = (_at, _n)
    _at += _n
NCONST = _at


def shape_constants():
    c = np.zeros((P, NCONST), np.float32)

    def put(name, a):
        at, n = CONSTS[name]
        c[:, at:at + n] = np.asarray(a, np.float32).reshape(P, n)

    p = np.arange(P)
    put("ident", np.eye(P))
    put("causal", np.where(p[None, :] <= p[:, None], 0.0, BIG))
    put("same_l", np.where(p[None, :] // NB == p[:, None] // NB, 0.0, BIG))
    put("before", p[:, None] < p[None, :])
    low = max(math.floor(ROPE * math.log(1024 / (32.0 * 2 * math.pi)) / (2 * math.log(10000.0))), 0)
    high = min(math.ceil(ROPE * math.log(1024 / (2 * math.pi)) / (2 * math.log(10000.0))), ROPE - 1)
    hi = high + 0.001 if low == high else float(high)
    keep = 1.0 - np.clip((np.arange(ROPE // 2, dtype=np.float32) - low) / (hi - low), 0.0, 1.0)
    extra = 1.0 / 10000.0 ** (np.arange(0, ROPE, 2, dtype=np.float32) / ROPE)
    freq = extra / 128.0 * (1.0 - keep) + extra * keep
    angle = np.outer(np.arange(SEQ, dtype=np.float32), freq)
    cos, sin = np.cos(angle), np.sin(angle)
    one = np.ones((SEQ, KVR))
    put("cos", np.concatenate([cos, cos, one], 1).reshape(2, P, KC).transpose(1, 0, 2))
    put("sin", np.concatenate([-sin, sin], 1).reshape(2, P, ROPE).transpose(1, 0, 2))
    mean = np.zeros((P, 2, 15))
    tok = p[:, None] + P * np.arange(2)[None, :]
    mean[:, :, 7] = ((tok >= MEAN_FROM) & (tok < MEAN_TO)) / (MEAN_TO - MEAN_FROM)
    put("mean", mean)
    e = np.arange(E)
    put("earlier_e", np.tile((e[None, :] < e[:, None]).reshape(1, -1), (P, 1)))
    put("tile_starts", np.tile(P * np.arange(16), (P, 1)))
    put("block_ids", np.tile(np.arange(NBLK), (P, 1)))
    return c


class Chain:

    def __init__(self, eng, sem, base=0):
        self.eng, self.sem, self.base, self.n = eng, sem, base, 0

    def __call__(self, ins):
        ins.then_inc(self.sem, 1)
        self.n += 1

    def wait(self):
        self.eng.wait_ge(self.sem, self.base + self.n)

    def then(self, ins):
        self(ins)
        self.wait()


def build(nc, a, out, dbg=None):
    dbg = dbg or {}
    with ExitStack() as ctx:
        def sb(name, shape, dt=F32):
            return ctx.enter_context(nc.sbuf_tensor(name, shape, dt))

        X = sb("x_keep", [P, NT, D])
        XN = sb("xn_keep", [P, NT, D])
        C = sb("consts_sb", [P, NCONST])
        identb = sb("identb", [P, P], BF16)
        maskb = sb("maskb", [P, P], BF16)
        vecs = sb("vecs_sb", [P, D + QR + KVR + NE])
        ROOM = 33750
        R = sb("room", [P, ROOM])
        bank = [ctx.enter_context(nc.psum_tensor(f"bank{i}", [P, 1024], F32)) for i in range(4)]

        def psum(i):
            return bank[i // 2][:, 512 * (i % 2):512 * (i % 2) + 512]

        def const(name, pattern=None, **k):
            at, n = CONSTS[name]
            v = C[:, at:at + n]
            return v.rearrange(pattern, **k) if pattern else v

        ident = const("ident")
        stages = Stages(nc, ctx, a, out, dbg)
        stages.X, stages.XN, stages.C, stages.R, stages.vecs = X, XN, C, R, vecs
        stages.identb, stages.maskb, stages.bank = identb, maskb, bank
        stages.psum, stages.const, stages.ident, stages.ROOM = psum, const, ident, ROOM
        first_projections(stages)
        normalise_latents(stages)
        attention(stages)
        if dbg.get("stop") == "attn":
            return finish_dbg(stages)
        across_batch(stages)
        if dbg.get("stop") == "route":
            return finish_dbg(stages)
        experts(stages)
        combine(stages)


def finish_dbg(s):
    sm = s.sem("dbg")
    with s.nc.Block() as blk:
        @blk.sync
        def _(sp):
            n = 0
            for name, view in s.dbg.get("dumps", lambda s: {})(s).items():
                sp.dma_start(s.dbg["outs"][name], view).then_inc(sm, 16)
                n += 16
            sp.wait_ge(sm, n)


class Stages:

    def __init__(self, nc, ctx, a, out, dbg):
        self.nc, self.ctx, self.a, self.out, self.dbg, self.at = nc, ctx, a, out, dbg, 0

    def sem(self, name):
        return self.ctx.enter_context(self.nc.semaphore(name))

    def carve(self, *shape, dt=F32):
        n = int(np.prod(shape))
        v = self.R[:, self.at:self.at + n]
        self.at += n
        assert self.at <= self.ROOM, self.at
        if dt != F32:
            v = v.bitcast(dt)
        if len(shape) > 1:
            names = "abcd"[:len(shape)]
            v = v.rearrange(f"p ({' '.join(names)}) -> p {' '.join(names)}", **dict(zip(names, shape)))
        return v


def first_projections(s):
    nc, a, sem = s.nc, s.a, s.sem
    X, XN, psum, const, ident = s.X, s.XN, s.psum, s.const, s.ident
    s.at = 0
    s.WqT = s.carve(H, KC)
    s.WoP = s.carve(NB, D)
    s.ss = s.carve(NT, 2)
    s.latents_at = s.at
    wqn = s.carve(H, QR)
    wkb = s.carve(H, KVR)
    s.at = s.latents_at + NT * KC + NT * P + (NT + 2) * P
    s.QKA = s.carve(NT, QKW)
    wo = s.carve(2, 8, D)
    W = s.carve(KT_PER_D, D)
    A = s.carve(KT_PER_D, P)
    B = s.carve(D)
    wqkv = s.carve(KT_PER_D, QKW)
    wvb = s.carve(H, KVR)
    rW = s.carve(KT_PER_D, NE)
    xnT = s.carve(2, KT_PER_D, P)
    tT = s.carve(2, P)
    junk = s.carve(P)
    st, mv, rs, tmp = s.carve(NT, 6), s.carve(NT, 2), s.carve(NT), s.carve(NT)
    qm, qmT, lg, m8, ex, sm8, rexp, rt = (s.carve(D), s.carve(KT_PER_D, NB), s.carve(NE), s.carve(1), s.carve(NE),
                                          s.carve(1), s.carve(NE, RANK), s.carve(NB))
    bias = s.vecs[:, 0:D]
    rbias = s.vecs[0:NB, D + QR + KVR:D + QR + KVR + NE]

    x_in = [sem(f"x_in{i}") for i in range(4)]
    consts_in, gate_w_in, qkv_w_in, fold_q_in, fold_v_in = (sem(n) for n in (
        "consts_in", "gate_w_in", "qkv_w_in", "fold_q_in", "fold_v_in"))
    wo_in = [sem(f"wo_in{i}") for i in range(2)]
    cast, var_ready, std_ready, xn_ready, dv, junk_done = (sem(n) for n in (
        "cast", "var_ready", "std_ready", "xn_ready", "first_dve", "junk_done"))
    means, means_out, means_t, means_t_out, logits, logits_out, exps, rexp_ready, rt_ps, rt_ready = (sem(n) for n in (
        "means", "means_out", "means_t", "means_t_out", "logits", "logits_out", "exps", "rexp_ready", "rt_ps",
        "rt_ready"))
    foldq, foldq_out, foldo, foldo_out = (sem(n) for n in ("foldq", "foldq_out", "foldo", "foldo_out"))
    turned, turned_out, lo_done, base_done, gate_done = (sem(n) for n in (
        "turned", "turned_out", "lo_done", "base_done", "gate_done"))
    qka_out, squares, tT_ready, gate_out, silu_done = (sem(n) for n in (
        "qka_out", "squares", "tT_ready", "gate_out", "silu_done"))

    with nc.Block() as block:
        @block.sync
        def _(sp):
            sp.dma_start(s.C[:, :], a["consts"]).then_inc(consts_in, 16)
            for g in range(4):
                sp.dma_start(X[:, 4 * g:4 * g + 4, :],
                             a["x"][512 * g:512 * g + 512, :].rearrange("(t p) h -> p t h", p=P)).then_inc(x_in[g], 16)
            sp.dma_start(wqkv, a["wqkv"]).then_inc(qkv_w_in, 16)
            sp.dma_start(s.WqT[:, :, 0:ROPE], a["wq_rope"]).then_inc(fold_q_in, 16)
            for c in range(4):
                if c >= 2:
                    sp.wait_ge(foldo, 2 * (c - 1))
                sp.dma_start(wo[:, c % 2], a["wo"][:, 8 * c:8 * c + 8, :]).then_inc(wo_in[c % 2], 16)

        @block.scalar
        def _(act):
            act.dma_start(s.vecs[:, :], a["vecs"].broadcast_to([P, D + QR + KVR + NE])).then_inc(consts_in, 16)
            act.dma_start(wqn[0:NOPE], a["wq_nope"]).then_inc(fold_q_in, 16)
            act.dma_start(wkb[0:NOPE], a["wkv_k"]).then_inc(fold_q_in, 16)
            act.dma_start(rW, a["router"]).then_inc(gate_w_in, 16)
            act.dma_start(A, a["lora_a"]).then_inc(gate_w_in, 16)
            act.dma_start(B, a["lora_b"]).then_inc(gate_w_in, 16)
            act.dma_start(W, a["gate_w"]).then_inc(gate_w_in, 16)
            act.dma_start(wvb, a["wkv_v"]).then_inc(fold_v_in, 16)
            for g in range(4):
                act.wait_ge(var_ready, g + 1)
                nc.scalar.activation(tmp[:, 4 * g:4 * g + 4], mv[:, 4 * g:4 * g + 4, 1], ACT.Sqrt).then_inc(std_ready, 1)
            for g in range(2):
                act.wait_ge(foldq, g + 1)
                nc.scalar.activation(s.WqT[:, 16 * g:16 * g + 16, ROPE:KC],
                                     psum(4 + g).rearrange("p (h c) -> p h c", h=16), ACT.Copy).then_inc(foldq_out, 1)
            act.wait_ge(logits_out, 2)
            nc.scalar.activation(ex[0:NB], lg[0:NB], ACT.Exp, bias=m8[0:NB], accum_out=sm8[0:NB]).then_inc(exps, 1)

            def turn_out(t):
                act.wait_ge(turned, t + 1)
                if t >= 2:
                    act.wait_ge(base_done, t - 1)
                nc.scalar.activation(xnT[:, t % 2], psum(t % 2).rearrange("p (k n) -> p k n", k=4),
                                     ACT.Copy).then_inc(turned_out, 1)

            junks = Chain(act, junk_done)
            turn_out(0)
            for t in range(NT):
                if t + 1 < NT:
                    turn_out(t + 1)
                act.wait_ge(qka_out, t + 1)
                if t:
                    junks.wait()
                junks.then(nc.scalar.activation(junk, s.QKA[:, t, 0:QR], ACT.Square, accum_out=s.ss[:, t, 0:1]))
                junks(nc.scalar.activation(junk[:, 0:KVR], s.QKA[:, t, QR + ROPE:QKW], ACT.Square,
                                           accum_out=s.ss[:, t, 1:2]))
                if t % 4 == 0 and t:
                    for i in range(t // 2 - 2, t // 2):
                        act.wait_ge(foldo, i + 1)
                        nc.scalar.activation(s.WoP[:, i], psum(6 + i % 2), ACT.Copy).then_inc(foldo_out, 1)
                if t:
                    act.wait_ge(gate_out, t)
                    nc.scalar.activation(XN[:, t - 1], XN[:, t - 1], ACT.Silu).then_inc(silu_done, 1)
            act.wait_ge(gate_out, NT)
            nc.scalar.activation(XN[:, NT - 1], XN[:, NT - 1], ACT.Silu).then_inc(silu_done, 1)
            for i in range(6, 8):
                act.wait_ge(foldo, i + 1)
                nc.scalar.activation(s.WoP[:, i], psum(6 + i % 2), ACT.Copy).then_inc(foldo_out, 1)

        @block.vector
        def _(dve):
            v = nc.vector
            step = Chain(dve, dv)
            dve.wait_ge(consts_in, 32)
            v.tensor_copy(s.identb[:, :], ident).then_inc(cast, 1)
            v.tensor_copy(s.maskb[:, :], const("causal")).then_inc(cast, 1)
            for g in range(4):
                q = slice(4 * g, 4 * g + 4)
                dve.wait_ge(x_in[g], 16)
                for t in range(4 * g, 4 * g + 4):
                    step(v.bn_stats(st[:, t], X[:, t]))
                step.wait()
                for t in range(4 * g, 4 * g + 4):
                    step(v.bn_aggr(mv[:, t], st[:, t]))
                step.wait()
                v.tensor_scalar(mv[:, q, 1], mv[:, q, 1], LN_EPS, None, ALU.add).then_inc(var_ready, 1)
                dve.wait_ge(std_ready, g + 1)
                rsqrt_refined(v, step, rs[:, q], tmp[:, q], mv[:, q, 1])
                for t in range(4 * g, 4 * g + 4):
                    v.tensor_scalar(XN[:, t], X[:, t], mv[:, t, 0:1], rs[:, t:t + 1], ALU.subtract,
                                    ALU.mult).then_inc(xn_ready, 1)
            dve.wait_ge(means, 1)
            v.tensor_copy(qm[0:NB], psum(6)[0:NB]).then_inc(means_out, 1)
            dve.wait_ge(means_t, 1)
            v.tensor_copy(qmT, psum(7)[:, 0:32].rearrange("p (k b) -> p k b", k=4)).then_inc(means_t_out, 1)
            dve.wait_ge(logits, 1)
            step.then(v.tensor_tensor(lg[0:NB], psum(7)[0:NB, 64:64 + NE], rbias, ALU.add))
            step.then(v.tensor_reduce(m8[0:NB], lg[0:NB], AX.X, ALU.max))
            v.tensor_scalar(m8[0:NB], m8[0:NB], -1.0, None, ALU.mult).then_inc(logits_out, 2)
            dve.wait_ge(exps, 1)
            step.then(v.reciprocal(sm8[0:NB], sm8[0:NB]))
            step.then(v.tensor_scalar(lg[0:NB], ex[0:NB], sm8[0:NB], LORA_SCALE, ALU.mult, ALU.mult))
            v.tensor_copy(rexp[0:NB], lg[0:NB].unsqueeze(2).broadcast_to([NB, NE, RANK])).then_inc(rexp_ready, 1)
            dve.wait_ge(rt_ps, 1)
            v.tensor_copy(rt, psum(7)[:, 128:128 + NB]).then_inc(rt_ready, 1)
            dve.wait_ge(rt_ready, 1)
            for t in range(NT):
                ps = psum(2 + t % 2)
                dve.wait_ge(lo_done, t + 1)
                if t >= 2:
                    dve.wait_ge(gate_done, t - 1)
                v.tensor_scalar(tT[:, t % 2], ps[:, 256:256 + P], rt[:, t // 2:t // 2 + 1], None,
                                ALU.mult).then_inc(tT_ready, 1)
                v.tensor_copy(s.QKA[:, t], ps[:, 0:QKW]).then_inc(qka_out, 1)
                dve.wait_ge(gate_done, t + 1)
                v.tensor_tensor(XN[:, t], psum(4 + t % 2), bias, ALU.add).then_inc(gate_out, 1)

        @block.tensor
        def _(pe):
            mm = nc.tensor.matmul
            pe.wait_ge(consts_in, 32)
            mean = const("mean", "p (k c) -> p k c", k=2)
            for t in range(NT):
                pe.wait_ge(xn_ready, t + 1)
                b = t // 2
                last = mm(psum(6)[0:NB], mean[:, t % 2, 7 - b:15 - b], XN[:, t], start=(t == 0), stop=(t == NT - 1))
            last.then_inc(means, 1)
            pe.wait_ge(fold_q_in, 48)
            for g in range(2):
                for h in range(16 * g, 16 * g + 16):
                    last = mm(psum(4 + g)[:, 32 * (h % 16):32 * (h % 16) + 32], wqn[0:NOPE, h], wkb[0:NOPE, h],
                              start=True, stop=True)
                last.then_inc(foldq, 1)
            pe.wait_ge(means_out, 1)
            for k in range(4):
                last = nc.tensor.transpose(psum(7)[:, 8 * k:8 * k + 8], qm[0:NB, P * k:P * k + P], ident[0:NB, 0:NB])
            last.then_inc(means_t, 1)
            pe.wait_ge(means_t_out, 1)
            pe.wait_ge(gate_w_in, 64)
            for k in range(4):
                last = mm(psum(7)[0:NB, 64:64 + NE], qmT[:, k], rW[:, k], start=(k == 0), stop=(k == 3))
            last.then_inc(logits, 1)

            def turn(t):
                if t >= 2:
                    pe.wait_ge(turned_out, t - 1)
                for k in range(4):
                    last = nc.tensor.transpose(psum(t % 2)[:, P * k:P * k + P], XN[:, t, P * k:P * k + P], ident)
                last.then_inc(turned, 1)

            turn(0)
            pe.wait_ge(rexp_ready, 1)
            mm(psum(7)[:, 128:128 + NB], rexp[0:NB].rearrange("p e r -> p (e r)"), ident[0:NB, 0:NB], start=True,
               stop=True).then_inc(rt_ps, 1)
            pe.wait_ge(qkv_w_in, 16)
            pe.wait_ge(foldq_out, 2)
            for t in range(NT):
                if t + 1 < NT:
                    turn(t + 1)
                pe.wait_ge(turned_out, t + 1)
                if t >= 2:
                    pe.wait_ge(qka_out, t - 1)
                ps, xT = psum(2 + t % 2), xnT[:, t % 2]
                for k in range(4):
                    mm(ps[:, 0:QKW], xT[:, k], wqkv[:, k], start=(k == 0), stop=(k == 3))
                for k in range(4):
                    last = mm(ps[:, 256:256 + P], A[:, k], xT[:, k], start=(k == 0), stop=(k == 3))
                last.then_inc(lo_done, 1)
                if t >= 2:
                    pe.wait_ge(gate_out, t - 1)
                for k in range(4):
                    last = mm(psum(4 + t % 2), xT[:, k], W[:, k], start=(k == 0), stop=False)
                last.then_inc(base_done, 1)
                pe.wait_ge(tT_ready, t + 1)
                mm(psum(4 + t % 2), tT[:, t % 2], B, start=False, stop=True).then_inc(gate_done, 1)
                if t % 4 == 3:
                    c = t // 4
                    if c == 0:
                        pe.wait_ge(fold_v_in, 16)
                        pe.wait_ge(rt_ready, 1)
                    pe.wait_ge(wo_in[c % 2], 16 * (c // 2 + 1))
                    for i in (2 * c, 2 * c + 1):
                        if i >= 2:
                            pe.wait_ge(foldo_out, i - 1)
                        for j in range(4):
                            last = mm(psum(6 + i % 2)[32 * j:32 * j + 32], wvb[:, 4 * i + j],
                                      wo[:, c % 2, (4 * i + j) % 8], start=True, stop=True)
                        last.then_inc(foldo, 1)


def rsqrt_refined(v, step, r, root, x):
    step.then(v.reciprocal(r, root))
    step.then(v.tensor_tensor(root, r, r, ALU.mult))
    step.then(v.tensor_tensor(root, root, x, ALU.mult))
    step.then(v.tensor_scalar(root, root, -0.5, 1.5, ALU.mult, ALU.add))
    step.then(v.tensor_tensor(r, r, root, ALU.mult))


def normalise_latents(s):
    nc, sem, psum, const, ident = s.nc, s.sem, s.psum, s.const, s.ident
    QKA = s.QKA
    s.at = s.latents_at
    s.KR = s.carve(NT, KC)
    s.KT = s.carve(NT * P)
    s.QAT = s.carve(NT + 2, P)
    s.keep = s.at
    s.at += NT * QKW
    t2 = s.carve(NT, ROPE)
    var, root, rr = s.carve(NT, 2), s.carve(NT, 2), s.carve(NT, 2)
    qln = s.vecs[:, D:D + QR]
    kvln = s.vecs[:, D + QR:D + QR + KVR]
    lat_dve, var2, std2, rr_ready, q_ready, pl, k_ready, tq, tq_out, spare = (sem(n) for n in (
        "lat_dve", "var2", "std2", "rr_ready", "q_ready", "lat_pool", "k_ready", "tq", "tq_out", "spare"))

    with nc.Block() as block:
        @block.scalar
        def _(act):
            act.wait_ge(var2, 2)
            nc.scalar.activation(root, var, ACT.Sqrt).then_inc(std2, 1)
            for g in range(4):
                act.wait_ge(tq, g + 1)
                nc.scalar.activation(s.QAT[:, 4 * g:4 * g + 4], psum(g).rearrange("p (t n) -> p t n", t=4),
                                     ACT.Copy).then_inc(tq_out, 1)

        @block.vector
        def _(dve):
            v = nc.vector
            step = Chain(dve, lat_dve)
            v.tensor_scalar(var[:, :, 0], s.ss[:, :, 0], 1.0 / QR, RMS_EPS, ALU.mult, ALU.add).then_inc(var2, 1)
            v.tensor_scalar(var[:, :, 1], s.ss[:, :, 1], 1.0 / KVR, RMS_EPS, ALU.mult, ALU.add).then_inc(var2, 1)
            v.memset(s.QAT[:, NT:NT + 2], 0.0).then_inc(spare, 1)
            dve.wait_ge(std2, 1)
            rsqrt_refined(v, step, rr, root, var)
            v.tensor_copy(root, rr).then_inc(rr_ready, 1)
            for g in range(4):
                part = QKA[:, 4 * g:4 * g + 4, 0:QR]
                step.then(v.tensor_tensor(part, part, rr[:, 4 * g:4 * g + 4, 0:1].broadcast_to([P, 4, QR]), ALU.mult))
                v.tensor_tensor(part, part, qln.unsqueeze(1).broadcast_to([P, 4, QR]), ALU.mult).then_inc(q_ready, 1)
            for g in range(4):
                dve.wait_ge(tq, 4 + g + 1)
                v.tensor_copy(s.KT[0:KC, 512 * g:512 * g + 512], psum(4 + g)[0:KC]).then_inc(tq_out, 1)

        @block.gpsimd
        def _(pool):
            g = nc.gpsimd
            step = Chain(pool, pl)
            pe = QKA[:, :, QR:QR + ROPE].rearrange("p (b k) c -> p b k c", k=2)
            kr = s.KR[:, :, 0:ROPE].rearrange("p (b k) c -> p b k c", k=2)
            turn = t2.rearrange("p (b k) c -> p b k c", k=2)
            cos = const("cos", "p (k c) -> p k c", k=2)
            sin = const("sin", "p (k c) -> p k c", k=2)
            half = ROPE // 2

            def over_b(table):
                return table.unsqueeze(1).broadcast_to([P, NB, 2, table.shape[-1]])

            step(g.tensor_tensor(kr, pe, over_b(cos[:, :, 0:ROPE]), ALU.mult))
            step(g.tensor_tensor(turn[:, :, :, 0:half], pe[:, :, :, half:ROPE], over_b(sin[:, :, 0:half]), ALU.mult))
            step(g.tensor_tensor(turn[:, :, :, half:ROPE], pe[:, :, :, 0:half], over_b(sin[:, :, half:ROPE]), ALU.mult))
            step.wait()
            step(g.tensor_tensor(s.KR[:, :, 0:ROPE], s.KR[:, :, 0:ROPE], t2, ALU.add))
            pool.wait_ge(rr_ready, 1)
            lat = s.KR[:, :, ROPE:KC]
            step.then(g.tensor_tensor(lat, QKA[:, :, QR + ROPE:QKW], rr[:, :, 1:2].broadcast_to([P, NT, KVR]), ALU.mult))
            g.tensor_tensor(lat, lat, kvln.unsqueeze(1).broadcast_to([P, NT, KVR]), ALU.mult).then_inc(k_ready, 1)

        @block.tensor
        def _(pe):
            for g in range(4):
                pe.wait_ge(q_ready, g + 1)
                for i in range(4):
                    last = nc.tensor.transpose(psum(g)[:, P * i:P * i + P], QKA[:, 4 * g + i, 0:QR], ident)
                last.then_inc(tq, 1)
            pe.wait_ge(k_ready, 1)
            for g in range(4):
                for i in range(4):
                    last = nc.tensor.transpose(psum(4 + g)[0:KC, P * i:P * i + P], s.KR[:, 4 * g + i], ident)
                last.then_inc(tq, 1)


def attention(s):
    nc, sem, psum, const, ident = s.nc, s.sem, s.psum, s.const, s.ident
    X, XN = s.X, s.XN
    s.at = s.keep
    QT = s.carve(2, H, P)
    Pr = s.carve(4, 4, SEQ)
    PT = s.carve(2, 2, 4 * P)
    OT = s.carve(2, 8, P)
    qtok = s.carve(2, 4, KC)
    qrot = s.carve(2, 4, ROPE)
    qs = s.carve(2, P)
    cks = s.carve(2, KVR)
    prod = s.carve(D)
    mx, nb, sm, rs = s.carve(2, 4), s.carve(2, 4), s.carve(2, 4), s.carve(2, 4)
    half = ROPE // 2
    cos = const("cos", "p (k c) -> p k c", k=2)
    sin = const("sin", "p (k c) -> p k c", k=2)
    (scored, maxed, bias_ready, expd, summed, normed, chunk_done, roped, q_added, q_turned, q_out, p_turned, p_out,
     k1_turned, k1_out, pv_done, o_out, proj_done, proj_used, prod_ready, x_done, q_staged, v_staged) = (sem(n) for n in (
         "scored", "maxed", "bias_ready", "expd", "summed", "normed", "chunk_done", "roped", "q_added", "q_turned",
         "q_out", "p_turned", "p_out", "k1_turned", "k1_out", "pv_done", "o_out", "proj_done", "proj_used",
         "prod_ready", "x_done", "q_staged", "v_staged"))
    LAST = NB - 1
    PRO = 8

    def scores_bank(m):
        return s.bank[m % 2]

    def k1_before(m):
        return m - 2 if m < 2 else max(0, m - 10)

    def kw(m):
        return P if m % 16 < 8 else SEQ

    def heads(m):
        u = m % 8
        return [4 * (4 * (u // 4) + ii) + u % 4 for ii in range(4)]

    class PE:
        def __init__(self, pe):
            self.pe = pe

        def chunk(self, b, m, n):
            pe = self.pe
            qt = (m // 8 + 1) % 2
            pe.wait_ge(chunk_free := roped, n + PRO) if not (isinstance(n, int) and n + PRO <= 0) else None
            if m % 8 == 0:
                if m < 0:
                    pe.wait_ge(q_staged, 1)
                elif m == 0:
                    pe.wait_ge(q_staged, b * 2 + 2)
                else:
                    pe.wait_ge(q_staged, b * 2 + 3)
            u = m % 8
            nc.tensor.matmul(psum(6)[:, 0:4 * KC], qs[:, qt], s.WqT[:, 4 * u:4 * u + 4].rearrange("p h c -> p (h c)"),
                             start=True, stop=True).then_inc(chunk_done, 1)

        def turn_q(self, b, m, n):
            pe = self.pe
            pe.wait_ge(q_added, n + PRO)
            if not (isinstance(n, int) and n + PRO <= 1):
                pe.wait_ge(q_out, n + PRO - 1)
            if m >= 0 and not (isinstance(b, int) and b == 0 and k1_before(m) <= 0):
                pe.wait_ge(k1_out, b * 8 + k1_before(m))
            for hh in range(4):
                last = nc.tensor.transpose(psum(4)[0:KC, P * hh:P * hh + P], qtok[:, (m - 1) % 2, hh], ident)
            last.then_inc(q_turned, 1)

        def score(self, b, m, n):
            pe = self.pe
            qt, u = m // 8, m % 8
            pe.wait_ge(q_out, b * 16 + 8 * qt + 4 * (u // 4 + 1))
            if not (isinstance(n, int) and n < 2):
                pe.wait_ge(expd, n - 1)
            w = kw(m)
            ps = scores_bank(m)
            for hh, h in enumerate(heads(m)):
                nc.tensor.matmul(ps[:, w * hh:w * hh + w], QT[0:KC, qt, h], s.KT[0:KC, ds(b * SEQ, w)],
                                 start=True, stop=False, skip_group_check=True)
                last = nc.tensor.matmul(ps[:, w * (hh + 1) - P:w * (hh + 1)], s.identb[:, :], s.maskb[:, :],
                                        start=False, stop=True, skip_group_check=True)
            last.then_inc(scored, 1)

        def turn_p(self, m, n, kt):
            pe = self.pe
            if kt == 0:
                pe.wait_ge(normed, n + 1)
                if not (isinstance(n, int) and n < 1):
                    pe.wait_ge(p_out, n)
            for hh in range(4):
                last = nc.tensor.transpose(psum(5 - kt)[:, P * hh:P * hh + P],
                                           Pr[:, m % 4, hh, P * kt:P * kt + P], ident)
            last.then_inc(k1_turned if kt else p_turned, 1)

        def values(self, b, m, n):
            pe = self.pe
            pe.wait_ge(p_out, n + 1)
            if kw(m) == SEQ:
                pe.wait_ge(k1_out, b * 8 + (m - 8) + 1)
            if m % 4 == 0 and not (isinstance(n, int) and n < 4):
                pe.wait_ge(o_out, b * 4 + m // 4)
            if m == 0:
                pe.wait_ge(v_staged, b + 1)
            j = m % 4
            for kt in range(kw(m) // P):
                last = nc.tensor.matmul(psum(7)[32 * j:32 * j + 32], cks[:, kt], PT[:, m % 2, kt],
                                        start=(kt == 0), stop=(kt == kw(m) // P - 1))
            last.then_inc(pv_done, 1)

        def project(self, b, qt):
            pe = self.pe
            pe.wait_ge(o_out, b * 4 + 2 * qt + 2)
            for i in range(8):
                last = nc.tensor.matmul(psum(6), OT[:, qt, i], s.WoP[:, i], start=(i == 0), stop=(i == 7))
            last.then_inc(proj_done, 1)

    def parts(b, m, first):
        def behind(lag):
            if m - lag >= 0:
                return b, m - lag
            return None if first else (b - 1, m - lag + 16)
        return behind

    def pe_step(pe, b, m, first=False, live=True):
        n = b * 16 + m
        w = PE(pe)
        behind = parts(b, m, first)
        if m in (5, 13) and not (first and m == 5) or (not live and m == 3):
            bb, qt = (b - 1, 1) if m in (5, 3) else (b, 0)
            pe.wait_ge(roped, n + PRO if live else b * 16 + PRO)
            w.project(bb, qt)
        if live:
            w.score(b, m, n)
            if m in (5, 13) and not (first and m == 5):
                pe.wait_ge(proj_used, b * 2 if m == 5 else b * 2 + 1)
            w.chunk(b, m, n)
        two = behind(2)
        if two and (live or m < 2):
            w.turn_p(two[1], n - 2, 0)
        if live:
            w.turn_q(b, m, n)
        three = behind(3)
        if three and (live or m < 3):
            w.values(three[0], three[1], n - 3)
        if two and (live or m < 2) and kw(two[1]) == SEQ:
            if live:
                pe.wait_ge(q_out, n + PRO)
            elif m == 1 or True:
                pe.wait_ge(k1_out, two[0] * 8 + two[1] - 8)
            w.turn_p(two[1], n - 2, 1)

    def dve_step(dve, b, m, first=False, live=True):
        v = nc.vector
        n = b * 16 + m
        behind = parts(b, m, first)
        if m == 3 and live:
            if not first:
                dve.wait_ge(pv_done, b * 16)
            v.tensor_copy(cks, s.KR[:, ds(b * 2, 2), ROPE:KC]).then_inc(v_staged, 1)
        if m in (5, 13) and not (first and m == 5) or (not live and m == 3):
            tile = b * 2 - 1 if m in (5, 3) else b * 2
            dve.wait_ge(proj_done, tile + 1)
            if not (isinstance(tile, int) and tile == 0):
                dve.wait_ge(x_done, tile)
            v.tensor_tensor(prod, psum(6), XN[:, ds(tile, 1)].rearrange("p t n -> p (t n)"),
                            ALU.mult).then_inc(proj_used, 1)
            dve.wait_ge(proj_used, tile + 1)
            xt = X[:, ds(tile, 1)].rearrange("p t n -> p (t n)")
            v.tensor_tensor(xt, xt, prod, ALU.add).then_inc(x_done, 1)
        if live:
            par, w = m % 2, kw(m)
            dve.wait_ge(scored, n + 1)
            v.tensor_reduce(mx[:, par], scores_bank(m)[:, 0:4 * w].rearrange("p (h k) -> p h k", h=4), AX.X,
                            ALU.max).then_inc(maxed, 1)
            dve.wait_ge(maxed, n + 1)
            v.tensor_scalar(nb[:, par], mx[:, par], -SCALE, None, ALU.mult).then_inc(bias_ready, 1)
            rope(dve, b, m, n)
        one = behind(1)
        if one and (live or m < 1):
            dve.wait_ge(expd, n)
            if not (isinstance(n, int) and n < 3):
                dve.wait_ge(normed, n - 2)
            v.reciprocal(rs[:, one[1] % 2], sm[:, one[1] % 2]).then_inc(summed, 1)
        two = behind(2)
        if two and (live or m < 2):
            dve.wait_ge(p_turned, n - 1)
            v.tensor_copy(PT[:, two[1] % 2, 0], psum(5)).then_inc(p_out, 1)

    def rope(dve, b, m, n):
        v = nc.vector
        par, k = m % 2, (m // 8 + 1) % 2
        q = psum(6)[:, 0:4 * KC].rearrange("p (h c) -> p h c", h=4)
        dve.wait_ge(chunk_done, n + PRO + 1)
        if not (isinstance(n, int) and n + PRO < 2):
            dve.wait_ge(q_turned, n + PRO - 1)

        def over_h(table):
            return table.unsqueeze(1).broadcast_to([P, 4, table.shape[-1]])

        v.tensor_tensor(qtok[:, par], q, over_h(cos[:, k]), ALU.mult)
        v.tensor_tensor(qrot[:, par, :, 0:half], q[:, :, half:ROPE], over_h(sin[:, k, 0:half]), ALU.mult)
        v.tensor_tensor(qrot[:, par, :, half:ROPE], q[:, :, 0:half], over_h(sin[:, k, half:ROPE]),
                        ALU.mult).then_inc(roped, 1)

    def act_step(act, b, m, first=False, live=True):
        sc = nc.scalar
        n = b * 16 + m
        behind = parts(b, m, first)
        if live:
            if m == 1:
                act.wait_ge(chunk_done, b * 16 + PRO)
                sc.activation(qs[:, 0], s.QAT[:, ds(b * 2 + 2, 1)].rearrange("p t n -> p (t n)"),
                              ACT.Copy).then_inc(q_staged, 1)
            if m == 9:
                act.wait_ge(chunk_done, b * 16 + PRO + 8)
                sc.activation(qs[:, 1], s.QAT[:, ds(b * 2 + 3, 1)].rearrange("p t n -> p (t n)"),
                              ACT.Copy).then_inc(q_staged, 1)
            par, w = m % 2, kw(m)
            act.wait_ge(bias_ready, n + 1)
            for hh in range(4):
                last = sc.activation(Pr[:, m % 4, hh, 0:w], scores_bank(m)[:, w * hh:w * hh + w], ACT.Exp,
                                     bias=nb[:, par, hh:hh + 1], scale=SCALE, accum_out=sm[:, par, hh:hh + 1])
            last.then_inc(expd, 1)
            q_leaves(act, m, n)
        two = behind(2)
        if two and (live or m < 2) and kw(two[1]) == SEQ:
            act.wait_ge(k1_turned, two[0] * 8 + two[1] - 8 + 1)
            sc.activation(PT[:, two[1] % 2, 1], psum(4), ACT.Copy).then_inc(k1_out, 1)
        three = behind(3)
        if three and (live or m < 3) and three[1] % 4 == 3:
            act.wait_ge(pv_done, n - 2)
            qt, hf = three[1] // 8, three[1] // 4 % 2
            sc.activation(OT[:, qt, 4 * hf:4 * hf + 4], psum(7).rearrange("p (i q) -> p i q", i=4),
                          ACT.Copy).then_inc(o_out, 1)

    def q_leaves(act, m, n):
        act.wait_ge(q_turned, n + PRO)
        qt, u = ((m - 1) // 8 + 1) % 2, (m - 1) % 8
        nc.scalar.activation(QT[0:KC, qt, 4 * u:4 * u + 4], psum(4)[0:KC].rearrange("p (h q) -> p h q", h=4),
                             ACT.Copy).then_inc(q_out, 1)

    def pool_step(pool, b, m, first=False, live=True):
        g = nc.gpsimd
        n = b * 16 + m
        one = parts(b, m, first)(1)
        if one and (live or m < 1):
            pool.wait_ge(summed, n)
            w = kw(one[1])
            pr = Pr[:, one[1] % 4, :, 0:w]
            g.tensor_tensor(pr, pr, rs[:, one[1] % 2].unsqueeze(2).broadcast_to([P, 4, w]), ALU.mult).then_inc(normed, 1)
        if live:
            q_sum(pool, m, n)

    def q_sum(pool, m, n):
        pool.wait_ge(roped, n + PRO + 1)
        q = qtok[:, m % 2, :, 0:ROPE]
        nc.gpsimd.tensor_tensor(q, q, qrot[:, m % 2], ALU.add).then_inc(q_added, 1)

    def whole(eng, step):
        for m in range(16):
            step(eng, 0, m, first=True)
        with eng.Fori(1, NB) as b:
            for m in range(16):
                step(eng, b, m)
        for m in range(4):
            step(eng, NB, m, live=False)

    with nc.Block() as block:
        @block.tensor
        def _(pe):
            w = PE(pe)
            for m in range(-8, 0):
                w.chunk(0, m, m)
                if m > -8:
                    w.turn_q(0, m, m)
            whole(pe, pe_step)

        @block.vector
        def _(dve):
            for m in range(-8, 0):
                rope(dve, 0, m, m)
            whole(dve, dve_step)

        @block.scalar
        def _(act):
            for t in range(2):
                nc.scalar.activation(qs[:, t], s.QAT[:, t], ACT.Copy).then_inc(q_staged, 1)
            for m in range(-7, 0):
                q_leaves(act, m, m)
            whole(act, act_step)

        @block.gpsimd
        def _(pool):
            for m in range(-8, 0):
                q_sum(pool, m, m)
            whole(pool, pool_step)


def carve_layer2(s):
    s.at = 0
    s.slot = [s.carve(SLOT), s.carve(SLOT)]
    s.XT = s.slot[0][:, 0:NT * D].rearrange("p (k n) -> p k n", k=KT_PER_D)
    s.XP = s.slot[1][:, 0:NT * D].rearrange("p (k h b) -> p k h b", k=2, b=NB)
    s.slots = s.carve(NT, 2, dt=I32)
    s.gatew = s.carve(NT, 2)
    s.ready_at = s.carve(NBLK, dt=I32)
    s.slot_at = s.carve(NBLK, dt=I32)
    s.ends = s.carve(E, dt=I32)
    s.keep = s.at


SLOT = KT_PER_D * 2 * FF + (FT + 1) * D


def across_batch(s):
    nc, sem, psum, const, ident = s.nc, s.sem, s.psum, s.const, s.ident
    X, XN = s.X, s.XN
    carve_layer2(s)
    XP, XT = s.XP, s.XT
    st, mv, rs, root = s.carve(NT, 6), s.carve(NT, 2), s.carve(NT), s.carve(NT)
    g1 = s.carve(KT_PER_D, E)
    zeros = s.carve(D)
    ones = s.carve(P)
    LT = s.carve(NT * P)
    p = s.carve(NT, E)
    top, sums = s.carve(NT), s.carve(NT)
    big1, big2 = s.carve(NT, E, E), s.carve(NT, E, E)
    rank, first, second, chosen = s.carve(NT, E), s.carve(NT, E), s.carve(NT, E), s.carve(NT, E)
    within, cum, n_blocks, starts = s.carve(NT, E), s.carve(NT + 1, E), s.carve(E), s.carve(E + 1)
    over = s.carve(E, 16)
    which = s.carve(NBLK, E - 1)
    of_block = s.carve(NBLK)
    odd = s.carve(NBLK)
    slotf, vals = s.carve(NT, 2), s.carve(NT, 2)
    pr, pt, xg = s.carve(2, 4, P), s.carve(2, 4, P), s.carve(2, 2, 4, P)
    mx, nb, sm, rc = s.carve(2, 4), s.carve(2, 4), s.carve(2, 4), s.carve(2, 4)
    ROUNDS = 8
    INV = 1.0 / math.sqrt(SEQ)
    xs = s.nc.dram_tensor("rows_by_expert", [NBLK * P, D], F32, kind="Internal").ap()
    s.xs = xs
    by_group = XP.rearrange("p k (g l) b -> p k g (l b)", l=16)

    (dv, var_ready, std_ready, xn_ready, turned, turned_out, g1_in, zeroed, blank, logit, logit_out, lt, p_ex, p_exd,
     chosen_ready, counted, slots_ready, sorted_, mask_ready, batched) = (sem(n) for n in (
         "l2_dve", "l2_var", "l2_std", "xn1_ready", "x1_turned", "x1_turned_out", "g1_in", "zeroed", "blank",
         "logit", "logit_out", "logit_turned", "p_ex", "p_exd", "chosen_ready", "counted", "slots_ready", "sorted",
         "mask_ready", "batched"))
    (a_scored, a_maxed, a_bias, a_exp, a_recip, a_norm, a_pt, a_pt_out, a_xt, a_xt_a, a_xt_v, a_msg, a_added) = (
        sem(n) for n in ("a_scored", "a_maxed", "a_bias", "a_exp", "a_recip", "a_norm", "a_pt", "a_pt_out", "a_xt",
                         "a_xt_a", "a_xt_v", "a_msg", "a_added"))

    with nc.Block() as block:
        @block.sync
        def _(sp):
            sp.dma_start(g1, s.a["gate1"]).then_inc(g1_in, 16)
            sp.wait_ge(zeroed, 1)
            sp.dma_start(xs.rearrange("(n p) h -> p n h", p=P),
                         zeros.unsqueeze(1).broadcast_to([P, NBLK, D])).then_inc(blank, 16)

        @block.gpsimd
        def _(pool):
            nc.gpsimd.memset(zeros, 0.0).then_inc(zeroed, 1)
            nc.gpsimd.memset(ones, 1.0).then_inc(zeroed, 1)
            for t in range(NT):
                pool.wait_ge(xn_ready, t + 1)
                nc.gpsimd.tensor_copy(XP[:, t % 2, :, t // 2], XN[:, t]).then_inc(batched, 1)
            pool.wait_ge(blank, 16)
            pool.wait_ge(slots_ready, 1)
            for t in range(NT):
                for k in range(2):
                    nc.gpsimd.indirect_dma_start(
                        out=xs, out_offset=bass.IndirectOffsetOnAxis(ap=s.slots[:, t, k:k + 1], axis=0),
                        in_=XN[:, t], in_offset=None).then_inc(sorted_, 16)
            pool.wait_ge(sorted_, 16 * 2 * NT)

        @block.scalar
        def _(act):
            sc = nc.scalar
            for g in range(4):
                act.wait_ge(var_ready, g + 1)
                sc.activation(root[:, 4 * g:4 * g + 4], mv[:, 4 * g:4 * g + 4, 1], ACT.Sqrt).then_inc(std_ready, 1)
            for t in range(NT):
                act.wait_ge(turned, t + 1)
                sc.activation(XT[:, :, P * t:P * t + P], psum(t % 2).rearrange("p (k n) -> p k n", k=4),
                              ACT.Copy).then_inc(turned_out, 1)
            for c in range(4):
                act.wait_ge(logit, c + 1)
                sc.activation(LT[0:E, 512 * c:512 * c + 512], psum(2 + c % 2)[0:E], ACT.Copy).then_inc(logit_out, 1)
            act.wait_ge(p_ex, 1)
            sc.activation(p, p, ACT.Exp).then_inc(p_exd, 1)

            def bring_x(r):
                act.wait_ge(a_xt, 2 * r + 1)
                if r >= 2:
                    act.wait_ge(a_msg, 2 * (r - 1))
                sc.activation(xg[:, r % 2, 0], psum(4).rearrange("p (g c) -> p g c", g=4), ACT.Copy).then_inc(a_xt_a, 1)

            def bring_p(r):
                act.wait_ge(a_pt, r + 1)
                sc.activation(pt[:, r % 2], psum(6).rearrange("p (g c) -> p g c", g=4), ACT.Copy).then_inc(a_pt_out, 1)

            for r in range(ROUNDS + 1):
                if r < ROUNDS:
                    act.wait_ge(a_bias, r + 1)
                    for g in range(4):
                        last = sc.activation(pr[:, r % 2, g], psum(2 + r % 2)[:, P * g:P * g + P], ACT.Exp,
                                             bias=nb[:, r % 2, g:g + 1], scale=INV, accum_out=sm[:, r % 2, g:g + 1])
                    last.then_inc(a_exp, 1)
                    bring_x(r)
                if r >= 1:
                    bring_p(r - 1)

        @block.vector
        def _(dve):
            v = nc.vector
            step = Chain(dve, dv)
            v.tensor_copy(s.maskb[:, :], const("same_l")).then_inc(mask_ready, 1)
            for g in range(4):
                q = slice(4 * g, 4 * g + 4)
                for t in range(4 * g, 4 * g + 4):
                    step(v.bn_stats(st[:, t], X[:, t]))
                step.wait()
                for t in range(4 * g, 4 * g + 4):
                    step(v.bn_aggr(mv[:, t], st[:, t]))
                step.wait()
                v.tensor_scalar(mv[:, q, 1], mv[:, q, 1], LN_EPS, None, ALU.add).then_inc(var_ready, 1)
                dve.wait_ge(std_ready, g + 1)
                rsqrt_refined(v, step, rs[:, q], root[:, q], mv[:, q, 1])
                for t in range(4 * g, 4 * g + 4):
                    v.tensor_scalar(XN[:, t], X[:, t], mv[:, t, 0:1], rs[:, t:t + 1], ALU.subtract,
                                    ALU.mult).then_inc(xn_ready, 1)
            dve.wait_ge(lt, 1)
            step.then(v.tensor_copy(p, psum(7)[:, 0:P].rearrange("p (t e) -> p t e", t=NT)))
            step.then(v.tensor_reduce(top, p, AX.X, ALU.max))
            v.tensor_tensor(p, p, top.unsqueeze(2).broadcast_to([P, NT, E]), ALU.subtract).then_inc(p_ex, 1)
            dve.wait_ge(p_exd, 1)
            step.then(v.tensor_reduce(sums, p, AX.X, ALU.add))
            step.then(v.reciprocal(sums, sums))
            step.then(v.tensor_tensor(p, p, sums.unsqueeze(2).broadcast_to([P, NT, E]), ALU.mult))
            other = p.unsqueeze(2).broadcast_to([P, NT, E, E])
            this = p.unsqueeze(3).broadcast_to([P, NT, E, E])
            earlier = const("earlier_e", "p (e f) -> p e f", e=E).unsqueeze(1).broadcast_to([P, NT, E, E])
            step(v.tensor_tensor(big1, other, this, ALU.is_gt))
            step.then(v.tensor_tensor(big2, other, this, ALU.is_equal))
            step.then(v.tensor_tensor(big2, big2, earlier, ALU.mult))
            step.then(v.tensor_tensor(big1, big1, big2, ALU.add))
            step.then(v.tensor_reduce(rank, big1, AX.X, ALU.add))
            v.tensor_scalar(chosen, rank, 2.0, None, ALU.is_lt).then_inc(chosen_ready, 1)
            step(v.tensor_scalar(first, rank, 0.0, None, ALU.is_equal))
            step.then(v.tensor_scalar(second, rank, 1.0, None, ALU.is_equal))
            small1, small2 = big1[:, :, 0], big2[:, :, 0]
            step(v.tensor_tensor(small1, first, p, ALU.mult))
            step.then(v.tensor_tensor(small2, second, p, ALU.mult))
            step(v.tensor_reduce(vals[:, :, 0], small1, AX.X, ALU.add))
            step.then(v.tensor_reduce(vals[:, :, 1], small2, AX.X, ALU.add))
            step.then(v.tensor_tensor(sums, vals[:, :, 0], vals[:, :, 1], ALU.add))
            step.then(v.reciprocal(sums, sums))
            step.then(v.tensor_tensor(s.gatew, vals, sums.unsqueeze(2).broadcast_to([P, NT, 2]), ALU.mult))
            dve.wait_ge(counted, 1)
            step(v.tensor_copy(within, psum(7)[:, 128:256].rearrange("p (t e) -> p t e", t=NT)))
            step.then(v.memset(cum[:, 0], 0.0))
            for t in range(NT):
                step.then(v.tensor_tensor(cum[:, t + 1], cum[:, t], psum(7)[:, 256 + E * t:256 + E * t + E], ALU.add))
            step.then(v.tensor_tensor(over, cum[:, NT].unsqueeze(2).broadcast_to([P, E, 16]),
                                      const("tile_starts").unsqueeze(1).broadcast_to([P, E, 16]), ALU.is_gt))
            step(v.tensor_reduce(n_blocks, over, AX.X, ALU.add))
            step.then(v.memset(starts[:, 0:1], 0.0))
            for e in range(E):
                step.then(v.tensor_tensor(starts[:, e + 1:e + 2], starts[:, e:e + 1], n_blocks[:, e:e + 1], ALU.add))
            step(v.tensor_tensor(within, within, cum[:, 0:NT], ALU.add))
            step.then(v.tensor_scalar(n_blocks, starts[:, 0:E], float(P), None, ALU.mult))
            step.then(v.tensor_tensor(within, within, n_blocks.unsqueeze(1).broadcast_to([P, NT, E]), ALU.add))
            step(v.tensor_tensor(small1, first, within, ALU.mult))
            step.then(v.tensor_tensor(small2, second, within, ALU.mult))
            step(v.tensor_reduce(slotf[:, :, 0], small1, AX.X, ALU.add))
            step.then(v.tensor_reduce(slotf[:, :, 1], small2, AX.X, ALU.add))
            v.tensor_copy(s.slots, slotf).then_inc(slots_ready, 1)
            step(v.tensor_scalar(s.ends, starts[:, 1:E + 1], 1.0, None, ALU.add))
            step.then(v.tensor_tensor(which, const("block_ids").unsqueeze(2).broadcast_to([P, NBLK, E - 1]),
                                      starts[:, 1:E].unsqueeze(1).broadcast_to([P, NBLK, E - 1]), ALU.is_ge))
            step.then(v.tensor_reduce(of_block, which, AX.X, ALU.add))
            step(v.tensor_scalar(s.ready_at, of_block, 1.0, None, ALU.add))
            step.then(v.tensor_scalar(odd, of_block, 1.0, None, ALU.is_equal))
            for k in (3.0, 5.0, 7.0):
                step.then(v.scalar_tensor_tensor(out=odd, in0=of_block, scalar=k, in1=odd, op0=ALU.is_equal,
                                                 op1=ALU.add))
            step(v.tensor_scalar(s.slot_at, odd, float(SLOT), None, ALU.mult))

            for r in range(ROUNDS + 2):
                if r < ROUNDS:
                    dve.wait_ge(a_scored, r + 1)
                    v.tensor_reduce(mx[:, r % 2], psum(2 + r % 2).rearrange("p (g k) -> p g k", g=4), AX.X,
                                    ALU.max).then_inc(a_maxed, 1)
                    dve.wait_ge(a_maxed, r + 1)
                    v.tensor_scalar(nb[:, r % 2], mx[:, r % 2], -INV, None, ALU.mult).then_inc(a_bias, 1)
                    dve.wait_ge(a_xt, 2 * r + 2)
                    if r >= 2:
                        dve.wait_ge(a_msg, 2 * (r - 1))
                    v.tensor_copy(xg[:, r % 2, 1], psum(5).rearrange("p (g c) -> p g c", g=4)).then_inc(a_xt_v, 1)
                    dve.wait_ge(a_exp, r + 1)
                    v.reciprocal(rc[:, r % 2], sm[:, r % 2]).then_inc(a_recip, 1)
                    dve.wait_ge(a_recip, r + 1)
                    v.tensor_tensor(pr[:, r % 2], pr[:, r % 2], rc[:, r % 2].unsqueeze(2).broadcast_to([P, 4, P]),
                                    ALU.mult).then_inc(a_norm, 1)
                if r >= 2:
                    for k in range(2):
                        dve.wait_ge(a_msg, 2 * (r - 2) + k + 1)
                        of_round = by_group[:, k, 4 * (r - 2):4 * (r - 2) + 4].rearrange("p g c -> p (g c)")
                        v.tensor_tensor(of_round, psum(k), of_round, ALU.add).then_inc(a_added, 1)

        @block.tensor
        def _(pe):
            mm, tr = nc.tensor.matmul, nc.tensor.transpose
            for t in range(NT):
                pe.wait_ge(xn_ready, t + 1)
                if t >= 2:
                    pe.wait_ge(turned_out, t - 1)
                for k in range(4):
                    last = tr(psum(t % 2)[:, P * k:P * k + P], XN[:, t, P * k:P * k + P], ident)
                last.then_inc(turned, 1)
            pe.wait_ge(g1_in, 16)
            for c in range(4):
                pe.wait_ge(turned_out, 4 * c + 4)
                if c >= 2:
                    pe.wait_ge(logit_out, c - 1)
                for k in range(4):
                    last = mm(psum(2 + c % 2)[0:E], g1[:, k], XT[:, k, 512 * c:512 * c + 512], start=(k == 0),
                              stop=(k == 3))
                last.then_inc(logit, 1)
            for t in range(NT):
                pe.wait_ge(logit_out, t // 4 + 1)
                last = tr(psum(7)[:, E * t:E * t + E], LT[0:E, P * t:P * t + P], ident[0:E, 0:E])
            last.then_inc(lt, 1)

            def count():
                pe.wait_ge(chosen_ready, 1)
                pe.wait_ge(zeroed, 2)
                mm(psum(7)[:, 128:256], const("before"), chosen.rearrange("p t e -> p (t e)"), start=True, stop=True)
                mm(psum(7)[:, 256:384], ones, chosen.rearrange("p t e -> p (t e)"), start=True,
                   stop=True).then_inc(counted, 1)

            def score(r):
                if r >= 2:
                    pe.wait_ge(a_exp, r - 1)
                for g in range(4):
                    ps = psum(2 + r % 2)[:, P * g:P * g + P]
                    for k in range(2):
                        xk = by_group[:, k, 4 * r + g]
                        mm(ps, xk, xk, start=(k == 0), stop=False)
                    last = mm(ps, s.identb[:, :], s.maskb[:, :], start=False, stop=True)
                last.then_inc(a_scored, 1)

            def turn_x(r):
                for k in range(2):
                    if r:
                        pe.wait_ge(a_xt_v if k else a_xt_a, r)
                    for g in range(4):
                        last = tr(psum(4 + k)[:, P * g:P * g + P], by_group[:, k, 4 * r + g], ident)
                    last.then_inc(a_xt, 1)

            def turn_p(r):
                pe.wait_ge(a_norm, r + 1)
                if r:
                    pe.wait_ge(a_pt_out, r)
                for g in range(4):
                    last = tr(psum(6)[:, P * g:P * g + P], pr[:, r % 2, g], ident)
                last.then_inc(a_pt, 1)

            def message(r):
                pe.wait_ge(a_pt_out, r + 1)
                pe.wait_ge(a_xt_a, r + 1)
                pe.wait_ge(a_xt_v, r + 1)
                for k in range(2):
                    if r:
                        pe.wait_ge(a_added, 2 * (r - 1) + k + 1)
                    for g in range(4):
                        last = mm(psum(k)[:, P * g:P * g + P], xg[:, r % 2, k, g], pt[:, r % 2, g], start=True,
                                  stop=True)
                    last.then_inc(a_msg, 1)

            pe.wait_ge(mask_ready, 1)
            pe.wait_ge(batched, NT)
            count()
            for r in range(ROUNDS + 1):
                if r < ROUNDS:
                    score(r)
                    turn_x(r)
                if r >= 1:
                    turn_p(r - 1)
                    message(r - 1)


def experts(s):
    nc, sem, psum, ident = s.nc, s.sem, s.psum, s.ident
    s.at = s.keep
    xg, xgT = s.carve(2, D), s.carve(2, KT_PER_D, P)
    sg = s.carve(FF)
    act_ = s.carve(2, FF)
    actT = s.carve(FT + 1, P)
    y = s.carve(2, D)
    HF = FF // 2
    W13 = KT_PER_D * 2 * FF
    ys = nc.dram_tensor("results_by_row", [NBLK * P, D], F32, kind="Internal").ap()
    s.ys = ys
    xs = s.xs
    (w_in0, w_in1, w_ready, x_in0, x_in1, x_turned, x_turned_out, h_done, silu_out, act_ready, a_turned,
     a_out_a, a_out_v, y_done, y_out, y_in0, y_in1, moved) = (sem(n) for n in (
         "w_in0", "w_in1", "w_ready", "xrows_in0", "xrows_in1", "rows_turned", "rows_turned_out", "h_done",
         "silu_out", "act_ready", "act_turned", "act_out_a", "act_out_v", "y_done", "y_out", "y_stored0", "y_stored1",
         "moved"))
    w_in, x_in, y_in = (w_in0, w_in1), (x_in0, x_in1), (y_in0, y_in1)

    with nc.Block() as block:
        @block.gpsimd
        def _(pool):
            g = nc.gpsimd

            def bring(e):
                to = s.slot[e % 2]
                g.dma_start(to[:, 0:W13], s.a["w13"][e]).then_inc(w_in[e % 2], 16)
                g.dma_start(to[:, W13:W13 + FT * D].rearrange("p (t n) -> p t n", t=FT),
                            s.a["w2"][e, 0:FT * P].rearrange("(t p) n -> p t n", p=P)).then_inc(w_in[e % 2], 16)
                g.dma_start(to[0:FR, W13 + FT * D:SLOT], s.a["w2"][e, FT * P:FF]).then_inc(w_in[e % 2], 16)

            def arrived(e):
                pool.wait_ge(w_in[e % 2], 48 * (e // 2 + 1))
                pool.sem_inc(w_ready, 1)

            bring(0)
            pool.wait_ge(moved, NT)
            bring(1)
            arrived(0)
            arrived(1)
            for e in range(2, E):
                end = pool.value_load(s.ends[0:1, e - 2:e - 1], min_val=1, max_val=NBLK + 1)
                pool.wait_ge(y_done, end)
                pool.nop(nofuse=True)
                bring(e)
                arrived(e)

        @block.sync
        def _(sp):
            def load(b, par):
                sp.dma_start(xg[:, par], xs[ds(b * P, P), :]).then_inc(x_in[par], 16)

            def store(b, par):
                sp.wait_ge(y_out, b + 1)
                sp.dma_start(ys[ds(b * P, P), :], y[:, par]).then_inc(y_in[par], 16)

            load(0, 0)
            load(1, 1)
            sp.wait_ge(x_turned, 1)
            load(2, 0)
            store(0, 0)
            with sp.Fori(0, (NBLK - 3) // 2) as i:
                for par in (1, 0):
                    b = i * 2 + (1 if par else 2)
                    sp.wait_ge(x_turned, b + 1)
                    load(b + 2, par)
                    store(b, par)
            store(NBLK - 2, 1)
            store(NBLK - 1, 0)
            sp.wait_ge(y_in0, 16 * (NBLK // 2 + 1))
            sp.wait_ge(y_in1, 16 * (NBLK // 2))

        @block.scalar
        def _(act):
            sc = nc.scalar
            for t in range(NT):
                sc.activation(s.XN[:, t], s.XP[:, t % 2, :, t // 2], ACT.Copy).then_inc(moved, 1)

            def rows(b, par):
                act.wait_ge(x_turned, b + 1)
                sc.activation(xgT[:, par], psum(4).rearrange("p (k n) -> p k n", k=4), ACT.Copy).then_inc(
                    x_turned_out, 1)

            def step(act, b, par, first):
                for hf in range(2):
                    act.wait_ge(h_done, b * 2 + hf + 1)
                    if not (first and hf == 0):
                        act.wait_ge(act_ready, b * 2 + hf)
                    sc.activation(sg[:, HF * hf:HF * hf + HF], psum(2 * hf)[:, 0:HF], ACT.Silu).then_inc(silu_out, 1)
                    if hf == 0:
                        if not first:
                            act.wait_ge(a_turned, b)
                            sc.activation(actT[:, 0:4], psum(5).rearrange("p (t n) -> p t n", t=4),
                                          ACT.Copy).then_inc(a_out_a, 1)
                        rows(b + 1, 1 - par)

            rows(0, 0)
            step(act, 0, 0, True)
            with act.Fori(0, (NBLK - 3) // 2) as i:
                step(act, i * 2 + 1, 1, False)
                step(act, i * 2 + 2, 0, False)
            step(act, NBLK - 2, 1, False)
            b = NBLK - 1
            for hf in range(2):
                act.wait_ge(h_done, b * 2 + hf + 1)
                act.wait_ge(act_ready, b * 2 + hf)
                sc.activation(sg[:, HF * hf:HF * hf + HF], psum(2 * hf)[:, 0:HF], ACT.Silu).then_inc(silu_out, 1)
                if hf == 0:
                    act.wait_ge(a_turned, b)
                    sc.activation(actT[:, 0:4], psum(5).rearrange("p (t n) -> p t n", t=4),
                                  ACT.Copy).then_inc(a_out_a, 1)
            act.wait_ge(a_turned, NBLK)
            sc.activation(actT[:, 0:4], psum(5).rearrange("p (t n) -> p t n", t=4), ACT.Copy).then_inc(a_out_a, 1)

        @block.vector
        def _(dve):
            v = nc.vector

            def multiply(b, par, hf, first):
                dve.wait_ge(silu_out, b * 2 + hf + 1)
                v.tensor_tensor(act_[:, par, HF * hf:HF * hf + HF], sg[:, HF * hf:HF * hf + HF],
                                psum(2 * hf + 1)[:, 0:HF], ALU.mult).then_inc(act_ready, 1)

            def turned(b):
                dve.wait_ge(a_turned, b)
                v.tensor_copy(actT[:, 4:FT], psum(6)[:, 0:2 * P].rearrange("p (t n) -> p t n", t=2))
                v.tensor_copy(actT[0:FR, FT], psum(6)[0:FR, 2 * P:3 * P]).then_inc(a_out_v, 1)

            def result(b, par, early):
                dve.wait_ge(y_done, b + 1)
                if not early:
                    dve.wait_ge(y_in[1 - par], b * 8 - 8 if par == 1 else b * 8 - 16)
                v.tensor_copy(y[:, 1 - par], psum(7)).then_inc(y_out, 1)

            multiply(0, 0, 0, True)
            multiply(0, 0, 1, True)

            def step(b, par, early=False):
                multiply(b, par, 0, False)
                turned(b)
                multiply(b, par, 1, False)
                result(b, par, early)

            step(1, 1, True)
            step(2, 0, True)
            with dve.Fori(1, (NBLK - 1) // 2) as i:
                step(i * 2 + 1, 1)
                step(i * 2 + 2, 0)
            turned(NBLK)
            result(NBLK, 1, False)

        @block.tensor
        def _(pe):
            mm, tr = nc.tensor.matmul, nc.tensor.transpose

            def turn_rows(b, par):
                pe.wait_ge(x_in[par], b * 8 + 16 if par == 0 else b * 8 + 8)
                if not (isinstance(b, int) and b == 0):
                    pe.wait_ge(x_turned_out, b)
                for k in range(4):
                    last = tr(psum(4)[:, P * k:P * k + P], xg[:, par, P * k:P * k + P], ident)
                last.then_inc(x_turned, 1)

            def up(b, par, off, hf):
                pe.wait_ge(x_turned_out, b + 1)
                if not (isinstance(b, int) and b == 0):
                    pe.wait_ge(act_ready, b * 2 - 1 + hf)
                for w in range(2):
                    for k in range(4):
                        last = mm(psum(2 * hf + w)[:, 0:HF], xgT[:, par, k],
                                  s.R[:, ds(off + (k * 2 + w) * FF + hf * HF, HF)], start=(k == 0), stop=(k == 3))
                last.then_inc(h_done, 1)

            def turn_act(b, par):
                pe.wait_ge(act_ready, b * 2 + 2)
                for t in range(FT + 1):
                    n = P if t < FT else FR
                    ps = psum(5)[:, P * t:P * t + P] if t < 4 else psum(6)[0:n, P * (t - 4):P * (t - 4) + P]
                    last = tr(ps, act_[:, par, P * t:P * t + n], ident)
                last.then_inc(a_turned, 1)

            def down(b, off):
                pe.wait_ge(a_out_a, b + 1)
                pe.wait_ge(a_out_v, b + 1)
                if not (isinstance(b, int) and b == 0):
                    pe.wait_ge(y_out, b)
                for t in range(FT + 1):
                    n = P if t < FT else FR
                    last = mm(psum(7), actT[0:n, t], s.R[0:n, ds(off + W13 + t * D, D)], start=(t == 0), stop=(t == FT))
                last.then_inc(y_done, 1)

            def place(b):
                return pe.value_load(s.slot_at[0:1, ds(b, 1)], min_val=0, max_val=SLOT)

            def weights(b):
                off = place(b)
                pe.wait_ge(w_ready, pe.value_load(s.ready_at[0:1, ds(b, 1)], min_val=1, max_val=E))
                return off

            turn_rows(0, 0)
            off = weights(0)
            up(0, 0, off, 0)
            turn_rows(1, 1)
            up(0, 0, off, 1)
            pe.sem_inc(y_done, 1)

            def step(b, par, last=False):
                off = weights(b)
                up(b, par, off, 0)
                if not last:
                    turn_rows(b + 1, 1 - par)
                turn_act(b - 1, 1 - par)
                up(b, par, off, 1)
                before = place(b - 1)
                down(b - 1, before)

            with pe.Fori(0, (NBLK - 3) // 2) as i:
                step(i * 2 + 1, 1)
                step(i * 2 + 2, 0)
            step(NBLK - 2, 1)
            step(NBLK - 1, 0, last=True)
            turn_act(NBLK - 1, 0)
            down(NBLK - 1, place(NBLK - 1))


def combine(s):
    nc, sem = s.nc, s.sem
    X, XN = s.X, s.XN
    s.at = s.keep
    yy = s.carve(4, 2, D)
    z = s.carve(2, D)
    got = [sem(f"rows_got{i}") for i in range(4)]
    dv, mixed, gated, used, done, stored = (sem(n) for n in ("c_dve", "mixed", "c_gated", "used", "c_done", "stored"))
    with nc.Block() as block:
        @block.gpsimd
        def _(pool):
            for t in range(NT):
                if t >= 4:
                    pool.wait_ge(mixed, t - 3)
                for k in range(2):
                    nc.gpsimd.indirect_dma_start(
                        out=yy[:, t % 4, k], out_offset=None, in_=s.ys,
                        in_offset=bass.IndirectOffsetOnAxis(ap=s.slots[:, t, k:k + 1], axis=0)).then_inc(got[t % 4], 16)

        @block.vector
        def _(dve):
            v = nc.vector
            step = Chain(dve, dv)

            def finish(t):
                dve.wait_ge(gated, t + 1)
                step.then(v.tensor_tensor(z[:, t % 2], z[:, t % 2], XN[:, t], ALU.mult))
                v.tensor_tensor(X[:, t], X[:, t], z[:, t % 2], ALU.add).then_inc(done, 1)

            for t in range(NT):
                dve.wait_ge(got[t % 4], 32 * (t // 4 + 1))
                if t >= 2:
                    dve.wait_ge(done, t - 1)
                step.then(v.tensor_scalar(z[:, t % 2], yy[:, t % 4, 0], s.gatew[:, t, 0:1], None, ALU.mult))
                v.scalar_tensor_tensor(out=z[:, t % 2], in0=yy[:, t % 4, 1], scalar=s.gatew[:, t, 1:2],
                                       in1=z[:, t % 2], op0=ALU.mult, op1=ALU.add).then_inc(mixed, 1)
                if t:
                    finish(t - 1)
            finish(NT - 1)

        @block.scalar
        def _(act):
            for t in range(NT):
                act.wait_ge(mixed, t + 1)
                nc.scalar.activation(z[:, t % 2], z[:, t % 2], ACT.Silu).then_inc(gated, 1)

        @block.sync
        def _(sp):
            for t in range(NT):
                sp.wait_ge(done, t + 1)
                sp.dma_start(s.out[P * t:P * t + P, :], X[:, t]).then_inc(stored, 16)
            sp.wait_ge(stored, 16 * NT)


ROPE_ORDER = np.concatenate([np.arange(0, ROPE, 2), np.arange(1, ROPE, 2)])


def lay_out(i):
    f = lambda n: np.asarray(i[n])
    wqb = f("L0_attn_wq_b").reshape(H, NOPE + ROPE, QR)
    wkb = f("L0_attn_wkv_b").reshape(H, NOPE + VD, KVR)
    wkva = f("L0_attn_wkv_a")
    wkva = np.concatenate([wkva[KVR:][ROPE_ORDER], wkva[:KVR]], 0)

    def by_k(wt):
        return wt.reshape(KT_PER_D, P, -1).transpose(1, 0, 2)

    r = {
        "consts": shape_constants(),
        "x": f("L0_attn_x").reshape(NB * SEQ, D),
        "vecs": np.concatenate([f("L0_ffn_b"), f("L0_attn_q_a_ln_w"), f("L0_attn_kv_a_ln_w"), f("L0_ffn_router_b")])[None],
        "wqkv": by_k(np.concatenate([f("L0_attn_wq_a"), wkva], 0).T),
        "wq_rope": wqb[:, NOPE:][:, ROPE_ORDER].transpose(2, 0, 1),
        "wq_nope": wqb[:, :NOPE].transpose(1, 0, 2),
        "wkv_k": wkb[:, :NOPE].transpose(1, 0, 2),
        "wkv_v": wkb[:, NOPE:].transpose(1, 0, 2),
        "wo": f("L0_attn_wo").T.reshape(H, VD, D).transpose(1, 0, 2),
        "gate_w": by_k(f("L0_ffn_W").T),
        "lora_a": by_k(f("L0_ffn_A").reshape(NE * RANK, D).T),
        "lora_b": f("L0_ffn_B").transpose(0, 2, 1).reshape(NE * RANK, D),
        "router": by_k(f("L0_ffn_router_W").T),
        "gate1": by_k(f("L1_ffn_gate_w").T),
        "w13": np.stack([f("L1_ffn_w1"), f("L1_ffn_w3")], 1).reshape(E, 2, FF, KT_PER_D, P).transpose(0, 4, 3, 1, 2)
                 .reshape(E, P, KT_PER_D * 2 * FF),
        "w2": f("L1_ffn_w2").transpose(0, 2, 1),
    }
    return {k: np.ascontiguousarray(v) for k, v in r.items()}


def kernel(**inputs):
    import concourse.bacc as bacc
    from concourse.bass_utils import run_bass_kernel_spmd

    nc = bacc.Bacc("TRN2", target_bir_lowering=False, num_devices=1)
    arrays = lay_out(inputs)
    aps = {k: nc.dram_tensor(k, v.shape, mybir.dt.from_np(v.dtype), kind="ExternalInput").ap()
           for k, v in arrays.items()}
    out = nc.dram_tensor("out", (NB * SEQ, D), F32, kind="ExternalOutput").ap()
    build(nc, aps, out)
    r = run_bass_kernel_spmd(nc, [arrays], core_ids=[0])
    return r.results[0]["out"].reshape(NB, SEQ, D)
```

```python
import math
from contextlib import ExitStack

import numpy as np

import concourse.bass as bass
from concourse import mybir

F32 = mybir.dt.float32
F32R = mybir.dt.float32r
BF16 = mybir.dt.bfloat16
I32 = mybir.dt.int32
ALU = mybir.AluOpType
ACT = mybir.ActivationFunctionType
AX = mybir.AxisListType
ds = bass.ds

P = 128
NB, SEQ, D = 8, 256, 512
NT = NB * SEQ // P
KT_PER_D = D // P
H, NOPE, ROPE, VD, KVR, QR = 32, 64, 64, 128, 32, 128
KC = ROPE + KVR
QKW = QR + KC
NE, RANK = 8, 16
E, FF = 8, 800
FT = FF // P
FR = FF - FT * P
MSCALE = 0.1 * math.log(128.0) + 1.0
SCALE = (NOPE + ROPE) ** -0.5 * MSCALE * MSCALE
LORA_SCALE = 2.0
MEAN_FROM, MEAN_TO = 107, 255
LN_EPS, RMS_EPS = 1e-5, 1e-6
BIG = -1.0e30
HIGH, LOW = 0, 1
PASSES = ((HIGH, HIGH), (HIGH, LOW), (LOW, HIGH))
NBLK = 2 * NB * SEQ // P + E - 1

CONSTS = {}
_at = 0
for _name, _n in (("ident", P), ("causal", P), ("cos", 2 * KC), ("sin", 2 * ROPE), ("mean", 2 * 15),
                  ("same_l", P), ("before", P), ("earlier_e", E * E), ("tile_starts", 16), ("block_ids", NBLK)):
    CONSTS[_name] = (_at, _n)
    _at += _n
NCONST = _at
LAYER1_AT, LAYER2_AT = CONSTS["causal"][0], CONSTS["same_l"][0]

W13 = KT_PER_D * 2 * FF
SLOT = W13 + (FT + 1) * D
CHUNK = 2 * FF
CHUNKS = ([(k * 2 * FF, P, 2 * FF) for k in range(KT_PER_D)] +
          [(W13 + t * D, P, FT // 2 * D) for t in (0, FT // 2)] + [(W13 + FT * D, FR, D)])


def shape_constants():
    c = np.zeros((P, NCONST), np.float32)

    def put(name, a):
        at, n = CONSTS[name]
        c[:, at:at + n] = np.asarray(a, np.float32).reshape(P, n)

    p = np.arange(P)
    put("ident", np.eye(P))
    put("causal", np.where(p[None, :] <= p[:, None], 0.0, BIG))
    put("same_l", np.where(p[None, :] // NB == p[:, None] // NB, 0.0, BIG))
    put("before", p[:, None] < p[None, :])
    low = max(math.floor(ROPE * math.log(1024 / (32.0 * 2 * math.pi)) / (2 * math.log(10000.0))), 0)
    high = min(math.ceil(ROPE * math.log(1024 / (2 * math.pi)) / (2 * math.log(10000.0))), ROPE - 1)
    hi = high + 0.001 if low == high else float(high)
    keep = 1.0 - np.clip((np.arange(ROPE // 2, dtype=np.float32) - low) / (hi - low), 0.0, 1.0)
    extra = 1.0 / 10000.0 ** (np.arange(0, ROPE, 2, dtype=np.float32) / ROPE)
    freq = extra / 128.0 * (1.0 - keep) + extra * keep
    angle = np.outer(np.arange(SEQ, dtype=np.float32), freq)
    cos, sin = np.cos(angle), np.sin(angle)
    one = np.ones((SEQ, KVR))
    put("cos", np.concatenate([cos, cos, one], 1).reshape(2, P, KC).transpose(1, 0, 2))
    put("sin", np.concatenate([-sin, sin], 1).reshape(2, P, ROPE).transpose(1, 0, 2))
    mean = np.zeros((P, 2, 15))
    tok = p[:, None] + P * np.arange(2)[None, :]
    mean[:, :, 7] = ((tok >= MEAN_FROM) & (tok < MEAN_TO)) / (MEAN_TO - MEAN_FROM)
    put("mean", mean)
    e = np.arange(E)
    put("earlier_e", np.tile((e[None, :] < e[:, None]).reshape(1, -1), (P, 1)))
    put("tile_starts", np.tile(P * np.arange(16), (P, 1)))
    put("block_ids", np.tile(np.arange(NBLK), (P, 1)))
    return c


class Chain:

    def __init__(self, eng, sem, base=0):
        self.eng, self.sem, self.base, self.n = eng, sem, base, 0

    def __call__(self, ins):
        ins.then_inc(self.sem, 1)
        self.n += 1

    def wait(self):
        self.eng.wait_ge(self.sem, self.base + self.n)

    def then(self, ins):
        self(ins)
        self.wait()


def build(nc, a, out, dbg=None):
    with ExitStack() as ctx:
        s = Stages(nc, ctx, a, out, dbg or {})

        def sb(scope, name, shape, dt=F32):
            return scope.enter_context(nc.sbuf_tensor(name, shape, dt))

        s.ident = sb(ctx, "ident_sb", [P, P])[:, :]
        s.identb = sb(ctx, "identb", [P, P], BF16)
        s.maskb = sb(ctx, "maskb", [P, P], BF16)
        tables = sb(ctx, "tables", [P, 6 * NT + 2 * NBLK + E])
        s.X = sb(ctx, "x_keep", [P, NT, D])
        s.room(tables)
        s.mv = s.carve(NT, 2)
        s.slots = s.carve(NT, 2, dt=I32)
        s.gatew = s.carve(NT, 2)
        s.ready_at = s.carve(NBLK, dt=I32)
        s.slot_at = s.carve(NBLK, dt=I32)
        s.ends = s.carve(E, dt=I32)
        s.bank = [ctx.enter_context(nc.psum_tensor(f"bank{i}", [P, 1024], F32)) for i in range(4)]
        s.x1 = nc.dram_tensor("x_after_layer1", [NB * SEQ, D], F32, kind="Internal").ap()
        s.messages = nc.dram_tensor("layer2_attention", [NB * SEQ, D], F32, kind="Internal").ap()
        s.xs = nc.dram_tensor("rows_by_expert", [NBLK * P, D], F32, kind="Internal").ap()
        s.ys = nc.dram_tensor("results_by_row", [NBLK * P, D], F32, kind="Internal").ap()
        s.x1_stored, s.converted, s.raw0_in, s.kept_in = (s.sem(n) for n in (
            "x1_stored", "converted", "raw0_in", "kept_in"))
        s.messages_stored = [s.sem(f"messages_stored{i}") for i in range(4)]

        with ExitStack() as scope:
            s.C, s.C_from = sb(scope, "consts_sb", [P, LAYER2_AT - LAYER1_AT]), LAYER1_AT
            s.vecs = sb(scope, "vecs_sb", [P, D + QR + KVR + NE])
            s.XN = sb(scope, "xn_keep", [P, NT, D])
            s.Wq = sb(scope, "wq_parts", [P, 2, H * KC], F32R)
            s.qs = sb(scope, "q_latent_parts", [P, 2, 2, P], F32R)
            s.room(sb(scope, "room", [P, 28300]))
            first_projections(s)
            normalise_latents(s)
            attention(s)
        if s.dbg.get("stop") == "attn":
            return finish_dbg(s)

        with ExitStack() as scope:
            room2 = sb(scope, "room2", [P, 2 * SLOT])
            s.raw0 = sb(scope, "first_expert", [P, SLOT])
            s.result = sb(scope, "attention_out", [P, 2 * NT * 2 * 64])
            s.C, s.C_from = sb(scope, "consts2_sb", [P, NCONST - LAYER2_AT]), LAYER2_AT
            s.room(room2)
            across_batch(s)
        with ExitStack() as scope:
            s.W = sb(scope, "expert_weights", [P, 4 * SLOT], F32R)
            s.xgT = sb(scope, "rows_t", [P, 2, 2, KT_PER_D * P], F32R)
            s.actT = sb(scope, "act_t", [P, 2, (FT + 1) * P], F32R)
            s.room(s.X[:, :, :].rearrange("p t n -> p (t n)"))
        s.kept = sb(ctx, "kept", [P, 2, NT, D])
        experts(s)
        s.room(sb(ctx, "room3", [P, 10000]))
        combine(s)


def finish_dbg(s):
    sm = s.sem("dbg")
    with s.nc.Block() as blk:
        @blk.sync
        def _(sp):
            n = 0
            for name, view in s.dbg.get("dumps", lambda s: {})(s).items():
                sp.dma_start(s.dbg["outs"][name], view).then_inc(sm, 16)
                n += 16
            sp.wait_ge(sm, n)


class Stages:

    def __init__(self, nc, ctx, a, out, dbg):
        self.nc, self.ctx, self.a, self.out, self.dbg = nc, ctx, a, out, dbg

    def room(self, r):
        self.R, self.ROOM, self.at = r, r.shape[-1], 0

    def psum(self, i):
        return self.bank[i // 2][:, 512 * (i % 2):512 * (i % 2) + 512]

    def const(self, name, pattern=None, **k):
        at, n = CONSTS[name]
        v = self.C[:, at - self.C_from:at - self.C_from + n]
        return v.rearrange(pattern, **k) if pattern else v

    def sem(self, name):
        return self.ctx.enter_context(self.nc.semaphore(name))

    def carve(self, *shape, dt=F32):
        n = int(np.prod(shape))
        v = self.R[:, self.at:self.at + n]
        self.at += n
        assert self.at <= self.ROOM, self.at
        if dt != F32:
            v = v.bitcast(dt)
        if len(shape) > 1:
            names = "abcd"[:len(shape)]
            v = v.rearrange(f"p ({' '.join(names)}) -> p {' '.join(names)}", **dict(zip(names, shape)))
        return v


def first_projections(s):
    nc, a, sem = s.nc, s.a, s.sem
    X, XN, psum, const, ident = s.X, s.XN, s.psum, s.const, s.ident
    s.at = 0
    s.WoP = s.carve(NB, D)
    s.ss = s.carve(NT, 2)
    s.latents_at = s.at
    wqn = s.carve(H, QR)
    wkb = s.carve(H, KVR)
    s.at = s.latents_at + NT * KC + NT * P + NT * P
    s.QKA = s.carve(NT, QKW)
    wo = s.carve(2, 4, D)
    rope_raw = s.carve(H, ROPE)
    W = s.carve(KT_PER_D, D)
    A = s.carve(KT_PER_D, P)
    B = s.carve(D)
    wqkv = s.carve(KT_PER_D, QKW)
    wvb = s.carve(H, KVR)
    rW = s.carve(KT_PER_D, NE)
    xnT = s.carve(2, KT_PER_D, P)
    tT = s.carve(2, P)
    junk = s.carve(P)
    st, mv, rs, tmp = s.carve(NT, 6), s.carve(NT, 2), s.carve(NT), s.carve(NT)
    qm, qmT, lg, m8, ex, sm8, rexp, rt = (s.carve(D), s.carve(KT_PER_D, NB), s.carve(NE), s.carve(1), s.carve(NE),
                                          s.carve(1), s.carve(NE, RANK), s.carve(NB))
    bias = s.vecs[:, 0:D]
    wq = s.Wq[:, :, :].rearrange("p i (h c) -> p i h c", h=H)
    rbias = s.vecs[0:NB, D + QR + KVR:D + QR + KVR + NE]

    GROUPS = ((0, 1), (1, 4), (4, 10), (10, 16))
    x_in = [sem(f"x_in{i}") for i in range(len(GROUPS))]
    consts_in, gate_w_in, qkv_w_in, fold_q_in, fold_v_in = (sem(n) for n in (
        "consts_in", "gate_w_in", "qkv_w_in", "fold_q_in", "fold_v_in"))
    rope_in, rope_high, foldq_low = sem("rope_in"), sem("rope_high"), sem("foldq_low")
    wo_in = [sem(f"wo_in{i}") for i in range(2)]
    cast, var_ready, std_ready, xn_ready, dv, junk_done = (sem(n) for n in (
        "cast", "var_ready", "std_ready", "xn_ready", "first_dve", "junk_done"))
    means, means_out, means_t, means_t_out, logits, logits_out, exps, rexp_ready, rt_ps, rt_ready = (sem(n) for n in (
        "means", "means_out", "means_t", "means_t_out", "logits", "logits_out", "exps", "rexp_ready", "rt_ps",
        "rt_ready"))
    foldq, foldq_out, foldo, foldo_out = (sem(n) for n in ("foldq", "foldq_out", "foldo", "foldo_out"))
    turned, turned_out, lo_done, base_done, gate_done = (sem(n) for n in (
        "turned", "turned_out", "lo_done", "base_done", "gate_done"))
    qka_out, squares, tT_ready, gate_out, silu_done = (sem(n) for n in (
        "qka_out", "squares", "tT_ready", "gate_out", "silu_done"))

    with nc.Block() as block:
        @block.sync
        def _(sp):
            for g, (t0, t1) in enumerate(GROUPS):
                sp.dma_start(X[:, t0:t1, :],
                             a["x"][P * t0:P * t1, :].rearrange("(t p) h -> p t h", p=P)).then_inc(x_in[g], 16)
                if g == 1:
                    sp.dma_start(wqn[0:NOPE], a["wq_nope"]).then_inc(fold_q_in, 16)
                    sp.dma_start(wkb[0:NOPE], a["wkv_k"]).then_inc(fold_q_in, 16)
                if g == 0:
                    sp.dma_start(s.ident, a["consts"][:, 0:LAYER1_AT]).then_inc(consts_in, 16)
                    sp.dma_start(s.C[:, :], a["consts"][:, LAYER1_AT:LAYER2_AT]).then_inc(consts_in, 16)
            sp.dma_start(wqkv, a["wqkv"]).then_inc(qkv_w_in, 16)
            sp.dma_start(rope_raw, a["wq_rope"]).then_inc(rope_in, 16)
            for c in range(8):
                if c >= 2:
                    sp.wait_ge(foldo, c - 1)
                sp.dma_start(wo[:, c % 2], a["wo"][:, 4 * c:4 * c + 4, :]).then_inc(wo_in[c % 2], 16)

        @block.gpsimd
        def _(pool):
            pool.wait_ge(x_in[2], 16)
            pool.dma_start(rW, a["router"]).then_inc(gate_w_in, 16)
            pool.dma_start(A, a["lora_a"]).then_inc(gate_w_in, 16)
            pool.dma_start(B, a["lora_b"]).then_inc(gate_w_in, 16)
            pool.dma_start(W, a["gate_w"]).then_inc(gate_w_in, 16)
            pool.dma_start(wvb, a["wkv_v"]).then_inc(fold_v_in, 16)

        @block.scalar
        def _(act):
            act.dma_start(s.vecs[:, :], a["vecs"].broadcast_to([P, D + QR + KVR + NE])).then_inc(consts_in, 16)
            for g, (t0, t1) in enumerate(GROUPS):
                act.wait_ge(var_ready, g + 1)
                nc.scalar.activation(tmp[:, t0:t1], mv[:, t0:t1, 1], ACT.Sqrt).then_inc(std_ready, 1)
            for g in range(2):
                act.wait_ge(foldq, g + 1)
                nc.scalar.activation(wq[:, HIGH, 16 * g:16 * g + 16, ROPE:KC],
                                     psum(4 + g).rearrange("p (h c) -> p h c", h=16), ACT.Copy).then_inc(foldq_out, 1)
            act.wait_ge(logits_out, 2)
            nc.scalar.activation(ex[0:NB], lg[0:NB], ACT.Exp, bias=m8[0:NB], accum_out=sm8[0:NB]).then_inc(exps, 1)

            def turn_out(t):
                act.wait_ge(turned, t + 1)
                if t >= 2:
                    act.wait_ge(base_done, t - 1)
                nc.scalar.activation(xnT[:, t % 2], psum(t % 2).rearrange("p (k n) -> p k n", k=4),
                                     ACT.Copy).then_inc(turned_out, 1)

            junks = Chain(act, junk_done)
            turn_out(0)
            for t in range(NT):
                if t + 1 < NT:
                    turn_out(t + 1)
                if t == 2:
                    act.wait_ge(rope_in, 16)
                    nc.scalar.activation(wq[:, HIGH, :, 0:ROPE], rope_raw, ACT.Copy).then_inc(rope_high, 1)
                act.wait_ge(qka_out, t + 1)
                if t:
                    junks.wait()
                junks.then(nc.scalar.activation(junk, s.QKA[:, t, 0:QR], ACT.Square, accum_out=s.ss[:, t, 0:1]))
                junks(nc.scalar.activation(junk[:, 0:KVR], s.QKA[:, t, QR + ROPE:QKW], ACT.Square,
                                           accum_out=s.ss[:, t, 1:2]))
                if t % 4 == 0 and t:
                    for i in range(t // 2 - 2, t // 2):
                        act.wait_ge(foldo, i + 1)
                        nc.scalar.activation(s.WoP[:, i], psum(6 + i % 2), ACT.Copy).then_inc(foldo_out, 1)
                if t:
                    act.wait_ge(gate_out, t)
                    nc.scalar.activation(XN[:, t - 1], XN[:, t - 1], ACT.Silu).then_inc(silu_done, 1)
            act.wait_ge(gate_out, NT)
            nc.scalar.activation(XN[:, NT - 1], XN[:, NT - 1], ACT.Silu).then_inc(silu_done, 1)
            for i in range(6, 8):
                act.wait_ge(foldo, i + 1)
                nc.scalar.activation(s.WoP[:, i], psum(6 + i % 2), ACT.Copy).then_inc(foldo_out, 1)

        @block.vector
        def _(dve):
            v = nc.vector
            step = Chain(dve, dv)

            def statistics(g):
                dve.wait_ge(x_in[g], 16)
                for t in range(*GROUPS[g]):
                    step(v.bn_stats(st[:, t], X[:, t]))

            for g, (t0, t1) in enumerate(GROUPS):
                q = slice(t0, t1)
                if g == 0:
                    statistics(0)
                step.wait()
                for t in range(t0, t1):
                    step(v.bn_aggr(mv[:, t], st[:, t]))
                step.wait()
                v.tensor_scalar(mv[:, q, 1], mv[:, q, 1], LN_EPS, None, ALU.add).then_inc(var_ready, 1)
                if g + 1 < len(GROUPS):
                    statistics(g + 1)
                dve.wait_ge(std_ready, g + 1)
                rsqrt_refined(v, step, rs[:, q], tmp[:, q], mv[:, q, 1])
                for t in range(t0, t1):
                    v.tensor_scalar(XN[:, t], X[:, t], mv[:, t, 0:1], rs[:, t:t + 1], ALU.subtract,
                                    ALU.mult).then_inc(xn_ready, 1)
            dve.wait_ge(consts_in, 48)
            v.tensor_copy(s.identb[:, :], ident).then_inc(cast, 1)
            v.tensor_copy(s.maskb[:, :], const("causal")).then_inc(cast, 1)
            for g in range(2):
                dve.wait_ge(foldq_out, g + 1)
                v.tensor_tensor(wq[:, LOW, 16 * g:16 * g + 16, ROPE:KC], psum(4 + g).rearrange("p (h c) -> p h c", h=16),
                                wq[:, HIGH, 16 * g:16 * g + 16, ROPE:KC], ALU.subtract).then_inc(foldq_low, 1)
            dve.wait_ge(means, 1)
            v.tensor_copy(qm[0:NB], psum(6)[0:NB]).then_inc(means_out, 1)
            dve.wait_ge(means_t, 1)
            v.tensor_copy(qmT, psum(7)[:, 0:32].rearrange("p (k b) -> p k b", k=4)).then_inc(means_t_out, 1)
            dve.wait_ge(logits, 1)
            step.then(v.tensor_tensor(lg[0:NB], psum(7)[0:NB, 64:64 + NE], rbias, ALU.add))
            step.then(v.tensor_reduce(m8[0:NB], lg[0:NB], AX.X, ALU.max))
            v.tensor_scalar(m8[0:NB], m8[0:NB], -1.0, None, ALU.mult).then_inc(logits_out, 2)
            dve.wait_ge(exps, 1)
            step.then(v.reciprocal(sm8[0:NB], sm8[0:NB]))
            step.then(v.tensor_scalar(lg[0:NB], ex[0:NB], sm8[0:NB], LORA_SCALE, ALU.mult, ALU.mult))
            v.tensor_copy(rexp[0:NB], lg[0:NB].unsqueeze(2).broadcast_to([NB, NE, RANK])).then_inc(rexp_ready, 1)
            dve.wait_ge(rt_ps, 1)
            v.tensor_copy(rt, psum(7)[:, 128:128 + NB]).then_inc(rt_ready, 1)
            dve.wait_ge(rt_ready, 1)
            for t in range(NT):
                ps = psum(2 + t % 2)
                dve.wait_ge(lo_done, t + 1)
                if t >= 2:
                    dve.wait_ge(gate_done, t - 1)
                v.tensor_scalar(tT[:, t % 2], ps[:, 256:256 + P], rt[:, t // 2:t // 2 + 1], None,
                                ALU.mult).then_inc(tT_ready, 1)
                v.tensor_copy(s.QKA[:, t], ps[:, 0:QKW]).then_inc(qka_out, 1)
                if t == 3:
                    dve.wait_ge(rope_high, 1)
                    v.tensor_tensor(wq[:, LOW, :, 0:ROPE], rope_raw, wq[:, HIGH, :, 0:ROPE],
                                    ALU.subtract).then_inc(foldq_low, 1)
                dve.wait_ge(gate_done, t + 1)
                v.tensor_tensor(XN[:, t], psum(4 + t % 2), bias, ALU.add).then_inc(gate_out, 1)

        @block.tensor
        def _(pe):
            mm = nc.tensor.matmul
            pe.wait_ge(consts_in, 48)
            mean = const("mean", "p (k c) -> p k c", k=2)

            def fold_q(g):
                pe.wait_ge(fold_q_in, 32)
                for h in range(16 * g, 16 * g + 16):
                    last = mm(psum(4 + g)[:, 32 * (h % 16):32 * (h % 16) + 32], wqn[0:NOPE, h], wkb[0:NOPE, h],
                              start=True, stop=True)
                last.then_inc(foldq, 1)

            for t in range(NT):
                pe.wait_ge(xn_ready, t + 1)
                b = t // 2
                last = mm(psum(6)[0:NB], mean[:, t % 2, 7 - b:15 - b], XN[:, t], start=(t == 0), stop=(t == NT - 1))
                if t == NT - 1:
                    last.then_inc(means, 1)
                if t in (7, 11):
                    fold_q(t // 4 - 1)
            pe.wait_ge(means_out, 1)
            for k in range(4):
                last = nc.tensor.transpose(psum(7)[:, 8 * k:8 * k + 8], qm[0:NB, P * k:P * k + P], ident[0:NB, 0:NB])
            last.then_inc(means_t, 1)
            pe.wait_ge(means_t_out, 1)
            pe.wait_ge(gate_w_in, 64)
            for k in range(4):
                last = mm(psum(7)[0:NB, 64:64 + NE], qmT[:, k], rW[:, k], start=(k == 0), stop=(k == 3))
            last.then_inc(logits, 1)

            def turn(t):
                if t >= 2:
                    pe.wait_ge(turned_out, t - 1)
                for k in range(4):
                    last = nc.tensor.transpose(psum(t % 2)[:, P * k:P * k + P], XN[:, t, P * k:P * k + P], ident)
                last.then_inc(turned, 1)

            turn(0)
            pe.wait_ge(rexp_ready, 1)
            mm(psum(7)[:, 128:128 + NB], rexp[0:NB].rearrange("p e r -> p (e r)"), ident[0:NB, 0:NB], start=True,
               stop=True).then_inc(rt_ps, 1)
            pe.wait_ge(qkv_w_in, 16)
            pe.wait_ge(foldq_low, 2)
            for t in range(NT):
                if t + 1 < NT:
                    turn(t + 1)
                pe.wait_ge(turned_out, t + 1)
                if t >= 2:
                    pe.wait_ge(qka_out, t - 1)
                ps, xT = psum(2 + t % 2), xnT[:, t % 2]
                for k in range(4):
                    mm(ps[:, 0:QKW], xT[:, k], wqkv[:, k], start=(k == 0), stop=(k == 3))
                for k in range(4):
                    last = mm(ps[:, 256:256 + P], A[:, k], xT[:, k], start=(k == 0), stop=(k == 3))
                last.then_inc(lo_done, 1)
                if t >= 2:
                    pe.wait_ge(gate_out, t - 1)
                for k in range(4):
                    last = mm(psum(4 + t % 2), xT[:, k], W[:, k], start=(k == 0), stop=False)
                last.then_inc(base_done, 1)
                pe.wait_ge(tT_ready, t + 1)
                mm(psum(4 + t % 2), tT[:, t % 2], B, start=False, stop=True).then_inc(gate_done, 1)
                if t % 4 == 3:
                    c = t // 4
                    if c == 0:
                        pe.wait_ge(fold_v_in, 16)
                        pe.wait_ge(rt_ready, 1)
                    for i in (2 * c, 2 * c + 1):
                        pe.wait_ge(wo_in[i % 2], 16 * (i // 2 + 1))
                        if i >= 2:
                            pe.wait_ge(foldo_out, i - 1)
                        for j in range(4):
                            last = mm(psum(6 + i % 2)[32 * j:32 * j + 32], wvb[:, 4 * i + j],
                                      wo[:, i % 2, j], start=True, stop=True)
                        last.then_inc(foldo, 1)


def rsqrt_refined(v, step, r, root, x):
    step.then(v.reciprocal(r, root))
    step.then(v.tensor_tensor(root, r, r, ALU.mult))
    step.then(v.tensor_tensor(root, root, x, ALU.mult))
    step.then(v.tensor_scalar(root, root, -0.5, 1.5, ALU.mult, ALU.add))
    step.then(v.tensor_tensor(r, r, root, ALU.mult))


def normalise_latents(s):
    nc, sem, psum, const, ident = s.nc, s.sem, s.psum, s.const, s.ident
    QKA = s.QKA
    s.at = s.latents_at
    s.KR = s.carve(NT, KC)
    s.KT = s.carve(NT * P)
    s.QAT = s.carve(NT, P)
    s.keep = s.at
    s.at += NT * QKW
    t2 = s.carve(NT, ROPE)
    var, root, rr = s.carve(NT, 2), s.carve(NT, 2), s.carve(NT, 2)
    qln = s.vecs[:, D:D + QR]
    kvln = s.vecs[:, D + QR:D + QR + KVR]
    lat_dve, var2, std2, rr_ready, q_ready, pl, k_ready, tq, tq_out = (sem(n) for n in (
        "lat_dve", "var2", "std2", "rr_ready", "q_ready", "lat_pool", "k_ready", "tq", "tq_out"))

    with nc.Block() as block:
        @block.scalar
        def _(act):
            act.wait_ge(var2, 2)
            nc.scalar.activation(root, var, ACT.Sqrt).then_inc(std2, 1)
            for g in range(4):
                act.wait_ge(tq, g + 1)
                nc.scalar.activation(s.QAT[:, 4 * g:4 * g + 4], psum(g).rearrange("p (t n) -> p t n", t=4),
                                     ACT.Copy).then_inc(tq_out, 1)

        @block.vector
        def _(dve):
            v = nc.vector
            step = Chain(dve, lat_dve)
            v.tensor_scalar(var[:, :, 0], s.ss[:, :, 0], 1.0 / QR, RMS_EPS, ALU.mult, ALU.add).then_inc(var2, 1)
            v.tensor_scalar(var[:, :, 1], s.ss[:, :, 1], 1.0 / KVR, RMS_EPS, ALU.mult, ALU.add).then_inc(var2, 1)
            dve.wait_ge(std2, 1)
            rsqrt_refined(v, step, rr, root, var)
            v.tensor_copy(root, rr).then_inc(rr_ready, 1)
            for g in range(4):
                part = QKA[:, 4 * g:4 * g + 4, 0:QR]
                step.then(v.tensor_tensor(part, part, rr[:, 4 * g:4 * g + 4, 0:1].broadcast_to([P, 4, QR]), ALU.mult))
                v.tensor_tensor(part, part, qln.unsqueeze(1).broadcast_to([P, 4, QR]), ALU.mult).then_inc(q_ready, 1)
            for g in range(4):
                dve.wait_ge(tq, 4 + g + 1)
                v.tensor_copy(s.KT[0:KC, 512 * g:512 * g + 512], psum(4 + g)[0:KC]).then_inc(tq_out, 1)

        @block.gpsimd
        def _(pool):
            g = nc.gpsimd
            step = Chain(pool, pl)
            pe = QKA[:, :, QR:QR + ROPE].rearrange("p (b k) c -> p b k c", k=2)
            kr = s.KR[:, :, 0:ROPE].rearrange("p (b k) c -> p b k c", k=2)
            turn = t2.rearrange("p (b k) c -> p b k c", k=2)
            cos = const("cos", "p (k c) -> p k c", k=2)
            sin = const("sin", "p (k c) -> p k c", k=2)
            half = ROPE // 2

            def over_b(table):
                return table.unsqueeze(1).broadcast_to([P, NB, 2, table.shape[-1]])

            step(g.tensor_tensor(kr, pe, over_b(cos[:, :, 0:ROPE]), ALU.mult))
            step(g.tensor_tensor(turn[:, :, :, 0:half], pe[:, :, :, half:ROPE], over_b(sin[:, :, 0:half]), ALU.mult))
            step(g.tensor_tensor(turn[:, :, :, half:ROPE], pe[:, :, :, 0:half], over_b(sin[:, :, half:ROPE]), ALU.mult))
            step.wait()
            step(g.tensor_tensor(s.KR[:, :, 0:ROPE], s.KR[:, :, 0:ROPE], t2, ALU.add))
            pool.wait_ge(rr_ready, 1)
            lat = s.KR[:, :, ROPE:KC]
            step.then(g.tensor_tensor(lat, QKA[:, :, QR + ROPE:QKW], rr[:, :, 1:2].broadcast_to([P, NT, KVR]), ALU.mult))
            g.tensor_tensor(lat, lat, kvln.unsqueeze(1).broadcast_to([P, NT, KVR]), ALU.mult).then_inc(k_ready, 1)

        @block.tensor
        def _(pe):
            for g in range(4):
                pe.wait_ge(q_ready, g + 1)
                for i in range(4):
                    last = nc.tensor.transpose(psum(g)[:, P * i:P * i + P], QKA[:, 4 * g + i, 0:QR], ident)
                last.then_inc(tq, 1)
            pe.wait_ge(k_ready, 1)
            for g in range(4):
                for i in range(4):
                    last = nc.tensor.transpose(psum(4 + g)[0:KC, P * i:P * i + P], s.KR[:, 4 * g + i], ident)
                last.then_inc(tq, 1)


def attention(s):
    nc, sem, psum, const, ident = s.nc, s.sem, s.psum, s.const, s.ident
    X, XN = s.X, s.XN
    s.at = s.keep
    QT = s.carve(2, H, P)
    Pr = s.carve(4, 4, SEQ)
    PT = s.carve(2, 2, 4 * P)
    OT = s.carve(2, 8, P)
    qtok = s.carve(2, 4, KC)
    qrot = s.carve(2, 4, ROPE)
    cks = s.carve(2, KVR)
    x_new = s.carve(D)
    qs, Wq = s.qs, s.Wq
    mx, nb, sm, rs = s.carve(2, 4), s.carve(2, 4), s.carve(2, 4), s.carve(2, 4)
    st, mv = s.carve(6), s.carve(2)
    half = ROPE // 2
    cos = const("cos", "p (k c) -> p k c", k=2)
    sin = const("sin", "p (k c) -> p k c", k=2)
    (scored, maxed, bias_ready, expd, summed, normed, chunk_done, roped, q_added, q_turned, q_out, p_turned, p_out,
     k1_turned, k1_out, pv_done, o_out, proj_done, proj_used, prod_ready, x_done, q_staged, q_low, v_staged, x_summed,
     stats_done) = (sem(n) for n in (
         "scored", "maxed", "bias_ready", "expd", "summed", "normed", "chunk_done", "roped", "q_added", "q_turned",
         "q_out", "p_turned", "p_out", "k1_turned", "k1_out", "pv_done", "o_out", "proj_done", "proj_used",
         "prod_ready", "x_done", "q_staged", "q_low", "v_staged", "x_summed",
         "stats_done"))
    LAST = NB - 1
    PRO = 8

    def scores_bank(m):
        return s.bank[m % 2]

    def k1_before(m):
        return m - 1 if m < 2 else max(0, m - 9)

    def kw(m):
        return P if m % 16 < 8 else SEQ

    def heads(m):
        u = m % 8
        return [4 * (4 * (u // 4) + ii) + u % 4 for ii in range(4)]

    class PE:
        def __init__(self, pe):
            self.pe = pe

        def chunk(self, b, m, n):
            pe = self.pe
            qt = (m // 8 + 1) % 2
            pe.wait_ge(chunk_free := roped, n + PRO) if not (isinstance(n, int) and n + PRO <= 0) else None
            if m % 8 == 0:
                pe.wait_ge(q_low, 1 if m < 0 else b * 2 + (2 if m == 0 else 3))
            u = m % 8
            for i, (of_q, of_w) in enumerate(PASSES):
                last = nc.tensor.matmul(psum(6)[:, 0:4 * KC], qs[:, of_q, qt], Wq[:, of_w, 4 * KC * u:4 * KC * (u + 1)],
                                        start=(i == 0), stop=(i == 2))
            last.then_inc(chunk_done, 1)

        def turn_q(self, b, m, n):
            pe = self.pe
            pe.wait_ge(q_added, n + PRO)
            if not (isinstance(n, int) and n + PRO <= 1):
                pe.wait_ge(q_out, n + PRO - 1)
            if m >= 0 and not (isinstance(b, int) and b == 0 and k1_before(m) <= 0):
                pe.wait_ge(k1_out, b * 8 + k1_before(m))
            for hh in range(4):
                last = nc.tensor.transpose(psum(4)[0:KC, P * hh:P * hh + P], qtok[:, (m - 1) % 2, hh], ident)
            last.then_inc(q_turned, 1)

        def score(self, b, m, n):
            pe = self.pe
            qt, u = m // 8, m % 8
            pe.wait_ge(q_out, b * 16 + 8 * qt + 4 * (u // 4 + 1))
            if not (isinstance(n, int) and n < 2):
                pe.wait_ge(expd, n - 1)
            w = kw(m)
            ps = scores_bank(m)
            for hh, h in enumerate(heads(m)):
                nc.tensor.matmul(ps[:, w * hh:w * hh + w], QT[0:KC, qt, h], s.KT[0:KC, ds(b * SEQ, w)],
                                 start=True, stop=False, skip_group_check=True)
                last = nc.tensor.matmul(ps[:, w * (hh + 1) - P:w * (hh + 1)], s.identb[:, :], s.maskb[:, :],
                                        start=False, stop=True, skip_group_check=True)
            last.then_inc(scored, 1)

        def turn_p(self, m, n, kt):
            pe = self.pe
            if kt == 0:
                pe.wait_ge(normed, n + 1)
                if not (isinstance(n, int) and n < 1):
                    pe.wait_ge(p_out, n)
            for hh in range(4):
                last = nc.tensor.transpose(psum(5 - kt)[:, P * hh:P * hh + P],
                                           Pr[:, m % 4, hh, P * kt:P * kt + P], ident)
            last.then_inc(k1_turned if kt else p_turned, 1)

        def values(self, b, m, n):
            pe = self.pe
            pe.wait_ge(p_out, n + 1)
            if kw(m) == SEQ:
                pe.wait_ge(k1_out, b * 8 + (m - 8) + 1)
            if m % 4 == 0 and not (isinstance(n, int) and n < 4):
                pe.wait_ge(o_out, b * 4 + m // 4)
            if m == 0:
                pe.wait_ge(v_staged, b + 1)
            j = m % 4
            for kt in range(kw(m) // P):
                last = nc.tensor.matmul(psum(7)[32 * j:32 * j + 32], cks[:, kt], PT[:, m % 2, kt],
                                        start=(kt == 0), stop=(kt == kw(m) // P - 1))
            last.then_inc(pv_done, 1)

        def project(self, b, qt):
            pe = self.pe
            pe.wait_ge(o_out, b * 4 + 2 * qt + 2)
            for i in range(8):
                last = nc.tensor.matmul(psum(6), OT[:, qt, i], s.WoP[:, i], start=(i == 0), stop=(i == 7))
            last.then_inc(proj_done, 1)

    def last_entry(b):
        return isinstance(b, int) and b >= LAST

    def chunk_here(b, m, live):
        return live and not (last_entry(b) and m >= 8)

    def chunk_turned(b, m, live):
        return live and not (last_entry(b) and m >= 9)

    def chunks_before(b, m, n, live):
        return n + PRO if not last_entry(b) or (b == LAST and m <= 8) else 16 * NB

    def parts(b, m, first):
        def behind(lag):
            if m - lag >= 0:
                return b, m - lag
            return None if first else (b - 1, m - lag + 16)
        return behind

    def pe_step(pe, b, m, first=False, live=True):
        n = b * 16 + m
        w = PE(pe)
        behind = parts(b, m, first)
        if m in (5, 13) and not (first and m == 5) or (not live and m == 3):
            bb, qt = (b - 1, 1) if m in (5, 3) else (b, 0)
            pe.wait_ge(roped, chunks_before(b, m, n, live))
            w.project(bb, qt)
        if live:
            w.score(b, m, n)
            if chunk_here(b, m, live):
                if m in (5, 13) and not (first and m == 5):
                    pe.wait_ge(proj_used, b * 2 if m == 5 else b * 2 + 1)
                w.chunk(b, m, n)
        two = behind(2)
        if two and (live or m < 2):
            w.turn_p(two[1], n - 2, 0)
            if kw(two[1]) == SEQ:
                if last_entry(b) and (b > LAST or m > 10):
                    pe.wait_ge(k1_out, two[0] * 8 + two[1] - 8)
                else:
                    pe.wait_ge(q_out, min(n + PRO - 1, 16 * NB) if last_entry(b) else n + PRO - 1)
                w.turn_p(two[1], n - 2, 1)
        three = behind(3)
        if three and (live or m < 3):
            w.values(three[0], three[1], n - 3)
        if chunk_turned(b, m, live):
            w.turn_q(b, m, n)

    def dve_step(dve, b, m, first=False, live=True):
        v = nc.vector
        n = b * 16 + m
        behind = parts(b, m, first)
        if m == 3 and live:
            if not first:
                dve.wait_ge(pv_done, b * 16)
            v.tensor_copy(cks, s.KR[:, ds(b * 2, 2), ROPE:KC]).then_inc(v_staged, 1)
        tile = None
        if m in (5, 13) and not (first and m == 5) or (not live and m == 3):
            tile = b * 2 - 1 if m in (5, 3) else b * 2
            dve.wait_ge(proj_done, tile + 1)
            if not (isinstance(tile, int) and tile == 0):
                dve.wait_ge(x_done, tile)
                dve.wait_ge(stats_done, tile * 3)
            v.tensor_tensor(x_new, psum(6), XN[:, ds(tile, 1)].rearrange("p t n -> p (t n)"),
                            ALU.mult).then_inc(proj_used, 1)
            dve.wait_ge(proj_used, tile + 1)
            v.tensor_tensor(x_new, X[:, ds(tile, 1)].rearrange("p t n -> p (t n)"), x_new, ALU.add).then_inc(x_summed, 1)
        if live:
            par, w = m % 2, kw(m)
            dve.wait_ge(scored, n + 1)
            v.tensor_reduce(mx[:, par], scores_bank(m)[:, 0:4 * w].rearrange("p (h k) -> p h k", h=4), AX.X,
                            ALU.max).then_inc(maxed, 1)
            dve.wait_ge(maxed, n + 1)
            v.tensor_scalar(nb[:, par], mx[:, par], -SCALE, None, ALU.mult).then_inc(bias_ready, 1)
            if chunk_here(b, m, live):
                rope(dve, b, m, n)
            if m in (1, 9) and not last_entry(b):
                tile = b * 2 + (2 if m == 1 else 3)
                dve.wait_ge(q_staged, tile + 1)
                v.tensor_tensor(qs[:, LOW, m // 9], s.QAT[:, ds(tile, 1)].rearrange("p t n -> p (t n)"),
                                qs[:, HIGH, m // 9], ALU.subtract).then_inc(q_low, 1)
                tile = None
        one = behind(1)
        if one and (live or m < 1):
            dve.wait_ge(expd, n)
            if not (isinstance(n, int) and n < 3):
                dve.wait_ge(normed, n - 2)
            v.reciprocal(rs[:, one[1] % 2], sm[:, one[1] % 2]).then_inc(summed, 1)
        two = behind(2)
        if two and (live or m < 2):
            dve.wait_ge(p_turned, n - 1)
            v.tensor_copy(PT[:, two[1] % 2, 0], psum(5)).then_inc(p_out, 1)
        if tile is not None:
            dve.wait_ge(x_summed, tile + 1)
            v.bn_stats(st, x_new).then_inc(stats_done, 1)
            dve.wait_ge(stats_done, tile * 3 + 1)
            dve.nop(nofuse=True)
            v.bn_aggr(mv, st).then_inc(stats_done, 1)
            dve.wait_ge(stats_done, tile * 3 + 2)
            v.tensor_copy(s.mv[:, ds(tile, 1)].rearrange("p t n -> p (t n)"), mv).then_inc(stats_done, 1)

    def rope(dve, b, m, n):
        v = nc.vector
        par, k = m % 2, (m // 8 + 1) % 2
        q = psum(6)[:, 0:4 * KC].rearrange("p (h c) -> p h c", h=4)
        dve.wait_ge(chunk_done, n + PRO + 1)
        if not (isinstance(n, int) and n + PRO < 2):
            dve.wait_ge(q_turned, n + PRO - 1)

        def over_h(table):
            return table.unsqueeze(1).broadcast_to([P, 4, table.shape[-1]])

        v.tensor_tensor(qtok[:, par], q, over_h(cos[:, k]), ALU.mult)
        v.tensor_tensor(qrot[:, par, :, 0:half], q[:, :, half:ROPE], over_h(sin[:, k, 0:half]), ALU.mult)
        v.tensor_tensor(qrot[:, par, :, half:ROPE], q[:, :, 0:half], over_h(sin[:, k, half:ROPE]),
                        ALU.mult).then_inc(roped, 1)

    def act_step(act, b, m, first=False, live=True):
        sc = nc.scalar
        n = b * 16 + m
        behind = parts(b, m, first)
        two = behind(2)
        if two and (live or m < 2) and kw(two[1]) == SEQ:
            act.wait_ge(k1_turned, two[0] * 8 + two[1] - 8 + 1)
            sc.activation(PT[:, two[1] % 2, 1], psum(4), ACT.Copy).then_inc(k1_out, 1)
        if live:
            if m == 1 and not last_entry(b):
                act.wait_ge(chunk_done, b * 16 + PRO)
                sc.activation(qs[:, HIGH, 0], s.QAT[:, ds(b * 2 + 2, 1)].rearrange("p t n -> p (t n)"),
                              ACT.Copy).then_inc(q_staged, 1)
            if m == 9 and not last_entry(b):
                act.wait_ge(chunk_done, b * 16 + PRO + 8)
                sc.activation(qs[:, HIGH, 1], s.QAT[:, ds(b * 2 + 3, 1)].rearrange("p t n -> p (t n)"),
                              ACT.Copy).then_inc(q_staged, 1)
            par, w = m % 2, kw(m)
            act.wait_ge(bias_ready, n + 1)
            for hh in range(4):
                last = sc.activation(Pr[:, m % 4, hh, 0:w], scores_bank(m)[:, w * hh:w * hh + w], ACT.Exp,
                                     bias=nb[:, par, hh:hh + 1], scale=SCALE, accum_out=sm[:, par, hh:hh + 1])
            last.then_inc(expd, 1)
            if chunk_turned(b, m, live):
                q_leaves(act, m, n)
        three = behind(3)
        if three and (live or m < 3) and three[1] % 4 == 3:
            act.wait_ge(pv_done, n - 2)
            qt, hf = three[1] // 8, three[1] // 4 % 2
            sc.activation(OT[:, qt, 4 * hf:4 * hf + 4], psum(7).rearrange("p (i q) -> p i q", i=4),
                          ACT.Copy).then_inc(o_out, 1)
        if m in (5, 13) and not (first and m == 5) or (not live and m == 3):
            tile = b * 2 - 1 if m in (5, 3) else b * 2
            act.wait_ge(x_summed, tile + 1)
            nc.scalar.activation(X[:, ds(tile, 1)].rearrange("p t n -> p (t n)"), x_new, ACT.Copy).then_inc(x_done, 1)

    def q_leaves(act, m, n):
        act.wait_ge(q_turned, n + PRO)
        qt, u = ((m - 1) // 8 + 1) % 2, (m - 1) % 8
        nc.scalar.activation(QT[0:KC, qt, 4 * u:4 * u + 4], psum(4)[0:KC].rearrange("p (h q) -> p h q", h=4),
                             ACT.Copy).then_inc(q_out, 1)

    def pool_step(pool, b, m, first=False, live=True):
        g = nc.gpsimd
        n = b * 16 + m
        one = parts(b, m, first)(1)
        if one and (live or m < 1):
            pool.wait_ge(summed, n)
            w = kw(one[1])
            pr = Pr[:, one[1] % 4, :, 0:w]
            g.tensor_tensor(pr, pr, rs[:, one[1] % 2].unsqueeze(2).broadcast_to([P, 4, w]), ALU.mult).then_inc(normed, 1)
        if chunk_here(b, m, live):
            q_sum(pool, m, n)

    def q_sum(pool, m, n):
        pool.wait_ge(roped, n + PRO + 1)
        q = qtok[:, m % 2, :, 0:ROPE]
        nc.gpsimd.tensor_tensor(q, q, qrot[:, m % 2], ALU.add).then_inc(q_added, 1)

    def whole(eng, step):
        for m in range(16):
            step(eng, 0, m, first=True)
        with eng.Fori(1, LAST) as b:
            for m in range(16):
                step(eng, b, m)
        for m in range(16):
            step(eng, LAST, m)
        for m in range(4):
            step(eng, NB, m, live=False)

    with nc.Block() as block:
        @block.tensor
        def _(pe):
            w = PE(pe)
            for m in range(-8, 0):
                w.chunk(0, m, m)
                if m > -8:
                    w.turn_q(0, m, m)
            whole(pe, pe_step)

        @block.vector
        def _(dve):
            for t in range(2):
                dve.wait_ge(q_staged, t + 1)
                nc.vector.tensor_tensor(qs[:, LOW, t], s.QAT[:, t], qs[:, HIGH, t], ALU.subtract).then_inc(q_low, 1)
            for m in range(-8, 0):
                rope(dve, 0, m, m)
            whole(dve, dve_step)

        @block.scalar
        def _(act):
            for t in range(2):
                nc.scalar.activation(qs[:, HIGH, t], s.QAT[:, t], ACT.Copy).then_inc(q_staged, 1)
            for m in range(-7, 0):
                q_leaves(act, m, m)
            whole(act, act_step)

        @block.gpsimd
        def _(pool):
            for m in range(-8, 0):
                q_sum(pool, m, m)
            whole(pool, pool_step)

        @block.sync
        def _(sp):
            with sp.Fori(0, NT) as t:
                sp.wait_ge(x_done, t + 1)
                sp.dma_start(s.x1[ds(t * P, P), :], X[:, ds(t, 1)].rearrange("p t n -> p (t n)")).then_inc(
                    s.x1_stored, 16)


def bring_chunk(eng, s, e, c, to):
    at, rows, n = CHUNKS[c]
    if at < W13:
        return eng.dma_start(to[:, 0:n], s.a["w13"][e][:, at:at + n])
    t = (at - W13) // D
    if rows < P:
        return eng.dma_start(to[0:rows, 0:n], s.a["w2"][e, t * P:FF])
    return eng.dma_start(to[:, 0:n].rearrange("p (t n) -> p t n", n=D),
                         s.a["w2"][e, t * P:(t + n // D) * P].rearrange("(t p) n -> p t n", p=P))


def parts_of(s, c, at0):
    at, rows, n = CHUNKS[c]
    return s.W[0:rows, at0 + at:at0 + at + n], s.W[0:rows, at0 + SLOT + at:at0 + SLOT + at + n]


def across_batch(s):
    nc, sem, psum, const, ident = s.nc, s.sem, s.psum, s.const, s.ident
    X = s.X
    XP = s.carve(2, D, NB)
    XT = s.carve(2, KT_PER_D, 512)
    result = s.result[:, :].rearrange("p (r t c) -> p r t c", r=2, t=NT)
    mv, rs, root = s.mv, s.carve(NT), s.carve(NT)
    g1 = s.carve(KT_PER_D, E)
    zeros = s.carve(D)
    ones = s.carve(P)
    routing_at = s.at
    LT = s.carve(NT * P)
    p = s.carve(NT, E)
    top, sums = s.carve(NT), s.carve(NT)
    big1, big2 = s.carve(NT, E, E), s.carve(NT, E, E)
    rank, first, second, chosen = s.carve(NT, E), s.carve(NT, E), s.carve(NT, E), s.carve(NT, E)
    within, cum, n_blocks, starts = s.carve(NT, E), s.carve(NT + 1, E), s.carve(E), s.carve(E + 1)
    over = s.carve(E, 16)
    which = s.carve(NBLK, E - 1)
    of_block = s.carve(NBLK)
    odd = s.carve(NBLK)
    slotf, vals = s.carve(NT, 2), s.carve(NT, 2)
    s.at = routing_at
    pr, pt, xg = s.carve(3, 4, P), s.carve(2, 4, P), s.carve(3, 2, 4, P)
    mx, nb, sm, rc = s.carve(2, 4), s.carve(2, 4), s.carve(2, 4), s.carve(2, 4)
    ROUNDS = 8
    INV = 1.0 / math.sqrt(SEQ)
    xs = s.xs
    by_group = XP.rearrange("p k (g l) b -> p k g (l b)", l=16)

    (dv, var_ready, std_ready, xn_ready, turned, turned_out, g1_in, zeroed, blank, logit, logit_out, lt, p_ex, p_exd,
     chosen_ready, counted, slots_ready, sorted_, mask_ready, batched, consts2_in) = (sem(n) for n in (
         "l2_dve", "l2_var", "l2_std", "xn1_ready", "x1_turned", "x1_turned_out", "g1_in", "zeroed", "blank",
         "logit", "logit_out", "logit_turned", "p_ex", "p_exd", "chosen_ready", "counted", "slots_ready", "sorted",
         "mask_ready", "batched", "consts2_in"))
    (a_scored, a_maxed, a_bias, a_exp, a_recip, a_norm, a_pt, a_pt_out, a_xt, a_xt_a, a_xt_v, a_msg, a_added) = (
        sem(n) for n in ("a_scored", "a_maxed", "a_bias", "a_exp", "a_recip", "a_norm", "a_pt", "a_pt_out", "a_xt",
                         "a_xt_a", "a_xt_v", "a_msg", "a_added"))

    with nc.Block() as block:
        @block.sync
        def _(sp):
            sp.dma_start(g1, s.a["gate1"]).then_inc(g1_in, 16)
            sp.dma_start(s.C[:, :], s.a["consts"][:, LAYER2_AT:]).then_inc(consts2_in, 16)
            sp.wait_ge(zeroed, 1)
            sp.dma_start(xs.rearrange("(n p) h -> p n h", p=P),
                         zeros.unsqueeze(1).broadcast_to([P, NBLK, D])).then_inc(blank, 16)
            for c, (at, rows, n) in enumerate(CHUNKS):
                bring_chunk(sp, s, 0, c, s.raw0[:, at:at + n]).then_inc(s.raw0_in, 16)
            for two in range(ROUNDS // 2):
                sp.wait_ge(a_added, 4 * (two + 1))
                sp.dma_start(s.messages[:, P * two:P * two + P].rearrange("(t p) h -> p t h", p=P),
                             result[:, two % 2]).then_inc(s.messages_stored[two], 16)

        @block.gpsimd
        def _(pool):
            nc.gpsimd.memset(zeros, 0.0).then_inc(zeroed, 1)
            nc.gpsimd.memset(ones, 1.0).then_inc(zeroed, 1)
            for t in range(NT):
                pool.wait_ge(xn_ready, t + 1)
                nc.gpsimd.tensor_copy(XP[:, t % 2, :, t // 2], X[:, t]).then_inc(batched, 1)
            pool.wait_ge(blank, 16)
            pool.wait_ge(slots_ready, 1)
            for t in range(NT):
                for k in range(2):
                    nc.gpsimd.indirect_dma_start(
                        out=xs, out_offset=bass.IndirectOffsetOnAxis(ap=s.slots[:, t, k:k + 1], axis=0),
                        in_=X[:, t], in_offset=None).then_inc(sorted_, 16)
            pool.wait_ge(sorted_, 16 * 2 * NT)

        @block.scalar
        def _(act):
            sc = nc.scalar

            def logits_leave(c):
                act.wait_ge(logit, c + 1)
                sc.activation(LT[0:E, 512 * c:512 * c + 512], psum(2 + c % 2)[0:E], ACT.Copy).then_inc(logit_out, 1)

            act.wait_ge(var_ready, 1)
            sc.activation(root, mv[:, :, 1], ACT.Sqrt).then_inc(std_ready, 1)
            for t in range(NT):
                act.wait_ge(turned, t + 1)
                if t % 4 == 0 and t >= 8:
                    act.wait_ge(logit, t // 4 - 1)
                sc.activation(XT[:, t // 4 % 2, :, P * (t % 4):P * (t % 4) + P], psum(t % 2).rearrange("p (k n) -> p k n", k=4),
                              ACT.Copy).then_inc(turned_out, 1)
                if t % 4 == 2 and t > 4:
                    logits_leave(t // 4 - 1)
            logits_leave(3)
            act.wait_ge(p_ex, 1)
            sc.activation(p, p, ACT.Exp).then_inc(p_exd, 1)

            def bring_x(r):
                act.wait_ge(a_xt, 2 * r + 1)
                if r >= 3:
                    act.wait_ge(a_msg, 2 * (r - 2))
                sc.activation(xg[:, r % 3, 0], psum(4).rearrange("p (g c) -> p g c", g=4), ACT.Copy).then_inc(a_xt_a, 1)

            def bring_p(r):
                act.wait_ge(a_pt, r + 1)
                sc.activation(pt[:, r % 2], psum(6).rearrange("p (g c) -> p g c", g=4), ACT.Copy).then_inc(a_pt_out, 1)

            for r in range(ROUNDS + 2):
                if r >= 2:
                    bring_p(r - 2)
                if r < ROUNDS:
                    act.wait_ge(a_bias, r + 1)
                    for g in range(4):
                        last = sc.activation(pr[:, r % 3, g], psum(2 + r % 2)[:, P * g:P * g + P], ACT.Exp,
                                             bias=nb[:, r % 2, g:g + 1], scale=INV, accum_out=sm[:, r % 2, g:g + 1])
                    last.then_inc(a_exp, 1)
                    bring_x(r)

        @block.vector
        def _(dve):
            v = nc.vector
            step = Chain(dve, dv)
            by_entry = result.rearrange("p r (b k) c -> p r b k c", k=2)
            v.tensor_scalar(mv[:, :, 1], mv[:, :, 1], LN_EPS, None, ALU.add).then_inc(var_ready, 1)
            dve.wait_ge(std_ready, 1)
            rsqrt_refined(v, step, rs, root, mv[:, :, 1])
            dve.wait_ge(s.x1_stored, 16 * NT)
            for t in range(NT):
                v.tensor_scalar(X[:, t], X[:, t], mv[:, t, 0:1], rs[:, t:t + 1], ALU.subtract,
                                ALU.mult).then_inc(xn_ready, 1)
            dve.wait_ge(consts2_in, 16)
            v.tensor_copy(s.maskb[:, :], const("same_l")).then_inc(mask_ready, 1)
            dve.wait_ge(lt, 1)
            step.then(v.tensor_copy(p, psum(7)[:, 0:P].rearrange("p (t e) -> p t e", t=NT)))
            step.then(v.tensor_reduce(top, p, AX.X, ALU.max))
            v.tensor_tensor(p, p, top.unsqueeze(2).broadcast_to([P, NT, E]), ALU.subtract).then_inc(p_ex, 1)
            dve.wait_ge(p_exd, 1)
            step.then(v.tensor_reduce(sums, p, AX.X, ALU.add))
            step.then(v.reciprocal(sums, sums))
            step.then(v.tensor_tensor(p, p, sums.unsqueeze(2).broadcast_to([P, NT, E]), ALU.mult))
            other = p.unsqueeze(2).broadcast_to([P, NT, E, E])
            this = p.unsqueeze(3).broadcast_to([P, NT, E, E])
            earlier = const("earlier_e", "p (e f) -> p e f", e=E).unsqueeze(1).broadcast_to([P, NT, E, E])
            step(v.tensor_tensor(big1, other, this, ALU.is_gt))
            step.then(v.tensor_tensor(big2, other, this, ALU.is_equal))
            step.then(v.tensor_tensor(big2, big2, earlier, ALU.mult))
            step.then(v.tensor_tensor(big1, big1, big2, ALU.add))
            step.then(v.tensor_reduce(rank, big1, AX.X, ALU.add))
            v.tensor_scalar(chosen, rank, 2.0, None, ALU.is_lt).then_inc(chosen_ready, 1)
            step(v.tensor_scalar(first, rank, 0.0, None, ALU.is_equal))
            step.then(v.tensor_scalar(second, rank, 1.0, None, ALU.is_equal))
            small1, small2 = big1[:, :, 0], big2[:, :, 0]
            step(v.tensor_tensor(small1, first, p, ALU.mult))
            step.then(v.tensor_tensor(small2, second, p, ALU.mult))
            step(v.tensor_reduce(vals[:, :, 0], small1, AX.X, ALU.add))
            step.then(v.tensor_reduce(vals[:, :, 1], small2, AX.X, ALU.add))
            step.then(v.tensor_tensor(sums, vals[:, :, 0], vals[:, :, 1], ALU.add))
            step.then(v.reciprocal(sums, sums))
            step.then(v.tensor_tensor(s.gatew, vals, sums.unsqueeze(2).broadcast_to([P, NT, 2]), ALU.mult))
            dve.wait_ge(counted, 1)
            step(v.tensor_copy(within, psum(7)[:, 128:256].rearrange("p (t e) -> p t e", t=NT)))
            step.then(v.memset(cum[:, 0], 0.0))
            for t in range(NT):
                step.then(v.tensor_tensor(cum[:, t + 1], cum[:, t], psum(7)[:, 256 + E * t:256 + E * t + E], ALU.add))
            step.then(v.tensor_tensor(over, cum[:, NT].unsqueeze(2).broadcast_to([P, E, 16]),
                                      const("tile_starts").unsqueeze(1).broadcast_to([P, E, 16]), ALU.is_gt))
            step(v.tensor_reduce(n_blocks, over, AX.X, ALU.add))
            step.then(v.memset(starts[:, 0:1], 0.0))
            for e in range(E):
                step.then(v.tensor_tensor(starts[:, e + 1:e + 2], starts[:, e:e + 1], n_blocks[:, e:e + 1], ALU.add))
            step(v.tensor_tensor(within, within, cum[:, 0:NT], ALU.add))
            step.then(v.tensor_scalar(n_blocks, starts[:, 0:E], float(P), None, ALU.mult))
            step.then(v.tensor_tensor(within, within, n_blocks.unsqueeze(1).broadcast_to([P, NT, E]), ALU.add))
            step(v.tensor_tensor(small1, first, within, ALU.mult))
            step.then(v.tensor_tensor(small2, second, within, ALU.mult))
            step(v.tensor_reduce(slotf[:, :, 0], small1, AX.X, ALU.add))
            step.then(v.tensor_reduce(slotf[:, :, 1], small2, AX.X, ALU.add))
            v.tensor_copy(s.slots, slotf).then_inc(slots_ready, 1)
            step(v.tensor_scalar(s.ends, starts[:, 1:E + 1], 1.0, None, ALU.add))
            step.then(v.tensor_tensor(which, const("block_ids").unsqueeze(2).broadcast_to([P, NBLK, E - 1]),
                                      starts[:, 1:E].unsqueeze(1).broadcast_to([P, NBLK, E - 1]), ALU.is_ge))
            step.then(v.tensor_reduce(of_block, which, AX.X, ALU.add))
            step(v.tensor_scalar(s.ready_at, of_block, float(len(CHUNKS)), 1.0, ALU.mult, ALU.add))
            step.then(v.tensor_scalar(odd, of_block, 1.0, None, ALU.is_equal))
            for k in (3.0, 5.0, 7.0):
                step.then(v.scalar_tensor_tensor(out=odd, in0=of_block, scalar=k, in1=odd, op0=ALU.is_equal,
                                                 op1=ALU.add))
            step(v.tensor_scalar(s.slot_at, odd, 2.0 * SLOT, None, ALU.mult))

            for r in range(ROUNDS + 3):
                if r >= 3:
                    of = r - 3
                    if of % 2 == 0 and of >= 4:
                        dve.wait_ge(s.messages_stored[of // 2 - 2], 16)
                    for k in range(2):
                        dve.wait_ge(a_msg, 2 * of + k + 1)
                        own = XP[:, k, 64 * of:64 * of + 64]
                        to = by_entry[:, of // 2 % 2, :, k, 64 * (of % 2):64 * (of % 2) + 64]
                        v.tensor_tensor(to.rearrange("p b c -> p c b"), psum(k).rearrange("p (c b) -> p c b", b=NB),
                                        own, ALU.add).then_inc(a_added, 1)
                if r < ROUNDS:
                    dve.wait_ge(a_scored, r + 1)
                    v.tensor_reduce(mx[:, r % 2], psum(2 + r % 2).rearrange("p (g k) -> p g k", g=4), AX.X,
                                    ALU.max).then_inc(a_maxed, 1)
                    dve.wait_ge(a_maxed, r + 1)
                    v.tensor_scalar(nb[:, r % 2], mx[:, r % 2], -INV, None, ALU.mult).then_inc(a_bias, 1)
                    dve.wait_ge(a_xt, 2 * r + 2)
                    if r >= 3:
                        dve.wait_ge(a_msg, 2 * (r - 2))
                    v.tensor_copy(xg[:, r % 3, 1], psum(5).rearrange("p (g c) -> p g c", g=4)).then_inc(a_xt_v, 1)
                    dve.wait_ge(a_exp, r + 1)
                    v.reciprocal(rc[:, r % 2], sm[:, r % 2]).then_inc(a_recip, 1)
                    dve.wait_ge(a_recip, r + 1)
                    v.tensor_tensor(pr[:, r % 3], pr[:, r % 3], rc[:, r % 2].unsqueeze(2).broadcast_to([P, 4, P]),
                                    ALU.mult).then_inc(a_norm, 1)

        @block.tensor
        def _(pe):
            mm, tr = nc.tensor.matmul, nc.tensor.transpose

            def route(c):
                if c == 0:
                    pe.wait_ge(g1_in, 16)
                pe.wait_ge(turned_out, 4 * c + 4)
                if c >= 2:
                    pe.wait_ge(logit_out, c - 1)
                for k in range(4):
                    last = mm(psum(2 + c % 2)[0:E], g1[:, k], XT[:, c % 2, k], start=(k == 0), stop=(k == 3))
                last.then_inc(logit, 1)

            for t in range(NT):
                pe.wait_ge(xn_ready, t + 1)
                if t >= 2:
                    pe.wait_ge(turned_out, t - 1)
                for k in range(4):
                    last = tr(psum(t % 2)[:, P * k:P * k + P], X[:, t, P * k:P * k + P], ident)
                last.then_inc(turned, 1)
                if t % 4 == 1 and t > 4:
                    route(t // 4 - 1)
            route(3)
            for t in range(NT):
                pe.wait_ge(logit_out, t // 4 + 1)
                last = tr(psum(7)[:, E * t:E * t + E], LT[0:E, P * t:P * t + P], ident[0:E, 0:E])
            last.then_inc(lt, 1)

            def count():
                pe.wait_ge(chosen_ready, 1)
                pe.wait_ge(zeroed, 2)
                mm(psum(7)[:, 128:256], const("before"), chosen.rearrange("p t e -> p (t e)"), start=True, stop=True)
                mm(psum(7)[:, 256:384], ones, chosen.rearrange("p t e -> p (t e)"), start=True,
                   stop=True).then_inc(counted, 1)

            def score(r):
                if r >= 2:
                    pe.wait_ge(a_exp, r - 1)
                for g in range(4):
                    ps = psum(2 + r % 2)[:, P * g:P * g + P]
                    for k in range(2):
                        xk = by_group[:, k, 4 * r + g]
                        mm(ps, xk, xk, start=(k == 0), stop=False)
                    last = mm(ps, s.identb[:, :], s.maskb[:, :], start=False, stop=True)
                last.then_inc(a_scored, 1)

            def turn_x(r):
                for k in range(2):
                    if r:
                        pe.wait_ge(a_xt_v if k else a_xt_a, r)
                    for g in range(4):
                        last = tr(psum(4 + k)[:, P * g:P * g + P], by_group[:, k, 4 * r + g], ident)
                    last.then_inc(a_xt, 1)

            def turn_p(r):
                pe.wait_ge(a_norm, r + 1)
                if r:
                    pe.wait_ge(a_pt_out, r)
                for g in range(4):
                    last = tr(psum(6)[:, P * g:P * g + P], pr[:, r % 3, g], ident)
                last.then_inc(a_pt, 1)

            def message(r):
                pe.wait_ge(a_pt_out, r + 1)
                pe.wait_ge(a_xt_a, r + 1)
                pe.wait_ge(a_xt_v, r + 1)
                for k in range(2):
                    if r:
                        pe.wait_ge(a_added, 2 * (r - 1) + k + 1)
                    for g in range(4):
                        last = mm(psum(k)[:, P * g:P * g + P], xg[:, r % 3, k, g], pt[:, r % 2, g], start=True,
                                  stop=True)
                    last.then_inc(a_msg, 1)

            pe.wait_ge(mask_ready, 1)
            pe.wait_ge(batched, NT)
            score(0)
            turn_x(0)
            score(1)
            count()
            turn_x(1)
            for r in range(2, ROUNDS + 2):
                if r < ROUNDS:
                    score(r)
                turn_p(r - 2)
                if r < ROUNDS:
                    turn_x(r)
                message(r - 2)


def experts(s):
    nc, sem, psum, ident = s.nc, s.sem, s.psum, s.ident
    W, xgT, actT = s.W, s.xgT, s.actT
    xg = s.carve(2, D)
    act_ = s.carve(2, FF)
    y = s.carve(2, D)
    stage = s.carve(2, CHUNK)
    HF = FF // 2
    xs, ys = s.xs, s.ys
    (raw_in0, raw_in1, x_in0, x_in1, x_turned, x_high, x_low, h_done, silu_out, act_ready, a_turned,
     a_high, a_high_v, a_low, y_done, y_out, y_in0, y_in1) = (sem(n) for n in (
         "raw_in0", "raw_in1", "xrows_in0", "xrows_in1", "rows_turned", "rows_high", "rows_low", "h_done",
         "silu_out", "act_ready", "act_turned", "act_high", "act_high_v", "act_low", "y_done", "y_out", "y_stored0",
         "y_stored1"))
    raw_in, x_in, y_in = (raw_in0, raw_in1), (x_in0, x_in1), (y_in0, y_in1)
    first_high, first_low, first_w2 = (sem(n) for n in ("first_high", "first_low", "first_w2"))
    high_in = [sem(f"high_in{i}") for i in range(2)]
    NCH = len(CHUNKS)


    with nc.Block() as block:
        @block.gpsimd
        def _(pool):
            g = nc.gpsimd
            pool.sem_inc(s.converted, 1)
            pool.wait_ge(s.raw0_in, 16 * NCH)
            for c in range(KT_PER_D, NCH):
                at, rows, n = CHUNKS[c]
                high, low = parts_of(s, c, 0)
                raw = s.raw0[0:rows, at:at + n]
                pool.wait_ge(first_high, c + 1)
                g.tensor_tensor(low, raw, high, ALU.subtract).then_inc(first_w2, 1)

            def bring_raw(j):
                if j >= 2:
                    pool.wait_ge(s.converted, 1 + j - 1)
                bring_chunk(pool, s, 1 + j // NCH, j % NCH, stage[:, j % 2]).then_inc(raw_in[j % 2], 16)

            def bring_high(j):
                e, c = 1 + j // NCH, j % NCH
                at, rows, n = CHUNKS[c]
                if c == 0 and e >= 2:
                    end = pool.value_load(s.ends[0:1, e - 2:e - 1], min_val=1, max_val=NBLK + 1)
                    pool.wait_ge(y_done, end)
                    pool.nop(nofuse=True)
                at0 = e % 2 * 2 * SLOT + at
                bring_chunk(pool, s, e, c, W[:, at0:at0 + n]).then_inc(high_in[j % 2], 16)

            bring_raw(0)
            pool.wait_ge(first_low, KT_PER_D)
            pool.wait_ge(first_w2, NCH - KT_PER_D)
            for stored in s.messages_stored:
                pool.wait_ge(stored, 16)
            bring_high(0)
            for j in range((E - 1) * NCH):
                e, c = 1 + j // NCH, j % NCH
                more = j + 1 < (E - 1) * NCH
                if more:
                    bring_raw(j + 1)
                if more and c + 1 < NCH:
                    bring_high(j + 1)
                pool.wait_ge(raw_in[j % 2], 16 * (j // 2 + 1))
                pool.wait_ge(high_in[j % 2], 16 * (j // 2 + 1))
                high, low = parts_of(s, c, e % 2 * 2 * SLOT)
                at, rows, n = CHUNKS[c]
                g.tensor_tensor(low, stage[0:rows, j % 2, 0:n], high, ALU.subtract).then_inc(s.converted, 1)
                if more and c + 1 == NCH:
                    bring_high(j + 1)
            end = pool.value_load(s.ends[0:1, E - 2:E - 1], min_val=1, max_val=NBLK + 1)
            pool.wait_ge(y_done, end)
            pool.nop(nofuse=True)
            for q in range(NT // 2):
                pool.wait_ge(y_done, NBLK - NT // 2 + q)
                for i, rows in enumerate((s.x1, s.messages)):
                    pool.dma_start(s.kept[:, i, 2 * q:2 * q + 2],
                                   rows[2 * P * q:2 * P * q + 2 * P, :].rearrange("(t p) n -> p t n", p=P)).then_inc(
                                       s.kept_in, 16)

        @block.sync
        def _(sp):
            def load(b, par):
                sp.dma_start(xg[:, par], xs[ds(b * P, P), :]).then_inc(x_in[par], 16)

            load(0, 0)
            load(1, 1)
            sp.wait_ge(x_turned, 1)
            load(2, 0)
            with sp.Fori(0, (NBLK - 3) // 2) as i:
                for par in (1, 0):
                    b = i * 2 + (1 if par else 2)
                    sp.wait_ge(x_turned, b + 1)
                    load(b + 2, par)
            sp.wait_ge(y_in0, 16 * (NBLK // 2 + 1))
            sp.wait_ge(y_in1, 16 * (NBLK // 2))

        @block.scalar
        def _(act):
            sc = nc.scalar

            def rows(b, par):
                act.wait_ge(x_turned, b + 1)
                sc.activation(xgT[:, par, HIGH], psum(4), ACT.Copy).then_inc(x_high, 1)

            def silu(b, par, hf):
                act.wait_ge(h_done, b * 2 + hf + 1)
                sc.activation(act_[:, par, HF * hf:HF * hf + HF], psum(2 * hf)[:, 0:HF], ACT.Silu).then_inc(silu_out, 1)

            def turned(b):
                act.wait_ge(a_turned, b)
                sc.activation(actT[:, HIGH, 0:4 * P], psum(5), ACT.Copy).then_inc(a_high, 1)

            def result(b, par, early):
                act.wait_ge(y_done, b + 1)
                if not early:
                    act.wait_ge(y_in[1 - par], b * 8 - 8 if par == 1 else b * 8 - 16)
                sc.activation(y[:, 1 - par], psum(7), ACT.Copy).then_inc(y_out, 1)
                act.wait_ge(y_out, b)
                act.dma_start(ys[ds((b - 1) * P, P), :], y[:, 1 - par]).then_inc(y_in[1 - par], 16)

            def step(b, par, first=False, last=False, early=False):
                silu(b, par, 0)
                if not last:
                    rows(b + 1, 1 - par)
                if not first:
                    turned(b)
                silu(b, par, 1)
                if not first:
                    result(b, par, early)

            act.wait_ge(s.raw0_in, 16 * NCH)
            for c, (at, n_rows, n) in enumerate(CHUNKS):
                if c == KT_PER_D:
                    rows(0, 0)
                sc.activation(parts_of(s, c, 0)[HIGH], s.raw0[0:n_rows, at:at + n], ACT.Copy).then_inc(first_high, 1)
            step(0, 0, first=True)
            step(1, 1, early=True)
            step(2, 0, early=True)
            with act.Fori(1, (NBLK - 3) // 2) as i:
                step(i * 2 + 1, 1)
                step(i * 2 + 2, 0)
            step(NBLK - 2, 1)
            step(NBLK - 1, 0, last=True)
            turned(NBLK)
            result(NBLK, 1, False)

        @block.vector
        def _(dve):
            v = nc.vector

            def rows(b, par):
                dve.wait_ge(x_high, b + 1)
                v.tensor_tensor(xgT[:, par, LOW], psum(4), xgT[:, par, HIGH], ALU.subtract).then_inc(x_low, 1)

            def multiply(b, par, hf):
                dve.wait_ge(silu_out, b * 2 + hf + 1)
                half = act_[:, par, HF * hf:HF * hf + HF]
                v.tensor_tensor(half, half, psum(2 * hf + 1)[:, 0:HF], ALU.mult).then_inc(act_ready, 1)

            def turned(b):
                dve.wait_ge(a_turned, b)
                v.tensor_copy(actT[:, HIGH, 4 * P:6 * P], psum(6)[:, 0:2 * P]).then_inc(a_high_v, 1)
                v.tensor_copy(actT[0:FR, HIGH, 6 * P:7 * P], psum(6)[0:FR, 2 * P:3 * P]).then_inc(a_high_v, 1)
                dve.wait_ge(a_high, b)
                v.tensor_tensor(actT[:, LOW, 0:4 * P], psum(5), actT[:, HIGH, 0:4 * P], ALU.subtract).then_inc(a_low, 1)
                dve.wait_ge(a_high_v, b * 2)
                v.tensor_tensor(actT[:, LOW, 4 * P:6 * P], psum(6)[:, 0:2 * P], actT[:, HIGH, 4 * P:6 * P],
                                ALU.subtract).then_inc(a_low, 1)
                v.tensor_tensor(actT[0:FR, LOW, 6 * P:7 * P], psum(6)[0:FR, 2 * P:3 * P],
                                actT[0:FR, HIGH, 6 * P:7 * P], ALU.subtract).then_inc(a_low, 1)

            def step(b, par, last=False):
                multiply(b, par, 0)
                if not last:
                    rows(b + 1, 1 - par)
                turned(b)
                multiply(b, par, 1)

            dve.wait_ge(s.raw0_in, 16 * NCH)
            for c in range(KT_PER_D):
                at, _, n = CHUNKS[c]
                high, low = parts_of(s, c, 0)
                dve.wait_ge(first_high, c + 1)
                v.tensor_tensor(low, s.raw0[:, at:at + n], high, ALU.subtract).then_inc(first_low, 1)
            rows(0, 0)
            multiply(0, 0, 0)
            rows(1, 1)
            multiply(0, 0, 1)
            with dve.Fori(0, (NBLK - 3) // 2) as i:
                step(i * 2 + 1, 1)
                step(i * 2 + 2, 0)
            step(NBLK - 2, 1)
            step(NBLK - 1, 0, last=True)
            turned(NBLK)

        @block.tensor
        def _(pe):
            mm, tr = nc.tensor.matmul, nc.tensor.transpose

            def turn_rows(b, par):
                pe.wait_ge(x_in[par], b * 8 + 16 if par == 0 else b * 8 + 8)
                if not (isinstance(b, int) and b == 0):
                    pe.wait_ge(x_low, b)
                for k in range(4):
                    last = tr(psum(4)[:, P * k:P * k + P], xg[:, par, P * k:P * k + P], ident)
                last.then_inc(x_turned, 1)

            def up(b, par, off, hf):
                pe.wait_ge(x_high, b + 1)
                pe.wait_ge(x_low, b + 1)
                if not (isinstance(b, int) and b == 0):
                    pe.wait_ge(act_ready, b * 2 - 1 + hf)
                for w in range(2):
                    for i, (of_x, of_w) in enumerate(PASSES):
                        for k in range(4):
                            last = mm(psum(2 * hf + w)[:, 0:HF], xgT[:, par, of_x, P * k:P * k + P],
                                      W[:, ds(off + (of_w * SLOT + (k * 2 + w) * FF + hf * HF), HF)],
                                      start=(i == 0 and k == 0), stop=(i == 2 and k == 3))
                last.then_inc(h_done, 1)

            def turn_act(b, par):
                pe.wait_ge(act_ready, b * 2 + 2)
                for t in range(FT + 1):
                    n = P if t < FT else FR
                    ps = psum(5)[:, P * t:P * t + P] if t < 4 else psum(6)[0:n, P * (t - 4):P * (t - 4) + P]
                    last = tr(ps, act_[:, par, P * t:P * t + n], ident)
                last.then_inc(a_turned, 1)

            def down(b, off):
                pe.wait_ge(a_high, b + 1)
                pe.wait_ge(a_high_v, b * 2 + 2)
                if not (isinstance(b, int) and b == 0):
                    pe.wait_ge(y_out, b)
                for i, (of_a, of_w) in enumerate(PASSES):
                    if of_a == LOW:
                        pe.wait_ge(a_low, b * 3 + 3)
                    for t in range(FT + 1):
                        n = P if t < FT else FR
                        last = mm(psum(7), actT[0:n, of_a, P * t:P * t + P],
                                  W[0:n, ds(off + (of_w * SLOT + W13 + t * D), D)],
                                  start=(i == 0 and t == 0), stop=(i == 2 and t == FT))
                last.then_inc(y_done, 1)

            def place(b):
                return pe.value_load(s.slot_at[0:1, ds(b, 1)], min_val=0, max_val=2 * SLOT)

            def weights(b):
                off = place(b)
                pe.wait_ge(s.converted, pe.value_load(s.ready_at[0:1, ds(b, 1)], min_val=1, max_val=NCH * E))
                return off

            turn_rows(0, 0)
            off = weights(0)
            pe.wait_ge(first_low, KT_PER_D)
            up(0, 0, off, 0)
            turn_rows(1, 1)
            up(0, 0, off, 1)
            pe.wait_ge(first_w2, NCH - KT_PER_D)
            pe.sem_inc(y_done, 1)

            def step(b, par, last=False):
                off = weights(b)
                up(b, par, off, 0)
                if not last:
                    turn_rows(b + 1, 1 - par)
                turn_act(b - 1, 1 - par)
                up(b, par, off, 1)
                before = place(b - 1)
                down(b - 1, before)

            with pe.Fori(0, (NBLK - 3) // 2) as i:
                step(i * 2 + 1, 1)
                step(i * 2 + 2, 0)
            step(NBLK - 2, 1)
            step(NBLK - 1, 0, last=True)
            turn_act(NBLK - 1, 0)
            down(NBLK - 1, place(NBLK - 1))


def combine(s):
    nc, sem, X, S = s.nc, s.sem, s.kept[:, 0], s.kept[:, 1]
    DEEP = 8
    yy = s.carve(DEEP, 2, D)
    z = s.carve(2, D)
    got = [sem(f"rows_got{i}") for i in range(DEEP)]
    dv, mixed, gated, done, stored = (sem(n) for n in ("c_dve", "mixed", "c_gated", "c_done", "stored"))

    with nc.Block() as block:
        @block.gpsimd
        def _(pool):
            for t in range(NT):
                if t >= DEEP:
                    pool.wait_ge(mixed, t - DEEP + 1)
                for k in range(2):
                    nc.gpsimd.indirect_dma_start(
                        out=yy[:, t % DEEP, k], out_offset=None, in_=s.ys,
                        in_offset=bass.IndirectOffsetOnAxis(ap=s.slots[:, t, k:k + 1], axis=0)).then_inc(
                            got[t % DEEP], 16)

        @block.vector
        def _(dve):
            v = nc.vector
            step = Chain(dve, dv)

            def finish(t):
                dve.wait_ge(gated, t + 1)
                if t == 0:
                    dve.wait_ge(s.kept_in, 16 * NT)
                step.then(v.tensor_tensor(z[:, t % 2], z[:, t % 2], S[:, t], ALU.mult))
                v.tensor_tensor(X[:, t], X[:, t], z[:, t % 2], ALU.add).then_inc(done, 1)

            for t in range(NT):
                dve.wait_ge(got[t % DEEP], 32 * (t // DEEP + 1))
                if t >= 2:
                    dve.wait_ge(done, t - 1)
                step.then(v.tensor_scalar(z[:, t % 2], yy[:, t % DEEP, 0], s.gatew[:, t, 0:1], None, ALU.mult))
                v.scalar_tensor_tensor(out=z[:, t % 2], in0=yy[:, t % DEEP, 1], scalar=s.gatew[:, t, 1:2],
                                       in1=z[:, t % 2], op0=ALU.mult, op1=ALU.add).then_inc(mixed, 1)
                if t:
                    finish(t - 1)
            finish(NT - 1)

        @block.scalar
        def _(act):
            for t in range(NT):
                act.wait_ge(mixed, t + 1)
                nc.scalar.activation(z[:, t % 2], z[:, t % 2], ACT.Silu).then_inc(gated, 1)

        @block.sync
        def _(sp):
            for t in range(NT):
                sp.wait_ge(done, t + 1)
                sp.dma_start(s.out[P * t:P * t + P, :], X[:, t]).then_inc(stored, 16)
            sp.wait_ge(stored, 16 * NT)


ROPE_ORDER = np.concatenate([np.arange(0, ROPE, 2), np.arange(1, ROPE, 2)])


def lay_out(i):
    f = lambda n: np.asarray(i[n])
    wqb = f("L0_attn_wq_b").reshape(H, NOPE + ROPE, QR)
    wkb = f("L0_attn_wkv_b").reshape(H, NOPE + VD, KVR)
    wkva = f("L0_attn_wkv_a")
    wkva = np.concatenate([wkva[KVR:][ROPE_ORDER], wkva[:KVR]], 0)

    def by_k(wt):
        return wt.reshape(KT_PER_D, P, -1).transpose(1, 0, 2)

    r = {
        "consts": shape_constants(),
        "x": f("L0_attn_x").reshape(NB * SEQ, D),
        "vecs": np.concatenate([f("L0_ffn_b"), f("L0_attn_q_a_ln_w"), f("L0_attn_kv_a_ln_w"), f("L0_ffn_router_b")])[None],
        "wqkv": by_k(np.concatenate([f("L0_attn_wq_a"), wkva], 0).T),
        "wq_rope": wqb[:, NOPE:][:, ROPE_ORDER].transpose(2, 0, 1),
        "wq_nope": wqb[:, :NOPE].transpose(1, 0, 2),
        "wkv_k": wkb[:, :NOPE].transpose(1, 0, 2),
        "wkv_v": wkb[:, NOPE:].transpose(1, 0, 2),
        "wo": f("L0_attn_wo").T.reshape(H, VD, D).transpose(1, 0, 2),
        "gate_w": by_k(f("L0_ffn_W").T),
        "lora_a": by_k(f("L0_ffn_A").reshape(NE * RANK, D).T),
        "lora_b": f("L0_ffn_B").transpose(0, 2, 1).reshape(NE * RANK, D),
        "router": by_k(f("L0_ffn_router_W").T),
        "gate1": by_k(f("L1_ffn_gate_w").T),
        "w13": np.stack([f("L1_ffn_w1"), f("L1_ffn_w3")], 1).reshape(E, 2, FF, KT_PER_D, P).transpose(0, 4, 3, 1, 2)
                 .reshape(E, P, KT_PER_D * 2 * FF),
        "w2": f("L1_ffn_w2").transpose(0, 2, 1),
    }
    return {k: np.ascontiguousarray(v) for k, v in r.items()}


def kernel(**inputs):
    import concourse.bacc as bacc
    from concourse.bass_utils import run_bass_kernel_spmd

    nc = bacc.Bacc("TRN2", target_bir_lowering=False, num_devices=1)
    arrays = lay_out(inputs)
    aps = {k: nc.dram_tensor(k, v.shape, mybir.dt.from_np(v.dtype), kind="ExternalInput").ap()
           for k, v in arrays.items()}
    out = nc.dram_tensor("out", (NB * SEQ, D), F32, kind="ExternalOutput").ap()
    build(nc, aps, out)
    r = run_bass_kernel_spmd(nc, [arrays], core_ids=[0])
    return r.results[0]["out"].reshape(NB, SEQ, D)
```

```python
import math
from contextlib import ExitStack

import numpy as np

import concourse.bass as bass
from concourse import mybir

F32 = mybir.dt.float32
F32R = mybir.dt.float32r
BF16 = mybir.dt.bfloat16
I32 = mybir.dt.int32
ALU = mybir.AluOpType
ACT = mybir.ActivationFunctionType
AX = mybir.AxisListType
ds = bass.ds

P = 128
NB, SEQ, D = 8, 256, 512
NT = NB * SEQ // P
KT_PER_D = D // P
H, NOPE, ROPE, VD, KVR, QR = 32, 64, 64, 128, 32, 128
KC = ROPE + KVR
QKW = QR + KC
NE, RANK = 8, 16
E, FF = 8, 800
FT = FF // P
FR = FF - FT * P
MSCALE = 0.1 * math.log(128.0) + 1.0
SCALE = (NOPE + ROPE) ** -0.5 * MSCALE * MSCALE
LORA_SCALE = 2.0
MEAN_FROM, MEAN_TO = 107, 255
LN_EPS, RMS_EPS = 1e-5, 1e-6
BIG = -1.0e30
HIGH, LOW = 0, 1
PASSES = ((HIGH, HIGH), (HIGH, LOW), (LOW, HIGH))
NBLK = 2 * NB * SEQ // P + E - 1

CONSTS = {}
_at = 0
for _name, _n in (("ident", P), ("causal", P), ("cos", 2 * KC), ("sin", 2 * ROPE), ("mean", 2 * 15),
                  ("same_l", P), ("before", P), ("earlier_e", E * E), ("tile_starts", 16), ("block_ids", NBLK)):
    CONSTS[_name] = (_at, _n)
    _at += _n
NCONST = _at
LAYER1_AT, LAYER2_AT = CONSTS["causal"][0], CONSTS["same_l"][0]

W13 = KT_PER_D * 2 * FF
SLOT = W13 + (FT + 1) * D
CHUNK = 2 * FF
CHUNKS = ([(k * 2 * FF, P, 2 * FF) for k in range(KT_PER_D)] +
          [(W13 + t * D, P, FT // 2 * D) for t in (0, FT // 2)] + [(W13 + FT * D, 3 * FR, D)])
REST_LOW = slice(0, FR)
REST_ALOW = slice(2 * FR, 3 * FR)


def shape_constants():
    c = np.zeros((P, NCONST), np.float32)

    def put(name, a):
        at, n = CONSTS[name]
        c[:, at:at + n] = np.asarray(a, np.float32).reshape(P, n)

    p = np.arange(P)
    put("ident", np.eye(P))
    put("causal", np.where(p[None, :] <= p[:, None], 0.0, BIG))
    put("same_l", np.where(p[None, :] // NB == p[:, None] // NB, 0.0, BIG))
    put("before", p[:, None] < p[None, :])
    low = max(math.floor(ROPE * math.log(1024 / (32.0 * 2 * math.pi)) / (2 * math.log(10000.0))), 0)
    high = min(math.ceil(ROPE * math.log(1024 / (2 * math.pi)) / (2 * math.log(10000.0))), ROPE - 1)
    hi = high + 0.001 if low == high else float(high)
    keep = 1.0 - np.clip((np.arange(ROPE // 2, dtype=np.float32) - low) / (hi - low), 0.0, 1.0)
    extra = 1.0 / 10000.0 ** (np.arange(0, ROPE, 2, dtype=np.float32) / ROPE)
    freq = extra / 128.0 * (1.0 - keep) + extra * keep
    angle = np.outer(np.arange(SEQ, dtype=np.float32), freq)
    cos, sin = np.cos(angle), np.sin(angle)
    one = np.ones((SEQ, KVR))
    put("cos", np.concatenate([cos, cos, one], 1).reshape(2, P, KC).transpose(1, 0, 2))
    put("sin", np.concatenate([-sin, sin], 1).reshape(2, P, ROPE).transpose(1, 0, 2))
    mean = np.zeros((P, 2, 15))
    tok = p[:, None] + P * np.arange(2)[None, :]
    mean[:, :, 7] = ((tok >= MEAN_FROM) & (tok < MEAN_TO)) / (MEAN_TO - MEAN_FROM)
    put("mean", mean)
    e = np.arange(E)
    put("earlier_e", np.tile((e[None, :] < e[:, None]).reshape(1, -1), (P, 1)))
    put("tile_starts", np.tile([-1] + [P * k for k in range(1, 16)], (P, 1)))
    put("block_ids", np.tile(np.arange(NBLK), (P, 1)))
    return c


class Chain:

    def __init__(self, eng, sem, base=0):
        self.eng, self.sem, self.base, self.n = eng, sem, base, 0

    def __call__(self, ins):
        ins.then_inc(self.sem, 1)
        self.n += 1

    def wait(self):
        self.eng.wait_ge(self.sem, self.base + self.n)

    def then(self, ins):
        self(ins)
        self.wait()


def build(nc, a, out):
    with ExitStack() as ctx:
        s = Stages(nc, ctx, a, out)

        def sb(scope, name, shape, dt=F32):
            return scope.enter_context(nc.sbuf_tensor(name, shape, dt))

        s.ident = sb(ctx, "ident_sb", [P, P])[:, :]
        s.identb = sb(ctx, "identb", [P, P], BF16)
        s.maskb = sb(ctx, "maskb", [P, P], BF16)
        tables = sb(ctx, "tables", [P, 6 * NT + 2 * NBLK + E])
        s.X = sb(ctx, "x_keep", [P, NT, D])
        s.room(tables)
        s.mv = s.carve(NT, 2)
        s.slots = s.carve(NT, 2, dt=I32)
        s.gatew = s.carve(NT, 2)
        s.ready_at = s.carve(NBLK, dt=I32)
        s.slot_at = s.carve(NBLK, dt=I32)
        s.ends = s.carve(E, dt=I32)
        s.bank = [ctx.enter_context(nc.psum_tensor(f"bank{i}", [P, 1024], F32)) for i in range(4)]
        s.x1 = nc.dram_tensor("x_after_layer1", [NB * SEQ, D], F32, kind="Internal").ap()
        s.gates = nc.dram_tensor("gates", [NB * SEQ, D], F32, kind="Internal").ap()
        s.gates_stored = s.sem("gates_stored")
        s.messages = nc.dram_tensor("layer2_attention", [NB * SEQ, D], F32, kind="Internal").ap()
        s.xs = nc.dram_tensor("rows_by_expert", [NBLK * P, D], F32, kind="Internal").ap()
        s.ys = nc.dram_tensor("results_by_row", [NBLK * P, D], F32, kind="Internal").ap()
        s.x1_stored, s.converted, s.raw0_in, s.kept_in = (s.sem(n) for n in (
            "x1_stored", "converted", "raw0_in", "kept_in"))
        s.messages_stored = [s.sem(f"messages_stored{i}") for i in range(4)]

        with ExitStack() as scope:
            s.C, s.C_from = sb(scope, "consts_sb", [P, LAYER2_AT - LAYER1_AT]), LAYER1_AT
            s.vecs = sb(scope, "vecs_sb", [P, D + QR + KVR + NE])
            s.Wq = sb(scope, "wq_parts", [P, 2, H * KC], F32R)
            s.Wo = sb(scope, "wo_parts", [P, 2, NB, D], F32R)
            s.room(sb(scope, "room", [P, 20640]))
            with ExitStack() as inner:
                s.XN = sb(inner, "xn_keep", [P, NT, D])
                first_projections(s)
            s.qs = sb(scope, "q_latent_parts", [P, 2, 2, P], F32R)
            s.OT = sb(scope, "out_latent_parts", [P, 2, 2, 8 * P], F32R)
            s.gate = sb(scope, "gate_tiles", [P, 2, D])
            s.PT = sb(scope, "probs_t", [P, 2, 2, 4 * P])
            normalise_latents(s)
            attention(s)

        with ExitStack() as scope:
            room2 = sb(scope, "room2", [P, 2 * SLOT])
            s.raw0 = sb(scope, "first_expert", [P, SLOT])
            s.result = sb(scope, "attention_out", [P, 2 * NT * 2 * 64])
            s.C, s.C_from = sb(scope, "consts2_sb", [P, NCONST - LAYER2_AT]), LAYER2_AT
            s.room(room2)
            across_batch(s)
        with ExitStack() as scope:
            s.W = sb(scope, "expert_weights", [P, 4 * SLOT], F32R)
            s.xgT = sb(scope, "rows_t", [P, 2, 2, KT_PER_D * P], F32R)
            s.actT = sb(scope, "act_t", [P, 2, (FT + 1) * P], F32R)
            s.room(s.X[:, :, :].rearrange("p t n -> p (t n)"))
        s.kept = sb(ctx, "kept", [P, 2, NT, D])
        experts(s)
        s.room(sb(ctx, "room3", [P, 10000]))
        combine(s)


class Stages:

    def __init__(self, nc, ctx, a, out):
        self.nc, self.ctx, self.a, self.out = nc, ctx, a, out

    def room(self, r):
        self.R, self.ROOM, self.at = r, r.shape[-1], 0

    def psum(self, i):
        return self.bank[i // 2][:, 512 * (i % 2):512 * (i % 2) + 512]

    def const(self, name, pattern=None, **k):
        at, n = CONSTS[name]
        v = self.C[:, at - self.C_from:at - self.C_from + n]
        return v.rearrange(pattern, **k) if pattern else v

    def sem(self, name):
        return self.ctx.enter_context(self.nc.semaphore(name))

    def carve(self, *shape, dt=F32):
        n = int(np.prod(shape))
        v = self.R[:, self.at:self.at + n]
        self.at += n
        assert self.at <= self.ROOM, self.at
        if dt != F32:
            v = v.bitcast(dt)
        if len(shape) > 1:
            names = "abcd"[:len(shape)]
            v = v.rearrange(f"p ({' '.join(names)}) -> p {' '.join(names)}", **dict(zip(names, shape)))
        return v


def first_projections(s):
    nc, a, sem = s.nc, s.a, s.sem
    X, XN, psum, const, ident = s.X, s.XN, s.psum, s.const, s.ident
    s.at = 0
    s.ss = s.carve(NT, 2)
    s.latents_at = s.at
    wqn = s.carve(H, QR)
    wkb = s.carve(H, KVR)
    s.at = s.latents_at + NT * KC + NT * P + NT * P
    s.QKA = s.carve(NT, QKW)
    wo = s.carve(2, 2, D)
    rope_raw = s.carve(H, ROPE)
    W = s.carve(KT_PER_D, D)
    A = s.carve(KT_PER_D, P)
    B = s.carve(D)
    wqkv = s.carve(KT_PER_D, QKW)
    wvb = s.carve(H, KVR)
    rW = s.carve(KT_PER_D, NE)
    xnT = s.carve(2, KT_PER_D, P)
    tT = s.carve(2, P)
    junk = s.carve(P)
    st, mv, rs, tmp = s.carve(NT, 6), s.carve(NT, 2), s.carve(NT), s.carve(NT)
    qm, qmT, lg, m8, ex, sm8, rexp, rt = (s.carve(D), s.carve(KT_PER_D, NB), s.carve(NE), s.carve(1), s.carve(NE),
                                          s.carve(1), s.carve(NE, RANK), s.carve(NB))
    bias = s.vecs[:, 0:D]
    wq = s.Wq[:, :, :].rearrange("p i (h c) -> p i h c", h=H)
    rbias = s.vecs[0:NB, D + QR + KVR:D + QR + KVR + NE]

    GROUPS = ((0, 1), (1, 3), (3, 6), (6, 11), (11, 16))
    x_in = [sem(f"x_in{i}") for i in range(len(GROUPS))]
    consts_in, gate_w_in, qkv_w_in, fold_q_in, fold_v_in = (sem(n) for n in (
        "consts_in", "gate_w_in", "qkv_w_in", "fold_q_in", "fold_v_in"))
    rope_in, rope_high, foldq_low, foldo_low = (sem(n) for n in ("rope_in", "rope_high", "foldq_low", "foldo_low"))
    wo_in = [sem(f"wo_in{i}") for i in range(2)]
    var_ready, std_ready, xn_ready, dv, junk_done = (sem(n) for n in (
        "var_ready", "std_ready", "xn_ready", "first_dve", "junk_done"))
    means, means_out, means_t, means_t_out, logits, logits_out, exps, rexp_ready, rt_ps, rt_ready = (sem(n) for n in (
        "means", "means_out", "means_t", "means_t_out", "logits", "logits_out", "exps", "rexp_ready", "rt_ps",
        "rt_ready"))
    foldq, foldq_out, foldo, foldo_out = (sem(n) for n in ("foldq", "foldq_out", "foldo", "foldo_out"))
    turned, turned_out, lo_done, base_done, gate_done = (sem(n) for n in (
        "turned", "turned_out", "lo_done", "base_done", "gate_done"))
    qka_out, tT_ready, gate_out, silu_done = (sem(n) for n in (
        "qka_out", "tT_ready", "gate_out", "silu_done"))

    with nc.Block() as block:
        @block.sync
        def _(sp):
            def keep_gate(t):
                sp.wait_ge(silu_done, t + 1)
                sp.dma_start(s.gates[P * t:P * t + P, :], XN[:, t]).then_inc(s.gates_stored, 16)

            for g, (t0, t1) in enumerate(GROUPS):
                sp.dma_start(X[:, t0:t1, :],
                             a["x"][P * t0:P * t1, :].rearrange("(t p) h -> p t h", p=P)).then_inc(x_in[g], 16)
                if g == 2:
                    sp.dma_start(wqn[0:NOPE], a["wq_nope"]).then_inc(fold_q_in, 16)
                    sp.dma_start(wkb[0:NOPE], a["wkv_k"]).then_inc(fold_q_in, 16)
                if g == 0:
                    sp.dma_start(s.ident, a["consts"][:, 0:LAYER1_AT]).then_inc(consts_in, 16)
                    sp.dma_start(s.C[:, :], a["consts"][:, LAYER1_AT:LAYER2_AT]).then_inc(consts_in, 16)
            sp.dma_start(wqkv, a["wqkv"]).then_inc(qkv_w_in, 16)
            sp.dma_start(rope_raw, a["wq_rope"]).then_inc(rope_in, 16)
            for c in range(H // 2):
                if c >= 2:
                    sp.wait_ge(foldo, c // 2)
                sp.dma_start(wo[:, c % 2], a["wo"][:, 2 * c:2 * c + 2, :]).then_inc(wo_in[c % 2], 16)
                if c >= 4:
                    keep_gate(c - 4)
            for t in range(H // 2 - 4, NT):
                keep_gate(t)

        @block.gpsimd
        def _(pool):
            pool.wait_ge(x_in[2], 16)
            pool.dma_start(rW, a["router"]).then_inc(gate_w_in, 16)
            pool.dma_start(A, a["lora_a"]).then_inc(gate_w_in, 16)
            pool.dma_start(B, a["lora_b"]).then_inc(gate_w_in, 16)
            pool.dma_start(W, a["gate_w"]).then_inc(gate_w_in, 16)
            pool.dma_start(wvb, a["wkv_v"]).then_inc(fold_v_in, 16)

        @block.scalar
        def _(act):
            act.dma_start(s.vecs[:, :], a["vecs"].broadcast_to([P, D + QR + KVR + NE])).then_inc(consts_in, 16)
            for g, (t0, t1) in enumerate(GROUPS):
                act.wait_ge(var_ready, g + 1)
                nc.scalar.activation(tmp[:, t0:t1], mv[:, t0:t1, 1], ACT.Sqrt).then_inc(std_ready, 1)
            for g in range(2):
                act.wait_ge(foldq, g + 1)
                nc.scalar.activation(wq[:, HIGH, 16 * g:16 * g + 16, ROPE:KC],
                                     psum(4 + g).rearrange("p (h c) -> p h c", h=16), ACT.Copy).then_inc(foldq_out, 1)
            act.wait_ge(logits_out, 2)
            nc.scalar.activation(ex[0:NB], lg[0:NB], ACT.Exp, bias=m8[0:NB], accum_out=sm8[0:NB]).then_inc(exps, 1)

            def turn_out(t):
                act.wait_ge(turned, t + 1)
                if t >= 2:
                    act.wait_ge(base_done, t - 1)
                nc.scalar.activation(xnT[:, t % 2], psum(t % 2).rearrange("p (k n) -> p k n", k=4),
                                     ACT.Copy).then_inc(turned_out, 1)

            def fold_leaves(i):
                act.wait_ge(foldo, i + 1)
                nc.scalar.activation(s.Wo[:, HIGH, i], psum(6 + i % 2), ACT.Copy).then_inc(foldo_out, 1)

            junks = Chain(act, junk_done)
            turn_out(0)
            for t in range(NT):
                if t + 1 < NT:
                    turn_out(t + 1)
                if t == 2:
                    act.wait_ge(rope_in, 16)
                    nc.scalar.activation(wq[:, HIGH, :, 0:ROPE], rope_raw, ACT.Copy).then_inc(rope_high, 1)
                act.wait_ge(qka_out, t + 1)
                if t:
                    junks.wait()
                junks.then(nc.scalar.activation(junk, s.QKA[:, t, 0:QR], ACT.Square, accum_out=s.ss[:, t, 0:1]))
                junks(nc.scalar.activation(junk[:, 0:KVR], s.QKA[:, t, QR + ROPE:QKW], ACT.Square,
                                           accum_out=s.ss[:, t, 1:2]))
                if t % 2 == 0 and t:
                    fold_leaves(t // 2 - 1)
                if t:
                    act.wait_ge(gate_out, t)
                    nc.scalar.activation(XN[:, t - 1], XN[:, t - 1], ACT.Silu).then_inc(silu_done, 1)
            act.wait_ge(gate_out, NT)
            nc.scalar.activation(XN[:, NT - 1], XN[:, NT - 1], ACT.Silu).then_inc(silu_done, 1)
            fold_leaves(NB - 1)

        @block.vector
        def _(dve):
            v = nc.vector
            step = Chain(dve, dv)

            def statistics(g):
                dve.wait_ge(x_in[g], 16)
                for t in range(*GROUPS[g]):
                    step(v.bn_stats(st[:, t], X[:, t]))

            for g, (t0, t1) in enumerate(GROUPS):
                q = slice(t0, t1)
                if g == 0:
                    statistics(0)
                step.wait()
                for t in range(t0, t1):
                    step(v.bn_aggr(mv[:, t], st[:, t]))
                step.wait()
                v.tensor_scalar(mv[:, q, 1], mv[:, q, 1], LN_EPS, None, ALU.add).then_inc(var_ready, 1)
                if g + 1 < len(GROUPS):
                    statistics(g + 1)
                dve.wait_ge(std_ready, g + 1)
                rsqrt_refined(v, step, rs[:, q], tmp[:, q], mv[:, q, 1])
                for t in range(t0, t1):
                    v.tensor_scalar(XN[:, t], X[:, t], mv[:, t, 0:1], rs[:, t:t + 1], ALU.subtract,
                                    ALU.mult).then_inc(xn_ready, 1)
            dve.wait_ge(consts_in, 48)
            v.tensor_copy(s.identb[:, :], ident)
            v.tensor_copy(s.maskb[:, :], const("causal"))
            for g in range(2):
                dve.wait_ge(foldq_out, g + 1)
                v.tensor_tensor(wq[:, LOW, 16 * g:16 * g + 16, ROPE:KC], psum(4 + g).rearrange("p (h c) -> p h c", h=16),
                                wq[:, HIGH, 16 * g:16 * g + 16, ROPE:KC], ALU.subtract).then_inc(foldq_low, 1)

            def fold_rest(i):
                dve.wait_ge(foldo_out, i + 1)
                v.tensor_tensor(s.Wo[:, LOW, i], psum(6 + i % 2), s.Wo[:, HIGH, i], ALU.subtract).then_inc(foldo_low, 1)

            dve.wait_ge(means, 1)
            v.tensor_copy(qm[0:NB], psum(6)[0:NB]).then_inc(means_out, 1)
            dve.wait_ge(means_t, 1)
            v.tensor_copy(qmT, psum(7)[:, 0:32].rearrange("p (k b) -> p k b", k=4)).then_inc(means_t_out, 1)
            dve.wait_ge(logits, 1)
            step.then(v.tensor_tensor(lg[0:NB], psum(7)[0:NB, 64:64 + NE], rbias, ALU.add))
            step.then(v.tensor_reduce(m8[0:NB], lg[0:NB], AX.X, ALU.max))
            v.tensor_scalar(m8[0:NB], m8[0:NB], -1.0, None, ALU.mult).then_inc(logits_out, 2)
            dve.wait_ge(exps, 1)
            step.then(v.reciprocal(sm8[0:NB], sm8[0:NB]))
            step.then(v.tensor_scalar(lg[0:NB], ex[0:NB], sm8[0:NB], LORA_SCALE, ALU.mult, ALU.mult))
            v.tensor_copy(rexp[0:NB], lg[0:NB].unsqueeze(2).broadcast_to([NB, NE, RANK])).then_inc(rexp_ready, 1)
            dve.wait_ge(rt_ps, 1)
            v.tensor_copy(rt, psum(7)[:, 128:128 + NB]).then_inc(rt_ready, 1)
            dve.wait_ge(rt_ready, 1)
            for t in range(NT):
                ps = psum(2 + t % 2)
                dve.wait_ge(lo_done, t + 1)
                if t >= 2:
                    dve.wait_ge(gate_done, t - 1)
                v.tensor_scalar(tT[:, t % 2], ps[:, 256:256 + P], rt[:, t // 2:t // 2 + 1], None,
                                ALU.mult).then_inc(tT_ready, 1)
                v.tensor_copy(s.QKA[:, t], ps[:, 0:QKW]).then_inc(qka_out, 1)
                if t == 3:
                    dve.wait_ge(rope_high, 1)
                    v.tensor_tensor(wq[:, LOW, :, 0:ROPE], rope_raw, wq[:, HIGH, :, 0:ROPE],
                                    ALU.subtract).then_inc(foldq_low, 1)
                dve.wait_ge(gate_done, t + 1)
                v.tensor_tensor(XN[:, t], psum(4 + t % 2), bias, ALU.add).then_inc(gate_out, 1)
                if t % 2 == 0 and t:
                    fold_rest(t // 2 - 1)
            fold_rest(NB - 1)

        @block.tensor
        def _(pe):
            mm = nc.tensor.matmul
            pe.wait_ge(consts_in, 48)
            mean = const("mean", "p (k c) -> p k c", k=2)

            def fold_q(g):
                pe.wait_ge(fold_q_in, 32)
                for h in range(16 * g, 16 * g + 16):
                    last = mm(psum(4 + g)[:, 32 * (h % 16):32 * (h % 16) + 32], wqn[0:NOPE, h], wkb[0:NOPE, h],
                              start=True, stop=True)
                last.then_inc(foldq, 1)

            for t in range(NT):
                pe.wait_ge(xn_ready, t + 1)
                b = t // 2
                last = mm(psum(6)[0:NB], mean[:, t % 2, 7 - b:15 - b], XN[:, t], start=(t == 0), stop=(t == NT - 1))
                if t == NT - 1:
                    last.then_inc(means, 1)
                if t in (7, 11):
                    fold_q(t // 4 - 1)
            pe.wait_ge(means_out, 1)
            for k in range(4):
                last = nc.tensor.transpose(psum(7)[:, 8 * k:8 * k + 8], qm[0:NB, P * k:P * k + P], ident[0:NB, 0:NB])
            last.then_inc(means_t, 1)
            pe.wait_ge(means_t_out, 1)
            pe.wait_ge(gate_w_in, 64)
            for k in range(4):
                last = mm(psum(7)[0:NB, 64:64 + NE], qmT[:, k], rW[:, k], start=(k == 0), stop=(k == 3))
            last.then_inc(logits, 1)

            def turn(t):
                if t >= 2:
                    pe.wait_ge(turned_out, t - 1)
                for k in range(4):
                    last = nc.tensor.transpose(psum(t % 2)[:, P * k:P * k + P], XN[:, t, P * k:P * k + P], ident)
                last.then_inc(turned, 1)

            turn(0)
            pe.wait_ge(rexp_ready, 1)
            mm(psum(7)[:, 128:128 + NB], rexp[0:NB].rearrange("p e r -> p (e r)"), ident[0:NB, 0:NB], start=True,
               stop=True).then_inc(rt_ps, 1)
            pe.wait_ge(qkv_w_in, 16)
            pe.wait_ge(foldq_low, 2)
            for t in range(NT):
                if t + 1 < NT:
                    turn(t + 1)
                pe.wait_ge(turned_out, t + 1)
                if t >= 2:
                    pe.wait_ge(qka_out, t - 1)
                ps, xT = psum(2 + t % 2), xnT[:, t % 2]
                for k in range(4):
                    mm(ps[:, 0:QKW], xT[:, k], wqkv[:, k], start=(k == 0), stop=(k == 3))
                for k in range(4):
                    last = mm(ps[:, 256:256 + P], A[:, k], xT[:, k], start=(k == 0), stop=(k == 3))
                last.then_inc(lo_done, 1)
                if t >= 2:
                    pe.wait_ge(gate_out, t - 1)
                for k in range(4):
                    last = mm(psum(4 + t % 2), xT[:, k], W[:, k], start=(k == 0), stop=False)
                last.then_inc(base_done, 1)
                pe.wait_ge(tT_ready, t + 1)
                mm(psum(4 + t % 2), tT[:, t % 2], B, start=False, stop=True).then_inc(gate_done, 1)
                if t % 2 == 1:
                    i = t // 2
                    if i == 0:
                        pe.wait_ge(fold_v_in, 16)
                        pe.wait_ge(rt_ready, 1)
                    if i >= 2:
                        pe.wait_ge(foldo_low, i - 1)
                    for j in range(4):
                        pe.wait_ge(wo_in[j // 2], 16 * (i + 1))
                        last = mm(psum(6 + i % 2)[32 * j:32 * j + 32], wvb[:, 4 * i + j], wo[:, j // 2, j % 2],
                                  start=True, stop=True)
                    last.then_inc(foldo, 1)


def rsqrt_refined(v, step, r, root, x):
    step.then(v.reciprocal(r, root))
    step.then(v.tensor_tensor(root, r, r, ALU.mult))
    step.then(v.tensor_tensor(root, root, x, ALU.mult))
    step.then(v.tensor_scalar(root, root, -0.5, 1.5, ALU.mult, ALU.add))
    step.then(v.tensor_tensor(r, r, root, ALU.mult))


def normalise_latents(s):
    nc, sem, psum, const, ident = s.nc, s.sem, s.psum, s.const, s.ident
    QKA = s.QKA
    s.at = s.latents_at
    s.KR = s.carve(NT, KC)
    s.KT = s.carve(NT * P)
    s.QAT = s.carve(NT, P)
    s.keep = s.at
    s.at += NT * QKW
    t2 = s.carve(NT, ROPE)
    var, root, rr = s.carve(NT, 2), s.carve(NT, 2), s.carve(NT, 2)
    qln = s.vecs[:, D:D + QR]
    kvln = s.vecs[:, D + QR:D + QR + KVR]
    lat_dve, var2, std2, rr_ready, q_ready, pl, k_ready, tq = (sem(n) for n in (
        "lat_dve", "var2", "std2", "rr_ready", "q_ready", "lat_pool", "k_ready", "tq"))

    with nc.Block() as block:
        @block.scalar
        def _(act):
            act.wait_ge(var2, 2)
            nc.scalar.activation(root, var, ACT.Sqrt).then_inc(std2, 1)
            for g in range(4):
                act.wait_ge(tq, g + 1)
                nc.scalar.activation(s.QAT[:, 4 * g:4 * g + 4], psum(g).rearrange("p (t n) -> p t n", t=4),
                                     ACT.Copy)

        @block.vector
        def _(dve):
            v = nc.vector
            step = Chain(dve, lat_dve)
            v.tensor_scalar(var[:, :, 0], s.ss[:, :, 0], 1.0 / QR, RMS_EPS, ALU.mult, ALU.add).then_inc(var2, 1)
            v.tensor_scalar(var[:, :, 1], s.ss[:, :, 1], 1.0 / KVR, RMS_EPS, ALU.mult, ALU.add).then_inc(var2, 1)
            dve.wait_ge(std2, 1)
            rsqrt_refined(v, step, rr, root, var)
            v.tensor_copy(root, rr).then_inc(rr_ready, 1)
            for g in range(4):
                part = QKA[:, 4 * g:4 * g + 4, 0:QR]
                step.then(v.tensor_tensor(part, part, rr[:, 4 * g:4 * g + 4, 0:1].broadcast_to([P, 4, QR]), ALU.mult))
                v.tensor_tensor(part, part, qln.unsqueeze(1).broadcast_to([P, 4, QR]), ALU.mult).then_inc(q_ready, 1)
            for g in range(4):
                dve.wait_ge(tq, 4 + g + 1)
                v.tensor_copy(s.KT[0:KC, 512 * g:512 * g + 512], psum(4 + g)[0:KC])

        @block.gpsimd
        def _(pool):
            g = nc.gpsimd
            step = Chain(pool, pl)
            pe = QKA[:, :, QR:QR + ROPE].rearrange("p (b k) c -> p b k c", k=2)
            kr = s.KR[:, :, 0:ROPE].rearrange("p (b k) c -> p b k c", k=2)
            turn = t2.rearrange("p (b k) c -> p b k c", k=2)
            cos = const("cos", "p (k c) -> p k c", k=2)
            sin = const("sin", "p (k c) -> p k c", k=2)
            half = ROPE // 2

            def over_b(table):
                return table.unsqueeze(1).broadcast_to([P, NB, 2, table.shape[-1]])

            step(g.tensor_tensor(kr, pe, over_b(cos[:, :, 0:ROPE]), ALU.mult))
            step(g.tensor_tensor(turn[:, :, :, 0:half], pe[:, :, :, half:ROPE], over_b(sin[:, :, 0:half]), ALU.mult))
            step(g.tensor_tensor(turn[:, :, :, half:ROPE], pe[:, :, :, 0:half], over_b(sin[:, :, half:ROPE]), ALU.mult))
            step.wait()
            step(g.tensor_tensor(s.KR[:, :, 0:ROPE], s.KR[:, :, 0:ROPE], t2, ALU.add))
            pool.wait_ge(rr_ready, 1)
            lat = s.KR[:, :, ROPE:KC]
            step.then(g.tensor_tensor(lat, QKA[:, :, QR + ROPE:QKW], rr[:, :, 1:2].broadcast_to([P, NT, KVR]), ALU.mult))
            g.tensor_tensor(lat, lat, kvln.unsqueeze(1).broadcast_to([P, NT, KVR]), ALU.mult).then_inc(k_ready, 1)
            pool.wait_ge(s.gates_stored, 16 * NT)

        @block.tensor
        def _(pe):
            for g in range(4):
                pe.wait_ge(q_ready, g + 1)
                for i in range(4):
                    last = nc.tensor.transpose(psum(g)[:, P * i:P * i + P], QKA[:, 4 * g + i, 0:QR], ident)
                last.then_inc(tq, 1)
            pe.wait_ge(k_ready, 1)
            for g in range(4):
                for i in range(4):
                    last = nc.tensor.transpose(psum(4 + g)[0:KC, P * i:P * i + P], s.KR[:, 4 * g + i], ident)
                last.then_inc(tq, 1)


def attention(s):
    nc, sem, psum, const, ident = s.nc, s.sem, s.psum, s.const, s.ident
    X = s.X
    s.at = s.keep
    QT = s.carve(2, H, P)
    Pr = s.carve(4, 4, SEQ)
    PT = s.PT
    OT = s.OT
    gate = s.gate
    qtok = s.carve(2, 4, KC)
    qrot = s.carve(2, 4, ROPE)
    cks = s.carve(2, KVR)
    x_new = s.carve(D)
    qs, Wq = s.qs, s.Wq
    mx, nb, sm, rs = s.carve(2, 4), s.carve(2, 4), s.carve(2, 4), s.carve(2, 4)
    st, mv = s.carve(6), s.carve(2)
    half = ROPE // 2
    cos = const("cos", "p (k c) -> p k c", k=2)
    sin = const("sin", "p (k c) -> p k c", k=2)
    (scored, maxed, bias_ready, expd, summed, normed, chunk_done, roped, q_added, q_turned, q_out, p_turned, p_out,
     k1_turned, k1_out, pv_done, o_out, proj_done, proj_used, x_done, q_staged, q_low, v_staged, x_summed,
     stats_done, o_low) = (sem(n) for n in (
         "scored", "maxed", "bias_ready", "expd", "summed", "normed", "chunk_done", "roped", "q_added", "q_turned",
         "q_out", "p_turned", "p_out", "k1_turned", "k1_out", "pv_done", "o_out", "proj_done", "proj_used",
         "x_done", "q_staged", "q_low", "v_staged", "x_summed",
         "stats_done", "o_low"))
    gate_in = [sem(f"gate_in{i}") for i in range(2)]
    LAST = NB - 1
    PRO = 8

    def scores_bank(m):
        return s.bank[m % 2]

    def k1_before(m):
        return m - 1 if m < 2 else max(0, m - 9)

    def kw(m):
        return P if m % 16 < 8 else SEQ

    def heads(m):
        u = m % 8
        return [4 * (4 * (u // 4) + ii) + u % 4 for ii in range(4)]

    class PE:
        def __init__(self, pe):
            self.pe = pe

        def chunk(self, b, m, n):
            pe = self.pe
            qt = (m // 8 + 1) % 2
            pe.wait_ge(chunk_free := roped, n + PRO) if not (isinstance(n, int) and n + PRO <= 0) else None
            if m % 8 == 0:
                pe.wait_ge(q_low, 1 if m < 0 else b * 2 + (2 if m == 0 else 3))
            u = m % 8
            for i, (of_q, of_w) in enumerate(PASSES):
                last = nc.tensor.matmul(psum(6)[:, 0:4 * KC], qs[:, of_q, qt], Wq[:, of_w, 4 * KC * u:4 * KC * (u + 1)],
                                        start=(i == 0), stop=(i == 2))
            last.then_inc(chunk_done, 1)

        def turn_q(self, b, m, n):
            pe = self.pe
            pe.wait_ge(q_added, n + PRO)
            if not (isinstance(n, int) and n + PRO <= 1):
                pe.wait_ge(q_out, n + PRO - 1)
            if m >= 0 and not (isinstance(b, int) and b == 0 and k1_before(m) <= 0):
                pe.wait_ge(k1_out, b * 8 + k1_before(m))
            for hh in range(4):
                last = nc.tensor.transpose(psum(4)[0:KC, P * hh:P * hh + P], qtok[:, (m - 1) % 2, hh], ident)
            last.then_inc(q_turned, 1)

        def score(self, b, m, n):
            pe = self.pe
            qt, u = m // 8, m % 8
            pe.wait_ge(q_out, b * 16 + 8 * qt + 4 * (u // 4 + 1))
            if not (isinstance(n, int) and n < 2):
                pe.wait_ge(expd, n - 1)
            w = kw(m)
            ps = scores_bank(m)
            for hh, h in enumerate(heads(m)):
                nc.tensor.matmul(ps[:, w * hh:w * hh + w], QT[0:KC, qt, h], s.KT[0:KC, ds(b * SEQ, w)],
                                 start=True, stop=False, skip_group_check=True)
                last = nc.tensor.matmul(ps[:, w * (hh + 1) - P:w * (hh + 1)], s.identb[:, :], s.maskb[:, :],
                                        start=False, stop=True, skip_group_check=True)
            last.then_inc(scored, 1)

        def turn_p(self, m, n, kt):
            pe = self.pe
            pe.wait_ge(normed, n + 1)
            if kt == 0 and not (isinstance(n, int) and n < 1):
                pe.wait_ge(p_out, n)
            for hh in range(4):
                last = nc.tensor.transpose(psum(5 - kt)[:, P * hh:P * hh + P],
                                           Pr[:, m % 4, hh, P * kt:P * kt + P], ident)
            last.then_inc(k1_turned if kt else p_turned, 1)

        def values(self, b, m, n):
            pe = self.pe
            pe.wait_ge(p_out, n + 1)
            if kw(m) == SEQ:
                pe.wait_ge(k1_out, b * 8 + (m - 8) + 1)
            if m % 4 == 0 and not (isinstance(n, int) and n < 4):
                pe.wait_ge(o_low, b * 4 + m // 4)
            if m == 0:
                pe.wait_ge(v_staged, b + 1)
            j = m % 4
            for kt in range(kw(m) // P):
                last = nc.tensor.matmul(psum(7)[32 * j:32 * j + 32], cks[:, kt], PT[:, m % 2, kt],
                                        start=(kt == 0), stop=(kt == kw(m) // P - 1))
            last.then_inc(pv_done, 1)

        def project(self, b, qt):
            pe = self.pe
            pe.wait_ge(o_low, b * 4 + 2 * qt + 2)
            for p, (of_o, of_w) in enumerate(PASSES):
                for i in range(8):
                    last = nc.tensor.matmul(psum(6), OT[:, of_o, qt, P * i:P * i + P], s.Wo[:, of_w, i],
                                            start=(p == 0 and i == 0), stop=(p == 2 and i == 7))
            last.then_inc(proj_done, 1)

    def last_entry(b):
        return isinstance(b, int) and b >= LAST

    def chunk_here(b, m, live):
        return live and not (last_entry(b) and m >= 8)

    def chunk_turned(b, m, live):
        return live and not (last_entry(b) and m >= 9)

    def chunks_before(b, m, n, live):
        return n + PRO if not last_entry(b) or (b == LAST and m <= 8) else 16 * NB

    def parts(b, m, first):
        def behind(lag):
            if m - lag >= 0:
                return b, m - lag
            return None if first else (b - 1, m - lag + 16)
        return behind

    def pe_step(pe, b, m, first=False, live=True):
        n = b * 16 + m
        w = PE(pe)
        behind = parts(b, m, first)
        if m in (5, 13) and not (first and m == 5) or (not live and m == 3):
            bb, qt = (b - 1, 1) if m in (5, 3) else (b, 0)
            pe.wait_ge(roped, chunks_before(b, m, n, live))
            w.project(bb, qt)
        if live:
            w.score(b, m, n)
            if chunk_here(b, m, live):
                if m in (5, 13) and not (first and m == 5):
                    pe.wait_ge(proj_used, b * 2 if m == 5 else b * 2 + 1)
                w.chunk(b, m, n)
        two = behind(2)
        if two and (live or m < 2):
            if kw(two[1]) == SEQ:
                if last_entry(b) and (b > LAST or m > 10):
                    pe.wait_ge(k1_out, two[0] * 8 + two[1] - 8)
                else:
                    pe.wait_ge(q_out, min(n + PRO - 1, 16 * NB) if last_entry(b) else n + PRO - 1)
                w.turn_p(two[1], n - 2, 1)
            w.turn_p(two[1], n - 2, 0)
        three = behind(3)
        if three and (live or m < 3):
            w.values(three[0], three[1], n - 3)
        if chunk_turned(b, m, live):
            w.turn_q(b, m, n)

    def dve_step(dve, b, m, first=False, live=True):
        v = nc.vector
        n = b * 16 + m
        behind = parts(b, m, first)
        if m == 3 and live:
            if not first:
                dve.wait_ge(pv_done, b * 16)
            v.tensor_copy(cks, s.KR[:, ds(b * 2, 2), ROPE:KC]).then_inc(v_staged, 1)
        tile = None
        if m in (5, 13) and not (first and m == 5) or (not live and m == 3):
            tile = b * 2 - 1 if m in (5, 3) else b * 2
            dve.wait_ge(proj_done, tile + 1)
            if not (isinstance(tile, int) and tile == 0):
                dve.wait_ge(x_done, tile)
                dve.wait_ge(stats_done, tile * 3)
            dve.wait_ge(gate_in[0 if m == 13 else 1], b * 16 + 16 if m == 13 else b * 16)
            v.tensor_tensor(x_new, psum(6), gate[:, 0 if m == 13 else 1], ALU.mult).then_inc(proj_used, 1)
            dve.wait_ge(proj_used, tile + 1)
            v.tensor_tensor(x_new, X[:, ds(tile, 1)].rearrange("p t n -> p (t n)"), x_new, ALU.add).then_inc(x_summed, 1)
        if live:
            par, w = m % 2, kw(m)
            dve.wait_ge(scored, n + 1)
            v.tensor_reduce(mx[:, par], scores_bank(m)[:, 0:4 * w].rearrange("p (h k) -> p h k", h=4), AX.X,
                            ALU.max).then_inc(maxed, 1)
            dve.wait_ge(maxed, n + 1)
            v.tensor_scalar(nb[:, par], mx[:, par], -SCALE, None, ALU.mult).then_inc(bias_ready, 1)
            if chunk_here(b, m, live):
                rope(dve, b, m, n)
            if m in (1, 9) and not last_entry(b):
                tile = b * 2 + (2 if m == 1 else 3)
                dve.wait_ge(q_staged, tile + 1)
                v.tensor_tensor(qs[:, LOW, m // 9], s.QAT[:, ds(tile, 1)].rearrange("p t n -> p (t n)"),
                                qs[:, HIGH, m // 9], ALU.subtract).then_inc(q_low, 1)
                tile = None
        one = behind(1)
        if one and (live or m < 1):
            dve.wait_ge(expd, n)
            if not (isinstance(n, int) and n < 3):
                dve.wait_ge(normed, n - 2)
            v.reciprocal(rs[:, one[1] % 2], sm[:, one[1] % 2]).then_inc(summed, 1)
        two = behind(2)
        if two and (live or m < 2):
            dve.wait_ge(p_turned, n - 1)
            v.tensor_copy(PT[:, two[1] % 2, 0], psum(5)).then_inc(p_out, 1)
        three = behind(3)
        if three and (live or m < 3) and three[1] % 4 == 3:
            dve.wait_ge(o_out, three[0] * 4 + three[1] // 4 + 1)
            half_of = slice(4 * P * (three[1] // 4 % 2), 4 * P * (three[1] // 4 % 2 + 1))
            v.tensor_tensor(OT[:, LOW, three[1] // 8, half_of], psum(7), OT[:, HIGH, three[1] // 8, half_of],
                            ALU.subtract).then_inc(o_low, 1)
        if tile is not None:
            dve.wait_ge(x_summed, tile + 1)
            v.bn_stats(st, x_new).then_inc(stats_done, 1)
            dve.wait_ge(stats_done, tile * 3 + 1)
            dve.nop(nofuse=True)
            v.bn_aggr(mv, st).then_inc(stats_done, 1)
            dve.wait_ge(stats_done, tile * 3 + 2)
            v.tensor_copy(s.mv[:, ds(tile, 1)].rearrange("p t n -> p (t n)"), mv).then_inc(stats_done, 1)

    def rope(dve, b, m, n):
        v = nc.vector
        par, k = m % 2, (m // 8 + 1) % 2
        q = psum(6)[:, 0:4 * KC].rearrange("p (h c) -> p h c", h=4)
        dve.wait_ge(chunk_done, n + PRO + 1)
        if not (isinstance(n, int) and n + PRO < 2):
            dve.wait_ge(q_turned, n + PRO - 1)

        def over_h(table):
            return table.unsqueeze(1).broadcast_to([P, 4, table.shape[-1]])

        v.tensor_tensor(qtok[:, par], q, over_h(cos[:, k]), ALU.mult)
        v.tensor_tensor(qrot[:, par, :, 0:half], q[:, :, half:ROPE], over_h(sin[:, k, 0:half]), ALU.mult)
        v.tensor_tensor(qrot[:, par, :, half:ROPE], q[:, :, 0:half], over_h(sin[:, k, half:ROPE]),
                        ALU.mult).then_inc(roped, 1)

    def act_step(act, b, m, first=False, live=True):
        sc = nc.scalar
        n = b * 16 + m
        behind = parts(b, m, first)
        two = behind(2)
        if two and (live or m < 2) and kw(two[1]) == SEQ:
            act.wait_ge(k1_turned, two[0] * 8 + two[1] - 8 + 1)
            sc.activation(PT[:, two[1] % 2, 1], psum(4), ACT.Copy).then_inc(k1_out, 1)
        if live:
            if m == 1 and not last_entry(b):
                act.wait_ge(chunk_done, b * 16 + PRO)
                sc.activation(qs[:, HIGH, 0], s.QAT[:, ds(b * 2 + 2, 1)].rearrange("p t n -> p (t n)"),
                              ACT.Copy).then_inc(q_staged, 1)
            if m == 9 and not last_entry(b):
                act.wait_ge(chunk_done, b * 16 + PRO + 8)
                sc.activation(qs[:, HIGH, 1], s.QAT[:, ds(b * 2 + 3, 1)].rearrange("p t n -> p (t n)"),
                              ACT.Copy).then_inc(q_staged, 1)
            par, w = m % 2, kw(m)
            act.wait_ge(bias_ready, n + 1)
            for hh in range(4):
                last = sc.activation(Pr[:, m % 4, hh, 0:w], scores_bank(m)[:, w * hh:w * hh + w], ACT.Exp,
                                     bias=nb[:, par, hh:hh + 1], scale=SCALE, accum_out=sm[:, par, hh:hh + 1])
            last.then_inc(expd, 1)
            if chunk_turned(b, m, live):
                q_leaves(act, m, n)
        three = behind(3)
        if three and (live or m < 3) and three[1] % 4 == 3:
            act.wait_ge(pv_done, n - 2)
            qt, hf = three[1] // 8, three[1] // 4 % 2
            sc.activation(OT[:, HIGH, qt, 4 * P * hf:4 * P * hf + 4 * P], psum(7), ACT.Copy).then_inc(o_out, 1)
        if m in (5, 13) and not (first and m == 5) or (not live and m == 3):
            tile = b * 2 - 1 if m in (5, 3) else b * 2
            act.wait_ge(x_summed, tile + 1)
            nc.scalar.activation(X[:, ds(tile, 1)].rearrange("p t n -> p (t n)"), x_new, ACT.Copy).then_inc(x_done, 1)

    def q_leaves(act, m, n):
        act.wait_ge(q_turned, n + PRO)
        qt, u = ((m - 1) // 8 + 1) % 2, (m - 1) % 8
        nc.scalar.activation(QT[0:KC, qt, 4 * u:4 * u + 4], psum(4)[0:KC].rearrange("p (h q) -> p h q", h=4),
                             ACT.Copy).then_inc(q_out, 1)

    def pool_step(pool, b, m, first=False, live=True):
        g = nc.gpsimd
        n = b * 16 + m
        one = parts(b, m, first)(1)
        if one and (live or m < 1):
            pool.wait_ge(summed, n)
            w = kw(one[1])
            pr = Pr[:, one[1] % 4, :, 0:w]
            g.tensor_tensor(pr, pr, rs[:, one[1] % 2].unsqueeze(2).broadcast_to([P, 4, w]), ALU.mult).then_inc(normed, 1)
        if chunk_here(b, m, live):
            q_sum(pool, m, n)

    def q_sum(pool, m, n):
        pool.wait_ge(roped, n + PRO + 1)
        q = qtok[:, m % 2, :, 0:ROPE]
        nc.gpsimd.tensor_tensor(q, q, qrot[:, m % 2], ALU.add).then_inc(q_added, 1)

    def whole(eng, step):
        for m in range(16):
            step(eng, 0, m, first=True)
        with eng.Fori(1, LAST) as b:
            for m in range(16):
                step(eng, b, m)
        for m in range(16):
            step(eng, LAST, m)
        for m in range(4):
            step(eng, NB, m, live=False)

    with nc.Block() as block:
        @block.tensor
        def _(pe):
            w = PE(pe)
            for m in range(-8, 0):
                w.chunk(0, m, m)
                if m > -8:
                    w.turn_q(0, m, m)
            whole(pe, pe_step)

        @block.vector
        def _(dve):
            for t in range(2):
                dve.wait_ge(q_staged, t + 1)
                nc.vector.tensor_tensor(qs[:, LOW, t], s.QAT[:, t], qs[:, HIGH, t], ALU.subtract).then_inc(q_low, 1)
            for m in range(-8, 0):
                rope(dve, 0, m, m)
            whole(dve, dve_step)

        @block.scalar
        def _(act):
            for t in range(2):
                nc.scalar.activation(qs[:, HIGH, t], s.QAT[:, t], ACT.Copy).then_inc(q_staged, 1)
            for m in range(-7, 0):
                q_leaves(act, m, m)
            whole(act, act_step)

        @block.gpsimd
        def _(pool):
            for m in range(-8, 0):
                q_sum(pool, m, m)
            whole(pool, pool_step)

        @block.sync
        def _(sp):
            def load(t, par):
                sp.dma_start(gate[:, par], s.gates[ds(t * P, P), :]).then_inc(gate_in[par], 16)

            def keep(t):
                sp.wait_ge(x_done, t + 1)
                sp.dma_start(s.x1[ds(t * P, P), :], X[:, ds(t, 1)].rearrange("p t n -> p (t n)")).then_inc(
                    s.x1_stored, 16)

            load(0, 0)
            load(1, 1)
            with sp.Fori(0, NT // 2 - 1) as i:
                for par in range(2):
                    keep(i * 2 + par)
                    load(i * 2 + par + 2, par)
            keep(NT - 2)
            keep(NT - 1)


def bring_chunk(eng, s, e, c, to):
    at, rows, n = CHUNKS[c]
    if at < W13:
        return eng.dma_start(to[:, 0:n], s.a["w13"][e][:, at:at + n])
    t = (at - W13) // D
    if rows < P:
        return eng.dma_start(to[0:rows, 0:n], s.a["w2_rest"][e])
    return eng.dma_start(to[:, 0:n].rearrange("p (t n) -> p t n", n=D),
                         s.a["w2"][e, t * P:(t + n // D) * P].rearrange("(t p) n -> p t n", p=P))


def parts_of(s, c, at0):
    at, rows, n = CHUNKS[c]
    return s.W[0:rows, at0 + at:at0 + at + n], s.W[0:rows, at0 + SLOT + at:at0 + SLOT + at + n]


def low_of(s, c, raw, at0):
    high, low = parts_of(s, c, at0)
    if c == len(CHUNKS) - 1:
        raw, high = raw[REST_LOW], high[REST_LOW]
        low = high
    return s.nc.gpsimd.tensor_tensor(low, raw, high, ALU.subtract)


def across_batch(s):
    nc, sem, psum, const, ident = s.nc, s.sem, s.psum, s.const, s.ident
    X = s.X
    XP = s.carve(2, D, NB)
    XT = s.carve(2, KT_PER_D, 512)
    result = s.result[:, :].rearrange("p (r t c) -> p r t c", r=2, t=NT)
    mv, rs, root = s.mv, s.carve(NT), s.carve(NT)
    g1 = s.carve(KT_PER_D, E)
    zeros = s.carve(D)
    onesb, beforeb, zerosb = s.carve(P // 2, dt=BF16), s.carve(P // 2, dt=BF16), s.carve(E * (NT + 1) // 2, dt=BF16)
    starts, of_block, odd = s.carve(E), s.carve(NBLK), s.carve(NBLK)
    n_blocks = s.carve(E)
    which = s.carve(NBLK, E - 1)
    routing_at = s.at
    LT = s.carve(NT * P)
    p = s.carve(NT, E)
    top, sums = s.carve(NT), s.carve(NT)
    big1, big2 = s.carve(NT, E, E), s.carve(NT, E, E)
    rank, first, second = s.carve(NT, E), s.carve(NT, E), s.carve(NT, E)
    chosen = s.carve(NT * E // 2, dt=BF16).rearrange("p (t e) -> p t e", e=E)
    within = s.carve(NT, E)
    over = s.carve(E, 16)
    before_e, row_starts = s.carve(E, E), s.carve(E)
    slotf, vals = s.carve(NT, 2), s.carve(NT, 2)
    s.at = routing_at
    pr, pt, xg = s.carve(3, 4, P), s.carve(2, 4, P), s.carve(3, 2, 4, P)
    mx, nb, sm, rc = s.carve(2, 4), s.carve(2, 4), s.carve(2, 4), s.carve(2, 4)
    ROUNDS = 8
    INV = 1.0 / math.sqrt(SEQ)
    xs = s.xs
    by_group = XP.rearrange("p k (g l) b -> p k g (l b)", l=16)

    (dv, var_ready, std_ready, xn_ready, turned, turned_out, g1_in, zeroed, blank, logit, logit_out, lt, p_ex, p_exd,
     chosen_ready, counted, slots_ready, sorted_, mask_ready, batched, consts2_in) = (sem(n) for n in (
         "l2_dve", "l2_var", "l2_std", "xn1_ready", "x1_turned", "x1_turned_out", "g1_in", "zeroed", "blank",
         "logit", "logit_out", "logit_turned", "p_ex", "p_exd", "chosen_ready", "counted", "slots_ready", "sorted",
         "mask_ready", "batched", "consts2_in"))
    (a_scored, a_maxed, a_bias, a_exp, a_recip, a_norm, a_pt, a_pt_out, a_xt, a_xt_a, a_xt_v, a_msg, a_added) = (
        sem(n) for n in ("a_scored", "a_maxed", "a_bias", "a_exp", "a_recip", "a_norm", "a_pt", "a_pt_out", "a_xt",
                         "a_xt_a", "a_xt_v", "a_msg", "a_added"))

    with nc.Block() as block:
        @block.sync
        def _(sp):
            sp.dma_start(g1, s.a["gate1"]).then_inc(g1_in, 16)
            sp.dma_start(s.C[:, :], s.a["consts"][:, LAYER2_AT:]).then_inc(consts2_in, 16)
            sp.wait_ge(zeroed, 1)
            sp.dma_start(xs.rearrange("(n p) h -> p n h", p=P),
                         zeros.unsqueeze(1).broadcast_to([P, NBLK, D])).then_inc(blank, 16)
            for c, (at, rows, n) in enumerate(CHUNKS):
                bring_chunk(sp, s, 0, c, s.raw0[:, at:at + n]).then_inc(s.raw0_in, 16)
            for two in range(ROUNDS // 2):
                sp.wait_ge(a_added, 4 * (two + 1))
                sp.dma_start(s.messages[:, P * two:P * two + P].rearrange("(t p) h -> p t h", p=P),
                             result[:, two % 2]).then_inc(s.messages_stored[two], 16)

        @block.gpsimd
        def _(pool):
            nc.gpsimd.memset(zeros, 0.0).then_inc(zeroed, 1)
            nc.gpsimd.memset(onesb, 1.0).then_inc(zeroed, 1)
            nc.gpsimd.memset(zerosb, 0.0).then_inc(zeroed, 1)
            for t in range(NT):
                pool.wait_ge(xn_ready, t + 1)
                nc.gpsimd.tensor_copy(XP[:, t % 2, :, t // 2], X[:, t]).then_inc(batched, 1)
            pool.wait_ge(blank, 16)
            pool.wait_ge(slots_ready, 1)
            for t in range(NT):
                for k in range(2):
                    nc.gpsimd.indirect_dma_start(
                        out=xs, out_offset=bass.IndirectOffsetOnAxis(ap=s.slots[:, t, k:k + 1], axis=0),
                        in_=X[:, t], in_offset=None).then_inc(sorted_, 16)
            pool.wait_ge(sorted_, 16 * 2 * NT)

        @block.scalar
        def _(act):
            sc = nc.scalar

            def logits_leave(c):
                act.wait_ge(logit, c + 1)
                sc.activation(LT[0:E, 512 * c:512 * c + 512], psum(2 + c % 2)[0:E], ACT.Copy).then_inc(logit_out, 1)

            act.wait_ge(var_ready, 1)
            sc.activation(root, mv[:, :, 1], ACT.Sqrt).then_inc(std_ready, 1)
            for t in range(NT):
                act.wait_ge(turned, t + 1)
                if t % 4 == 0 and t >= 8:
                    act.wait_ge(logit, t // 4 - 1)
                sc.activation(XT[:, t // 4 % 2, :, P * (t % 4):P * (t % 4) + P], psum(t % 2).rearrange("p (k n) -> p k n", k=4),
                              ACT.Copy).then_inc(turned_out, 1)
                if t % 4 == 2 and t > 4:
                    logits_leave(t // 4 - 1)
            logits_leave(3)
            act.wait_ge(p_ex, 1)
            sc.activation(p, p, ACT.Exp).then_inc(p_exd, 1)

            def bring_x(r):
                act.wait_ge(a_xt, 2 * r + 1)
                if r >= 3:
                    act.wait_ge(a_msg, 2 * (r - 2))
                sc.activation(xg[:, r % 3, 0], psum(4).rearrange("p (g c) -> p g c", g=4), ACT.Copy).then_inc(a_xt_a, 1)

            def bring_p(r):
                act.wait_ge(a_pt, r + 1)
                sc.activation(pt[:, r % 2], psum(6).rearrange("p (g c) -> p g c", g=4), ACT.Copy).then_inc(a_pt_out, 1)

            for r in range(ROUNDS + 2):
                if r >= 2:
                    bring_p(r - 2)
                if r < ROUNDS:
                    act.wait_ge(a_bias, r + 1)
                    for g in range(4):
                        last = sc.activation(pr[:, r % 3, g], psum(2 + r % 2)[:, P * g:P * g + P], ACT.Exp,
                                             bias=nb[:, r % 2, g:g + 1], scale=INV, accum_out=sm[:, r % 2, g:g + 1])
                    last.then_inc(a_exp, 1)
                    bring_x(r)

        @block.vector
        def _(dve):
            v = nc.vector
            step = Chain(dve, dv)
            by_entry = result.rearrange("p r (b k) c -> p r b k c", k=2)
            v.tensor_scalar(mv[:, :, 1], mv[:, :, 1], LN_EPS, None, ALU.add).then_inc(var_ready, 1)
            dve.wait_ge(std_ready, 1)
            rsqrt_refined(v, step, rs, root, mv[:, :, 1])
            dve.wait_ge(s.x1_stored, 16 * NT)
            for t in range(NT):
                v.tensor_scalar(X[:, t], X[:, t], mv[:, t, 0:1], rs[:, t:t + 1], ALU.subtract,
                                ALU.mult).then_inc(xn_ready, 1)
            dve.wait_ge(consts2_in, 16)
            v.tensor_copy(s.maskb[:, :], const("same_l")).then_inc(mask_ready, 1)
            v.tensor_copy(beforeb, const("before")).then_inc(mask_ready, 1)
            dve.wait_ge(lt, 1)
            step.then(v.tensor_copy(p, psum(7)[:, 0:P].rearrange("p (t e) -> p t e", t=NT)))
            step.then(v.tensor_reduce(top, p, AX.X, ALU.max))
            v.tensor_tensor(p, p, top.unsqueeze(2).broadcast_to([P, NT, E]), ALU.subtract).then_inc(p_ex, 1)
            dve.wait_ge(p_exd, 1)
            step.then(v.tensor_reduce(sums, p, AX.X, ALU.add))
            step.then(v.reciprocal(sums, sums))
            step.then(v.tensor_tensor(p, p, sums.unsqueeze(2).broadcast_to([P, NT, E]), ALU.mult))
            other = p.unsqueeze(2).broadcast_to([P, NT, E, E])
            this = p.unsqueeze(3).broadcast_to([P, NT, E, E])
            earlier = const("earlier_e", "p (e f) -> p e f", e=E).unsqueeze(1).broadcast_to([P, NT, E, E])
            step(v.tensor_tensor(big1, other, this, ALU.is_gt))
            step.then(v.tensor_tensor(big2, other, this, ALU.is_equal))
            step.then(v.tensor_tensor(big2, big2, earlier, ALU.mult))
            step.then(v.tensor_tensor(big1, big1, big2, ALU.add))
            step.then(v.tensor_reduce(rank, big1, AX.X, ALU.add))
            v.tensor_scalar(chosen, rank, 2.0, None, ALU.is_lt).then_inc(chosen_ready, 1)
            step(v.tensor_scalar(first, rank, 0.0, None, ALU.is_equal))
            step.then(v.tensor_scalar(second, rank, 1.0, None, ALU.is_equal))
            small1, small2 = big1[:, :, 0], big2[:, :, 0]
            step(v.tensor_tensor(small1, first, p, ALU.mult))
            step.then(v.tensor_tensor(small2, second, p, ALU.mult))
            step(v.tensor_reduce(vals[:, :, 0], small1, AX.X, ALU.add))
            step.then(v.tensor_reduce(vals[:, :, 1], small2, AX.X, ALU.add))
            step.then(v.tensor_tensor(sums, vals[:, :, 0], vals[:, :, 1], ALU.add))
            step.then(v.reciprocal(sums, sums))
            step.then(v.tensor_tensor(s.gatew, vals, sums.unsqueeze(2).broadcast_to([P, NT, 2]), ALU.mult))
            dve.wait_ge(counted, 1)
            counts = psum(7)[:, 128:128 + E * (NT + 1)].rearrange("p (t e) -> p t e", e=E)
            step.then(v.tensor_tensor(over, counts[:, NT].unsqueeze(2).broadcast_to([P, E, 16]),
                                      const("tile_starts").unsqueeze(1).broadcast_to([P, E, 16]), ALU.is_gt))
            step.then(v.tensor_reduce(n_blocks, over, AX.X, ALU.add))
            step.then(v.tensor_tensor(before_e, n_blocks.unsqueeze(1).broadcast_to([P, E, E]),
                                      const("earlier_e", "p (e f) -> p e f", e=E), ALU.mult))
            step.then(v.tensor_reduce(starts, before_e, AX.X, ALU.add))
            step.then(v.tensor_scalar(row_starts, starts, float(P), None, ALU.mult))
            step.then(v.tensor_tensor(within, counts[:, 0:NT], row_starts.unsqueeze(1).broadcast_to([P, NT, E]), ALU.add))
            step(v.tensor_tensor(small1, first, within, ALU.mult))
            step.then(v.tensor_tensor(small2, second, within, ALU.mult))
            step(v.tensor_reduce(slotf[:, :, 0], small1, AX.X, ALU.add))
            step.then(v.tensor_reduce(slotf[:, :, 1], small2, AX.X, ALU.add))
            v.tensor_copy(s.slots, slotf).then_inc(slots_ready, 1)

            for r in range(ROUNDS + 3):
                if r >= 3:
                    of = r - 3
                    if of % 2 == 0 and of >= 4:
                        dve.wait_ge(s.messages_stored[of // 2 - 2], 16)
                    for k in range(2):
                        dve.wait_ge(a_msg, 2 * of + k + 1)
                        own = XP[:, k, 64 * of:64 * of + 64]
                        to = by_entry[:, of // 2 % 2, :, k, 64 * (of % 2):64 * (of % 2) + 64]
                        v.tensor_tensor(to.rearrange("p b c -> p c b"), psum(k).rearrange("p (c b) -> p c b", b=NB),
                                        own, ALU.add).then_inc(a_added, 1)
                if r < ROUNDS:
                    dve.wait_ge(a_scored, r + 1)
                    v.tensor_reduce(mx[:, r % 2], psum(2 + r % 2).rearrange("p (g k) -> p g k", g=4), AX.X,
                                    ALU.max).then_inc(a_maxed, 1)
                    dve.wait_ge(a_maxed, r + 1)
                    v.tensor_scalar(nb[:, r % 2], mx[:, r % 2], -INV, None, ALU.mult).then_inc(a_bias, 1)
                    dve.wait_ge(a_xt, 2 * r + 2)
                    if r >= 3:
                        dve.wait_ge(a_msg, 2 * (r - 2))
                    v.tensor_copy(xg[:, r % 3, 1], psum(5).rearrange("p (g c) -> p g c", g=4)).then_inc(a_xt_v, 1)
                    dve.wait_ge(a_exp, r + 1)
                    v.reciprocal(rc[:, r % 2], sm[:, r % 2]).then_inc(a_recip, 1)
                    dve.wait_ge(a_recip, r + 1)
                    v.tensor_tensor(pr[:, r % 3], pr[:, r % 3], rc[:, r % 2].unsqueeze(2).broadcast_to([P, 4, P]),
                                    ALU.mult).then_inc(a_norm, 1)

            step(v.scalar_tensor_tensor(out=s.ends, in0=starts, scalar=1.0, in1=n_blocks, op0=ALU.add, op1=ALU.add))
            step.then(v.tensor_tensor(which, const("block_ids").unsqueeze(2).broadcast_to([P, NBLK, E - 1]),
                                      starts[:, 1:E].unsqueeze(1).broadcast_to([P, NBLK, E - 1]), ALU.is_ge))
            step.then(v.tensor_reduce(of_block, which, AX.X, ALU.add))
            step(v.tensor_scalar(s.ready_at, of_block, float(len(CHUNKS)), 1.0, ALU.mult, ALU.add))
            step.then(v.tensor_scalar(odd, of_block, 1.0, None, ALU.is_equal))
            for k in (3.0, 5.0, 7.0):
                step.then(v.scalar_tensor_tensor(out=odd, in0=of_block, scalar=k, in1=odd, op0=ALU.is_equal,
                                                 op1=ALU.add))
            step(v.tensor_scalar(s.slot_at, odd, 2.0 * SLOT, None, ALU.mult))

        @block.tensor
        def _(pe):
            mm, tr = nc.tensor.matmul, nc.tensor.transpose

            def route(c):
                if c == 0:
                    pe.wait_ge(g1_in, 16)
                pe.wait_ge(turned_out, 4 * c + 4)
                if c >= 2:
                    pe.wait_ge(logit_out, c - 1)
                for k in range(4):
                    last = mm(psum(2 + c % 2)[0:E], g1[:, k], XT[:, c % 2, k], start=(k == 0), stop=(k == 3))
                last.then_inc(logit, 1)

            for t in range(NT):
                pe.wait_ge(xn_ready, t + 1)
                if t >= 2:
                    pe.wait_ge(turned_out, t - 1)
                for k in range(4):
                    last = tr(psum(t % 2)[:, P * k:P * k + P], X[:, t, P * k:P * k + P], ident)
                last.then_inc(turned, 1)
                if t % 4 == 1 and t > 4:
                    route(t // 4 - 1)
            route(3)
            for t in range(NT):
                pe.wait_ge(logit_out, t // 4 + 1)
                last = tr(psum(7)[:, E * t:E * t + E], LT[0:E, P * t:P * t + P], ident[0:E, 0:E])
            last.then_inc(lt, 1)

            def count():
                pe.wait_ge(chosen_ready, 1)
                pe.wait_ge(zeroed, 3)
                counts = psum(7)[:, 128:128 + E * (NT + 1)]
                mm(counts, onesb, zerosb, start=True, stop=False, skip_group_check=True)
                mm(counts[:, 0:E * NT], beforeb, chosen.rearrange("p t e -> p (t e)"), start=False, stop=False,
                   skip_group_check=True)
                for t in range(NT):
                    last = mm(counts[:, E * (t + 1):].rearrange("p (t e) -> p t e", e=E), onesb,
                              chosen[:, t:t + 1].broadcast_to([P, NT - t, E]), start=False, stop=(t == NT - 1),
                              skip_group_check=True)
                last.then_inc(counted, 1)

            def score(r):
                if r >= 2:
                    pe.wait_ge(a_exp, r - 1)
                for g in range(4):
                    ps = psum(2 + r % 2)[:, P * g:P * g + P]
                    for k in range(2):
                        xk = by_group[:, k, 4 * r + g]
                        mm(ps, xk, xk, start=(k == 0), stop=False)
                    last = mm(ps, s.identb[:, :], s.maskb[:, :], start=False, stop=True)
                last.then_inc(a_scored, 1)

            def turn_x(r):
                for k in range(2):
                    if r:
                        pe.wait_ge(a_xt_v if k else a_xt_a, r)
                    for g in range(4):
                        last = tr(psum(4 + k)[:, P * g:P * g + P], by_group[:, k, 4 * r + g], ident)
                    last.then_inc(a_xt, 1)

            def turn_p(r):
                pe.wait_ge(a_norm, r + 1)
                if r:
                    pe.wait_ge(a_pt_out, r)
                for g in range(4):
                    last = tr(psum(6)[:, P * g:P * g + P], pr[:, r % 3, g], ident)
                last.then_inc(a_pt, 1)

            def message(r):
                pe.wait_ge(a_pt_out, r + 1)
                pe.wait_ge(a_xt_a, r + 1)
                pe.wait_ge(a_xt_v, r + 1)
                for k in range(2):
                    if r:
                        pe.wait_ge(a_added, 2 * (r - 1) + k + 1)
                    for g in range(4):
                        last = mm(psum(k)[:, P * g:P * g + P], xg[:, r % 3, k, g], pt[:, r % 2, g], start=True,
                                  stop=True)
                    last.then_inc(a_msg, 1)

            pe.wait_ge(mask_ready, 2)
            pe.wait_ge(batched, NT)
            score(0)
            turn_x(0)
            score(1)
            count()
            turn_x(1)
            for r in range(2, ROUNDS + 2):
                if r < ROUNDS:
                    score(r)
                turn_p(r - 2)
                if r < ROUNDS:
                    turn_x(r)
                message(r - 2)


def experts(s):
    nc, sem, psum, ident = s.nc, s.sem, s.psum, s.ident
    W, xgT, actT = s.W, s.xgT, s.actT
    xg = s.carve(2, D)
    act_ = s.carve(2, FF + 2 * FR)
    y = s.carve(2, D)
    stage = s.carve(2, CHUNK)
    HF = FF // 2
    xs, ys = s.xs, s.ys
    (raw_in0, raw_in1, x_in0, x_in1, x_turned, x_high, x_low, h_done, silu_out, act_ready, a_turned,
     a_high, a_high_v, a_low, y_done, y_out, y_in0, y_in1) = (sem(n) for n in (
         "raw_in0", "raw_in1", "xrows_in0", "xrows_in1", "rows_turned", "rows_high", "rows_low", "h_done",
         "silu_out", "act_ready", "act_turned", "act_high", "act_high_v", "act_low", "y_done", "y_out", "y_stored0",
         "y_stored1"))
    raw_in, x_in, y_in = (raw_in0, raw_in1), (x_in0, x_in1), (y_in0, y_in1)
    first_high, first_low, first_w2 = (sem(n) for n in ("first_high", "first_low", "first_w2"))
    high_in = [sem(f"high_in{i}") for i in range(2)]
    NCH = len(CHUNKS)


    with nc.Block() as block:
        @block.gpsimd
        def _(pool):
            pool.sem_inc(s.converted, 1)
            pool.wait_ge(s.raw0_in, 16 * NCH)
            for c in (1, *range(KT_PER_D, NCH)):
                at, rows, n = CHUNKS[c]
                pool.wait_ge(first_high, c + 1)
                low_of(s, c, s.raw0[0:rows, at:at + n], 0).then_inc(first_w2, 1)

            def bring_raw(j):
                if j >= 2:
                    pool.wait_ge(s.converted, 1 + j - 1)
                bring_chunk(pool, s, 1 + j // NCH, j % NCH, stage[:, j % 2]).then_inc(raw_in[j % 2], 16)

            def bring_high(j):
                e, c = 1 + j // NCH, j % NCH
                at, rows, n = CHUNKS[c]
                if c == 0 and e >= 2:
                    end = pool.value_load(s.ends[0:1, e - 2:e - 1], min_val=1, max_val=NBLK + 1)
                    pool.wait_ge(y_done, end)
                    pool.nop(nofuse=True)
                at0 = e % 2 * 2 * SLOT + at
                bring_chunk(pool, s, e, c, W[:, at0:at0 + n]).then_inc(high_in[j % 2], 16)

            bring_raw(0)
            pool.wait_ge(first_low, KT_PER_D - 1)
            pool.wait_ge(first_w2, NCH - KT_PER_D + 1)
            for stored in s.messages_stored:
                pool.wait_ge(stored, 16)
            bring_high(0)
            for j in range((E - 1) * NCH):
                e, c = 1 + j // NCH, j % NCH
                more = j + 1 < (E - 1) * NCH
                if more:
                    bring_raw(j + 1)
                if more and c + 1 < NCH:
                    bring_high(j + 1)
                pool.wait_ge(raw_in[j % 2], 16 * (j // 2 + 1))
                pool.wait_ge(high_in[j % 2], 16 * (j // 2 + 1))
                at, rows, n = CHUNKS[c]
                low_of(s, c, stage[0:rows, j % 2, 0:n], e % 2 * 2 * SLOT).then_inc(s.converted, 1)
                if more and c + 1 == NCH:
                    bring_high(j + 1)
            end = pool.value_load(s.ends[0:1, E - 2:E - 1], min_val=1, max_val=NBLK + 1)
            pool.wait_ge(y_done, end)
            pool.nop(nofuse=True)
            for q in range(NT // 2):
                pool.wait_ge(y_done, NBLK - NT // 2 + q)
                for i, rows in enumerate((s.x1, s.messages)):
                    pool.dma_start(s.kept[:, i, 2 * q:2 * q + 2],
                                   rows[2 * P * q:2 * P * q + 2 * P, :].rearrange("(t p) n -> p t n", p=P)).then_inc(
                                       s.kept_in, 16)

        @block.sync
        def _(sp):
            def load(b, par):
                sp.dma_start(xg[:, par], xs[ds(b * P, P), :]).then_inc(x_in[par], 16)

            load(0, 0)
            load(1, 1)
            sp.wait_ge(x_turned, 1)
            load(2, 0)
            with sp.Fori(0, (NBLK - 3) // 2) as i:
                for par in (1, 0):
                    b = i * 2 + (1 if par else 2)
                    sp.wait_ge(x_turned, b + 1)
                    load(b + 2, par)
            sp.wait_ge(y_in0, 16 * (NBLK // 2 + 1))
            sp.wait_ge(y_in1, 16 * (NBLK // 2))

        @block.scalar
        def _(act):
            sc = nc.scalar

            def rows(b, par):
                act.wait_ge(x_turned, b + 1)
                sc.activation(xgT[:, par, HIGH], psum(4), ACT.Copy).then_inc(x_high, 1)

            def silu(b, par, hf):
                act.wait_ge(h_done, b * 2 + hf + 1)
                sc.activation(act_[:, par, HF * hf:HF * hf + HF], psum(2 * hf)[:, 0:HF], ACT.Silu).then_inc(silu_out, 1)

            def turned(b):
                act.wait_ge(a_turned, b)
                sc.activation(actT[:, HIGH, 0:4 * P], psum(5), ACT.Copy).then_inc(a_high, 1)

            def result(b, par, early):
                act.wait_ge(y_done, b + 1)
                if not early:
                    act.wait_ge(y_in[1 - par], b * 8 - 8 if par == 1 else b * 8 - 16)
                sc.activation(y[:, 1 - par], psum(7), ACT.Copy).then_inc(y_out, 1)
                act.wait_ge(y_out, b)
                act.dma_start(ys[ds((b - 1) * P, P), :], y[:, 1 - par]).then_inc(y_in[1 - par], 16)

            def step(b, par, first=False, last=False, early=False):
                silu(b, par, 0)
                if not last:
                    rows(b + 1, 1 - par)
                if not first:
                    turned(b)
                silu(b, par, 1)
                if not first:
                    result(b, par, early)

            act.wait_ge(s.raw0_in, 16 * NCH)
            for c, (at, n_rows, n) in enumerate(CHUNKS):
                if c == KT_PER_D:
                    rows(0, 0)
                sc.activation(parts_of(s, c, 0)[HIGH], s.raw0[0:n_rows, at:at + n], ACT.Copy).then_inc(first_high, 1)
            step(0, 0, first=True)
            step(1, 1, early=True)
            step(2, 0, early=True)
            with act.Fori(1, (NBLK - 3) // 2) as i:
                step(i * 2 + 1, 1)
                step(i * 2 + 2, 0)
            step(NBLK - 2, 1)
            step(NBLK - 1, 0, last=True)
            turned(NBLK)
            result(NBLK, 1, False)

        @block.vector
        def _(dve):
            v = nc.vector

            def rows(b, par):
                dve.wait_ge(x_high, b + 1)
                v.tensor_tensor(xgT[:, par, LOW], psum(4), xgT[:, par, HIGH], ALU.subtract).then_inc(x_low, 1)

            def multiply(b, par, hf):
                dve.wait_ge(silu_out, b * 2 + hf + 1)
                half = act_[:, par, HF * hf:HF * hf + HF]
                if hf == 1:
                    def twice(columns):
                        return columns.unsqueeze(1).broadcast_to([P, 2, FR])

                    v.tensor_tensor(act_[:, par, FF:].rearrange("p (i n) -> p i n", i=2), twice(half[:, HF - FR:]),
                                    twice(psum(3)[:, HF - FR:HF]), ALU.mult).then_inc(act_ready, 1)
                    dve.wait_ge(act_ready, b * 3 + 2)
                v.tensor_tensor(half, half, psum(2 * hf + 1)[:, 0:HF], ALU.mult).then_inc(act_ready, 1)

            def turned(b):
                dve.wait_ge(a_turned, b)
                v.tensor_copy(actT[:, HIGH, 4 * P:6 * P], psum(6)[:, 0:2 * P]).then_inc(a_high_v, 1)
                v.tensor_copy(actT[0:3 * FR, HIGH, 6 * P:7 * P], psum(6)[0:3 * FR, 2 * P:3 * P]).then_inc(a_high_v, 1)
                dve.wait_ge(a_high, b)
                v.tensor_tensor(actT[:, LOW, 0:4 * P], psum(5), actT[:, HIGH, 0:4 * P], ALU.subtract).then_inc(a_low, 1)
                dve.wait_ge(a_high_v, b * 2)
                v.tensor_tensor(actT[:, LOW, 4 * P:6 * P], psum(6)[:, 0:2 * P], actT[:, HIGH, 4 * P:6 * P],
                                ALU.subtract).then_inc(a_low, 1)
                v.tensor_tensor(actT[REST_ALOW, HIGH, 6 * P:7 * P], psum(6)[REST_ALOW, 2 * P:3 * P],
                                actT[REST_ALOW, HIGH, 6 * P:7 * P], ALU.subtract).then_inc(a_low, 1)

            def step(b, par, last=False):
                multiply(b, par, 0)
                if not last:
                    rows(b + 1, 1 - par)
                turned(b)
                multiply(b, par, 1)

            dve.wait_ge(s.raw0_in, 16 * NCH)
            for c in (0, 2, 3):
                at, _, n = CHUNKS[c]
                high, low = parts_of(s, c, 0)
                dve.wait_ge(first_high, c + 1)
                v.tensor_tensor(low, s.raw0[:, at:at + n], high, ALU.subtract).then_inc(first_low, 1)
            rows(0, 0)
            multiply(0, 0, 0)
            rows(1, 1)
            multiply(0, 0, 1)
            with dve.Fori(0, (NBLK - 3) // 2) as i:
                step(i * 2 + 1, 1)
                step(i * 2 + 2, 0)
            step(NBLK - 2, 1)
            step(NBLK - 1, 0, last=True)
            turned(NBLK)

        @block.tensor
        def _(pe):
            mm, tr = nc.tensor.matmul, nc.tensor.transpose

            def turn_rows(b, par):
                pe.wait_ge(x_in[par], b * 8 + 16 if par == 0 else b * 8 + 8)
                if not (isinstance(b, int) and b == 0):
                    pe.wait_ge(x_low, b)
                for k in range(4):
                    last = tr(psum(4)[:, P * k:P * k + P], xg[:, par, P * k:P * k + P], ident)
                last.then_inc(x_turned, 1)

            def up(b, par, off, hf):
                pe.wait_ge(x_high, b + 1)
                pe.wait_ge(x_low, b + 1)
                if not (isinstance(b, int) and b == 0):
                    pe.wait_ge(act_ready, b * 3 - (0 if hf else 2))
                for w in range(2):
                    for i, (of_x, of_w) in enumerate(PASSES):
                        for k in range(4):
                            last = mm(psum(2 * hf + w)[:, 0:HF], xgT[:, par, of_x, P * k:P * k + P],
                                      W[:, ds(off + (of_w * SLOT + (k * 2 + w) * FF + hf * HF), HF)],
                                      start=(i == 0 and k == 0), stop=(i == 2 and k == 3))
                last.then_inc(h_done, 1)

            def turn_act(b, par):
                pe.wait_ge(act_ready, b * 3 + 3)
                for t in range(FT + 1):
                    n = P if t < FT else 3 * FR
                    ps = psum(5)[:, P * t:P * t + P] if t < 4 else psum(6)[0:n, P * (t - 4):P * (t - 4) + P]
                    last = tr(ps, act_[:, par, P * t:P * t + n], ident)
                last.then_inc(a_turned, 1)

            def down(b, off):
                pe.wait_ge(a_high, b + 1)
                pe.wait_ge(a_high_v, b * 2 + 2)
                if not (isinstance(b, int) and b == 0):
                    pe.wait_ge(y_out, b)
                for i, (of_a, of_w) in enumerate(PASSES):
                    if of_a == LOW:
                        pe.wait_ge(a_low, b * 3 + 3)
                    for t in range(FT):
                        mm(psum(7), actT[:, of_a, P * t:P * t + P], W[:, ds(off + (of_w * SLOT + W13 + t * D), D)],
                           start=(i == 0 and t == 0), stop=False)
                last = mm(psum(7), actT[0:3 * FR, HIGH, P * FT:P * FT + P],
                          W[0:3 * FR, ds(off + (W13 + FT * D), D)], start=False, stop=True)
                last.then_inc(y_done, 1)

            def place(b):
                return pe.value_load(s.slot_at[0:1, ds(b, 1)], min_val=0, max_val=2 * SLOT)

            def weights(b):
                off = place(b)
                pe.wait_ge(s.converted, pe.value_load(s.ready_at[0:1, ds(b, 1)], min_val=1, max_val=NCH * E))
                return off

            pe.sem_inc(y_done, 1)
            turn_rows(0, 0)
            off = weights(0)
            pe.wait_ge(first_low, KT_PER_D - 1)
            pe.wait_ge(first_w2, 1)
            up(0, 0, off, 0)
            turn_rows(1, 1)
            up(0, 0, off, 1)
            pe.wait_ge(first_w2, NCH - KT_PER_D + 1)

            def step(b, par, last=False):
                off = weights(b)
                up(b, par, off, 0)
                if not last:
                    turn_rows(b + 1, 1 - par)
                turn_act(b - 1, 1 - par)
                up(b, par, off, 1)
                before = place(b - 1)
                down(b - 1, before)

            with pe.Fori(0, (NBLK - 3) // 2) as i:
                step(i * 2 + 1, 1)
                step(i * 2 + 2, 0)
            step(NBLK - 2, 1)
            step(NBLK - 1, 0, last=True)
            turn_act(NBLK - 1, 0)
            down(NBLK - 1, place(NBLK - 1))


def combine(s):
    nc, sem, X, S = s.nc, s.sem, s.kept[:, 0], s.kept[:, 1]
    DEEP = 5
    yy = s.carve(DEEP, 2, D)
    z = s.carve(4, D)
    got = [sem(f"rows_got{i}") for i in range(DEEP)]
    dv, scaled, mixed, gated, done, stored = (sem(n) for n in ("c_dve", "scaled", "mixed", "c_gated", "c_done", "stored"))

    with nc.Block() as block:
        @block.gpsimd
        def _(pool):
            for t in range(NT):
                if t >= DEEP:
                    pool.wait_ge(mixed, t - DEEP + 1)
                for k in range(2):
                    nc.gpsimd.indirect_dma_start(
                        out=yy[:, t % DEEP, k], out_offset=None, in_=s.ys,
                        in_offset=bass.IndirectOffsetOnAxis(ap=s.slots[:, t, k:k + 1], axis=0)).then_inc(
                            got[t % DEEP], 16)

        @block.vector
        def _(dve):
            v = nc.vector
            step = Chain(dve, dv)

            def finish(t):
                dve.wait_ge(gated, t + 1)
                if t == 0:
                    dve.wait_ge(s.kept_in, 16 * NT)
                step.then(v.tensor_tensor(z[:, t % 4], z[:, t % 4], S[:, t], ALU.mult))
                v.tensor_tensor(X[:, t], X[:, t], z[:, t % 4], ALU.add).then_inc(done, 1)

            for t in range(NT):
                dve.wait_ge(scaled, t + 1)
                v.scalar_tensor_tensor(out=z[:, t % 4], in0=yy[:, t % DEEP, 1], scalar=s.gatew[:, t, 1:2],
                                       in1=z[:, t % 4], op0=ALU.mult, op1=ALU.add).then_inc(mixed, 1)
                if t:
                    finish(t - 1)
            finish(NT - 1)

        @block.scalar
        def _(act):
            def scale(t):
                act.wait_ge(got[t % DEEP], 32 * (t // DEEP + 1))
                if t >= 4:
                    act.wait_ge(done, t - 3)
                nc.scalar.activation(z[:, t % 4], yy[:, t % DEEP, 0], ACT.Copy, scale=s.gatew[:, t, 0:1]).then_inc(
                    scaled, 1)

            scale(0)
            for t in range(NT):
                if t + 1 < NT:
                    scale(t + 1)
                act.wait_ge(mixed, t + 1)
                nc.scalar.activation(z[:, t % 4], z[:, t % 4], ACT.Silu).then_inc(gated, 1)

        @block.sync
        def _(sp):
            for t in range(NT):
                sp.wait_ge(done, t + 1)
                sp.dma_start(s.out[P * t:P * t + P, :], X[:, t]).then_inc(stored, 16)
            sp.wait_ge(stored, 16 * NT)


ROPE_ORDER = np.concatenate([np.arange(0, ROPE, 2), np.arange(1, ROPE, 2)])


def lay_out(i):
    f = lambda n: np.asarray(i[n])
    wqb = f("L0_attn_wq_b").reshape(H, NOPE + ROPE, QR)
    wkb = f("L0_attn_wkv_b").reshape(H, NOPE + VD, KVR)
    wkva = f("L0_attn_wkv_a")
    wkva = np.concatenate([wkva[KVR:][ROPE_ORDER], wkva[:KVR]], 0)

    def by_k(wt):
        return wt.reshape(KT_PER_D, P, -1).transpose(1, 0, 2)

    r = {
        "consts": shape_constants(),
        "x": f("L0_attn_x").reshape(NB * SEQ, D),
        "vecs": np.concatenate([f("L0_ffn_b"), f("L0_attn_q_a_ln_w"), f("L0_attn_kv_a_ln_w"), f("L0_ffn_router_b")])[None],
        "wqkv": by_k(np.concatenate([f("L0_attn_wq_a"), wkva], 0).T),
        "wq_rope": wqb[:, NOPE:][:, ROPE_ORDER].transpose(2, 0, 1),
        "wq_nope": wqb[:, :NOPE].transpose(1, 0, 2),
        "wkv_k": wkb[:, :NOPE].transpose(1, 0, 2),
        "wkv_v": wkb[:, NOPE:].transpose(1, 0, 2),
        "wo": f("L0_attn_wo").T.reshape(H, VD, D).transpose(1, 0, 2),
        "gate_w": by_k(f("L0_ffn_W").T),
        "lora_a": by_k(f("L0_ffn_A").reshape(NE * RANK, D).T),
        "lora_b": f("L0_ffn_B").transpose(0, 2, 1).reshape(NE * RANK, D),
        "router": by_k(f("L0_ffn_router_W").T),
        "gate1": by_k(f("L1_ffn_gate_w").T),
        "w13": np.stack([f("L1_ffn_w1"), f("L1_ffn_w3")], 1).reshape(E, 2, FF, KT_PER_D, P).transpose(0, 4, 3, 1, 2)
                 .reshape(E, P, KT_PER_D * 2 * FF),
        "w2": f("L1_ffn_w2").transpose(0, 2, 1),
        "w2_rest": np.tile(f("L1_ffn_w2").transpose(0, 2, 1)[:, FT * P:], (1, 3, 1)),
    }
    return {k: np.ascontiguousarray(v) for k, v in r.items()}


def kernel(**inputs):
    import concourse.bacc as bacc
    from concourse.bass_utils import run_bass_kernel_spmd

    nc = bacc.Bacc("TRN2", target_bir_lowering=False, num_devices=1)
    arrays = lay_out(inputs)
    aps = {k: nc.dram_tensor(k, v.shape, mybir.dt.from_np(v.dtype), kind="ExternalInput").ap()
           for k, v in arrays.items()}
    out = nc.dram_tensor("out", (NB * SEQ, D), F32, kind="ExternalOutput").ap()
    build(nc, aps, out)
    r = run_bass_kernel_spmd(nc, [arrays], core_ids=[0])
    return r.results[0]["out"].reshape(NB, SEQ, D)
```
